# Optimizing a Trainium2 kernel written in Bass

```python
import numpy as np
import jax
import jax.numpy as jnp

def _softmax(x, axis=-1):
    return jax.nn.softmax(x, axis=axis)

def _gelu(x):
    return jax.nn.gelu(x, approximate=True)

def _silu(x):
    return jax.nn.silu(x)

def _sigmoid(x):
    return jax.nn.sigmoid(x)

def _layernorm(x, axis=-1, eps=1e-05):
    m = jnp.mean(x, axis=axis, keepdims=True)
    v = jnp.var(x, axis=axis, keepdims=True)
    return (x - m) / jnp.sqrt(v + eps)

def _scatter_add(tgt, idx, src, axis=0):
    return tgt.at[idx].add(src)

def _segment_sum(src, seg, n):
    return jax.ops.segment_sum(src, seg, n)
kernel_name = 'mk_seq_preln_d1_jaxref_r8_81d390'

def setup_inputs(seed: int=0):
    np.random.seed(seed)
    _w = jnp.asarray

    def _L0_attn_setup():
        import jax, jax.numpy as jnp
        import numpy as np
        B, S, E = (8, 128, 128)
        H = 16
        D = E // H

        def _split_heads(t, b, s):
            return t.reshape(b, s, H, D).transpose(0, 2, 1, 3)
        key = jax.random.key(seed)
        ks = jax.random.split(key, 5)
        scale = 1.0 / np.sqrt(E)
        return {'x': jax.random.normal(ks[0], (B, S, E), dtype=jnp.float32), 'Wq': jax.random.normal(ks[1], (E, E), dtype=jnp.float32) * scale, 'Wk': jax.random.normal(ks[2], (E, E), dtype=jnp.float32) * scale, 'Wv': jax.random.normal(ks[3], (E, E), dtype=jnp.float32) * scale, 'Wo': jax.random.normal(ks[4], (E, E), dtype=jnp.float32) * scale}
    _L0_attn_in = _L0_attn_setup()

    def _L0_ffn_setup():
        import jax, jax.numpy as jnp
        import numpy as np
        B, S, H = (2, 256, 128)
        F = 512
        E = 8
        TOP_K = 2
        SHARED_SCALE = 0.1
        EPS = 1e-09

        def _moe_forward(x3, Wg, W1, b1, W2, b2, Ws1, bs1, Ws2, bs2):
            b, s, h = x3.shape
            x = x3.reshape(-1, h)
            T = x.shape[0]
            logits = x @ Wg
            probs = jax.nn.softmax(logits, axis=-1)
            vals, idx = jax.lax.top_k(probs, TOP_K)
            weights = vals / (jnp.sum(vals, axis=-1, keepdims=True) + EPS)
            cw = jnp.zeros((T, E), dtype=x.dtype).at[jnp.arange(T)[:, None], idx].set(weights)
            hpre = jnp.einsum('th,ehf->tef', x, W1) + b1
            act = jax.nn.silu(hpre)
            y = jnp.einsum('tef,efh->teh', act, W2) + b2
            out = jnp.einsum('te,teh->th', cw, y)
            shared = jax.nn.silu(x @ Ws1 + bs1) @ Ws2 + bs2
            out = out + SHARED_SCALE * shared
            return out.reshape(b, s, h)
        key = jax.random.key(seed)
        ks = jax.random.split(key, 10)
        sc = 0.02
        return {'hidden_states': jax.random.normal(ks[0], (B, S, H), dtype=jnp.float32), 'Wg': jax.random.normal(ks[1], (H, E), dtype=jnp.float32) * sc, 'W1': jax.random.normal(ks[2], (E, H, F), dtype=jnp.float32) * sc, 'b1': jnp.zeros((E, F), dtype=jnp.float32), 'W2': jax.random.normal(ks[3], (E, F, H), dtype=jnp.float32) * sc, 'b2': jnp.zeros((E, H), dtype=jnp.float32), 'Ws1': jax.random.normal(ks[4], (H, F), dtype=jnp.float32) * sc, 'bs1': jnp.zeros((F,), dtype=jnp.float32), 'Ws2': jax.random.normal(ks[5], (F, H), dtype=jnp.float32) * sc, 'bs2': jnp.zeros((H,), dtype=jnp.float32)}
    _L0_ffn_in = _L0_ffn_setup()
    _d = {'L0_attn_x': _L0_attn_in['x'], 'L0_attn_Wq': _L0_attn_in['Wq'], 'L0_attn_Wk': _L0_attn_in['Wk'], 'L0_attn_Wv': _L0_attn_in['Wv'], 'L0_attn_Wo': _L0_attn_in['Wo'], 'L0_ffn_Wg': _L0_ffn_in['Wg'], 'L0_ffn_W1': _L0_ffn_in['W1'], 'L0_ffn_b1': _L0_ffn_in['b1'], 'L0_ffn_W2': _L0_ffn_in['W2'], 'L0_ffn_b2': _L0_ffn_in['b2'], 'L0_ffn_Ws1': _L0_ffn_in['Ws1'], 'L0_ffn_bs1': _L0_ffn_in['bs1'], 'L0_ffn_Ws2': _L0_ffn_in['Ws2'], 'L0_ffn_bs2': _L0_ffn_in['bs2']}
    _x0 = _d['L0_attn_x']
    _d['L0_attn_x'] = jax.random.normal(jax.random.fold_in(jax.random.key(seed), 1), (16, 256, 128), dtype=_x0.dtype)
    del _x0
    return _d

def reference(L0_attn_x, L0_attn_Wq, L0_attn_Wk, L0_attn_Wv, L0_attn_Wo, L0_ffn_Wg, L0_ffn_W1, L0_ffn_b1, L0_ffn_W2, L0_ffn_b2, L0_ffn_Ws1, L0_ffn_bs1, L0_ffn_Ws2, L0_ffn_bs2):

    def _L0_attn_ref(x, Wq, Wk, Wv, Wo):
        import jax, jax.numpy as jnp
        import numpy as np
        B, S, E = (8, 128, 128)
        H = 16
        D = E // H

        def _split_heads(t, b, s):
            return t.reshape(b, s, H, D).transpose(0, 2, 1, 3)
        b, s, e = x.shape
        q = _split_heads(x @ Wq.T, b, s)
        k = _split_heads(x @ Wk.T, b, s)
        v = _split_heads(x @ Wv.T, b, s)
        d = q.shape[-1]
        q_c = q - q.mean(axis=-1, keepdims=True)
        k_c = k - k.mean(axis=-1, keepdims=True)
        cov = jnp.einsum('bhqd,bhkd->bhqk', q_c, k_c) / d
        q_var = (q_c * q_c).sum(axis=-1, keepdims=True) / (d - 1)
        k_var = (k_c * k_c).sum(axis=-1, keepdims=True) / (d - 1)
        var = jnp.einsum('bhqo,bhko->bhqk', q_var, k_var) / d
        attn = jax.nn.softmax(cov + var, axis=-1)
        out = jnp.einsum('bhqk,bhkd->bhqd', attn, v)
        out = out.transpose(0, 2, 1, 3).reshape(b, s, e)
        return out @ Wo.T

    def _L0_ffn_ref(hidden_states, Wg, W1, b1, W2, b2, Ws1, bs1, Ws2, bs2):
        import jax, jax.numpy as jnp
        import numpy as np
        B, S, H = (2, 256, 128)
        F = 512
        E = 8
        TOP_K = 2
        SHARED_SCALE = 0.1
        EPS = 1e-09

        def _moe_forward(x3, Wg, W1, b1, W2, b2, Ws1, bs1, Ws2, bs2):
            b, s, h = x3.shape
            x = x3.reshape(-1, h)
            T = x.shape[0]
            logits = x @ Wg
            probs = jax.nn.softmax(logits, axis=-1)
            vals, idx = jax.lax.top_k(probs, TOP_K)
            weights = vals / (jnp.sum(vals, axis=-1, keepdims=True) + EPS)
            cw = jnp.zeros((T, E), dtype=x.dtype).at[jnp.arange(T)[:, None], idx].set(weights)
            hpre = jnp.einsum('th,ehf->tef', x, W1) + b1
            act = jax.nn.silu(hpre)
            y = jnp.einsum('tef,efh->teh', act, W2) + b2
            out = jnp.einsum('te,teh->th', cw, y)
            shared = jax.nn.silu(x @ Ws1 + bs1) @ Ws2 + bs2
            out = out + SHARED_SCALE * shared
            return out.reshape(b, s, h)
        return _moe_forward(hidden_states, Wg, W1, b1, W2, b2, Ws1, bs1, Ws2, bs2)
    x = L0_attn_x
    x = x + _L0_attn_ref(_layernorm(x, axis=-1), L0_attn_Wq, L0_attn_Wk, L0_attn_Wv, L0_attn_Wo)
    x = x + _L0_ffn_ref(_layernorm(x, axis=-1), L0_ffn_Wg, L0_ffn_W1, L0_ffn_b1, L0_ffn_W2, L0_ffn_b2, L0_ffn_Ws1, L0_ffn_bs1, L0_ffn_Ws2, L0_ffn_bs2)
    return x

_drawn_inputs = setup_inputs


def setup_inputs(seed=0):
    import zlib

    import numpy as np

    out = dict(_drawn_inputs(seed))
    spreads = {'L0_ffn_b1': (0.0, 0.492),
     'L0_ffn_b2': (0.0, 0.1),
     'L0_ffn_bs1': (0.0, 0.8),
     'L0_ffn_bs2': (0.0, 0.8)}
    factors = {'L0_ffn_Ws1': 8.0, 'L0_ffn_Ws2': 8.0}
    for name, (base, spread) in spreads.items():
        noise = np.random.default_rng([zlib.crc32(name.encode()), seed]).standard_normal(out[name].shape)
        drawn = base * np.exp(spread * noise) if base else spread * noise
        out[name] = jnp.asarray(drawn.astype(out[name].dtype))
    for name, factor in factors.items():
        out[name] = (out[name] * factor).astype(out[name].dtype)
    return out
```

```python
from contextlib import ExitStack

import numpy as np
import concourse.bass as bass
from concourse import mybir

F32 = mybir.dt.float32
BF16 = mybir.dt.bfloat16
I32 = mybir.dt.int32
U32 = mybir.dt.uint32
ALU = mybir.AluOpType
ACT = mybir.ActivationFunctionType
AX = mybir.AxisListType

P = 128
B, S, E = 16, 256, 128
H = 16
D = E // H
QT = S // P
NT = B * QT
G = 4
HG = H // G
UNITS = H // 2
ROWS = 32
NE, F = 8, 512
FC = F // P
SHARED = NE
TOPK = 2
EPS = 1e-5
EPS_W = 1e-9
SHARED_SCALE = 0.1
REGION = B * S + P
DUMMY = NE * REGION
SHARED_ROW = DUMMY + P
XROWS = SHARED_ROW + B * S
XW = E + 1
ROUTED_TILES = TOPK * B * S // P + NE - 1
TILES = -(-(NT + ROUTED_TILES) // 4) * 4
RT_TILES = TILES - NT
OROWS = (TOPK + 1) * B * S
SKIP = 1 << 20
MAGIC = float(0x5F3759DF)

_COLS = [("ident", P), ("centre", P), ("centre_q", P), ("ind_q", H), ("ind_k", H), ("tri", P), ("sel", P),
         ("iota8", NE), ("region", NE), ("ids", QT * 3), ("steps", 32), ("lower", NE * NE), ("tiles", RT_TILES),
         ("shared_starts", NT), ("padding", P), ("part", 1)]
COL = {}
for _n, _w in _COLS:
    COL[_n] = (sum(w for _, w in _COLS[:len(COL)]), _w)
NCONST = sum(w for _, w in _COLS)


def constants():
    c = np.zeros((P, NCONST), np.float32)

    def put(name, a):
        o, w = COL[name]
        c[:, o:o + w] = a

    same = (np.arange(P)[:, None] // D == np.arange(P)[None, :] // D).astype(np.float32)
    centre = np.eye(P, dtype=np.float32) - same / D
    ind = (np.arange(P)[:, None] // D == np.arange(H)[None, :]).astype(np.float32)
    put("ident", np.eye(P))
    put("centre", centre)
    put("centre_q", centre / D)
    put("ind_q", ind * (D / (D - 1)))
    put("ind_k", ind / (D - 1))
    put("tri", np.arange(P)[:, None] < np.arange(P)[None, :])
    put("sel", np.arange(P)[:, None] == (np.arange(P)[None, :] // ROWS) * ROWS + D)
    put("iota8", np.arange(NE)[None, :])
    put("region", np.arange(NE)[None, :] * REGION)
    q, k = np.arange(QT)[None, :, None], np.arange(3)[None, None, :]
    put("ids", (3 * (q * P + np.arange(P)[:, None, None]) + k).reshape(P, QT * 3))
    put("steps", np.arange(32)[None, :] * P)
    put("lower", (np.arange(NE)[None, :] < np.arange(NE)[:, None]).reshape(1, -1))
    put("tiles", np.arange(RT_TILES)[None, :])
    put("shared_starts", SHARED_ROW + P * np.arange(NT)[None, :])
    put("part", np.arange(P)[:, None])
    return c


def wait(eng, sem, value):
    if isinstance(value, int) and value <= 0:
        return
    eng.wait_ge(sem, value)


def wait_apart(eng, passed, *waits):
    for sem, value in waits:
        wait(eng, sem, value)
        eng.sem_inc(passed, 1)


class Chain:

    def __init__(self, eng, sem, steps, rnd, passed=None):
        self.eng, self.sem, self.steps, self.base, self.n, self.passed = eng, sem, steps, steps * rnd, 0, passed

    def __call__(self, ins):
        self.n += 1
        assert self.n <= self.steps
        ins.then_inc(self.sem, 1)
        if self.passed is None:
            self.eng.wait_ge(self.sem, self.base + self.n)
        else:
            wait_apart(self.eng, self.passed, (self.sem, self.base + self.n))

    def done(self):
        assert self.n == self.steps, (self.n, self.steps)


def block_kernel(nc, x, Wq, Wk, Wv, Wo, Wg, W1, b1, W2, b2, Ws1, bs1, Ws2, bs2, consts, out):
    ctx = ExitStack()
    with ctx:
        def sb(name, shape, dt=F32):
            return ctx.enter_context(nc.sbuf_tensor(name, shape, dt))

        def sem(name):
            return ctx.enter_context(nc.semaphore(name))

        dq = [nc.dram_tensor(f"dq{i}", [H, ROWS, S], BF16, kind="Internal").ap() for i in range(2)]
        dk = [nc.dram_tensor(f"dk{i}", [H, ROWS, S], BF16, kind="Internal").ap() for i in range(2)]
        xrows = nc.dram_tensor("xrows", [XROWS, XW], F32, kind="Internal").ap()
        orows = nc.dram_tensor("orows", [OROWS, E], F32, kind="Internal").ap()

        xs = sb("xs", [P, NT + 2, E])
        cst = sb("cst", [P, NCONST])
        w1h = sb("w1h", [P, (NE + 1) * F], BF16)
        w1l = sb("w1l", [P, (NE + 1) * F], BF16)
        w1f = sb("w1f", [P, NE + 1, F])
        w2 = sb("w2", [P, (NE + 1) * F])
        b1t = sb("b1t", [P, (NE + 1) * FC])
        b2bc = sb("b2bc", [P, (NE + 1) * E])
        logits = sb("logits", [P, NT + 2, NE])
        top8 = sb("top8", [P, NT + 2, 8])
        starts = sb("starts", [P, TILES + 4], I32)
        experts = sb("experts", [P, TILES + 4], I32)

        def con(name, rows=P):
            o, w = COL[name]
            return cst[0:rows, o:o + w]

        wraw = sb("wraw", [P, 4, E])
        wog = sb("wog", [P, G, HG, ROWS])
        wqT, wkT, wvT = sb("wqT", [P, E]), sb("wkT", [P, E]), sb("wvT", [P, E])
        woT = sb("woT", [P, G, E])
        wg = sb("wg", [P, NE])
        b1r = sb("b1r", [(NE + 1) * FC, P])
        b2r = sb("b2r", [1, (NE + 1) * E])
        ones_f = sb("ones_f", [1, P])
        ident_b, tri_b, ones_b = sb("ident_b", [P, P], BF16), sb("tri_b", [P, P], BF16), sb("ones_b", [P, P], BF16)
        fill = sb("fill", [P, 2, G, S], BF16)
        pad_row = sb("pad_row", [P, XW])
        st1 = sb("st1", [P, NT, 6])
        mv1 = sb("mv1", [P, NT, 2])
        ve1, y1, t1 = sb("ve1", [P, NT]), sb("y1", [P, NT + 2]), sb("t1", [P, NT])
        nmr1 = sb("nmr1", [P, NT + 2])
        xn = sb("xn", [P, QT, E])
        xnT = [sb(f"xnT{i}", [P, S]) for i in range(2)]
        qk_hi, qk_lo = sb("qk_hi", [P, 2, S], BF16), sb("qk_lo", [P, 2, S], BF16)
        qk_sq = sb("qk_sq", [P, 2, S])
        var_hi, var_lo = sb("var_hi", [H, 2, S], BF16), sb("var_lo", [H, 2, S], BF16)
        qa = [sb(f"qa{i}", [P, G, S], BF16) for i in range(2)]
        ka = [sb(f"ka{i}", [P, G, S], BF16) for i in range(2)]
        vx = [sb(f"vx{i}", [P, QT, H, ROWS]) for i in range(2)]
        negmax = sb("negmax", [P, QT, H])
        m_parts = sb("m_parts", [P, QT, 2, H], BF16)
        mT = sb("mT", [2 * H, S], BF16)
        probs = [sb(f"probs{i}", [P, 2, QT, S]) for i in range(2)]
        oT = sb("oT", [P, G, S])
        rden = sb("rden", [P, G, S])
        onT = sb("onT", [P, G, S])
        x2 = sb("x2", [P, QT, E])
        st2, mv2 = sb("st2", [P, QT, 6]), sb("mv2", [P, QT, 2])
        ve2, y2, t2, nmr2 = sb("ve2", [P, QT]), sb("y2", [P, QT]), sb("t2", [P, QT]), sb("nmr2", [P, QT])
        xrow = [sb(f"xrow{i}", [P, QT, 3, XW]) for i in range(2)]
        idrun = sb("idrun", [P, QT * 3])
        x2nT = sb("x2nT", [P, S])
        lg, v8 = sb("lg", [P, QT, NE]), sb("v8", [P, QT, 8])
        i8 = sb("i8", [P, QT, 8], U32)
        idxf = sb("idxf", [P, QT, TOPK])
        onehot = sb("onehot", [P, QT, TOPK, NE])
        taken = sb("taken", [P, QT, NE], BF16)
        taken_sum = sb("taken_sum", [P, NE], BF16)
        place = sb("place", [P, QT, NE])
        placed = sb("placed", [P, QT, TOPK, NE])
        slotf = sb("slotf", [P, QT * TOPK])
        slot = [sb(f"slot{i}", [P, QT * TOPK], I32) for i in range(2)]
        cnt = sb("cnt", [P, NE])
        cmp_ = sb("cmp_", [P, NE, 32])
        ntile, tbase, total = sb("ntile", [P, NE]), sb("tbase", [P, NE]), sb("total", [P, 1])
        low = sb("low", [P, NE, NE])
        ge = sb("ge", [P, RT_TILES, NE])
        gt_ = sb("gt_", [P, RT_TILES, NE])
        ex, tb, stf, dead = (sb(n, [P, RT_TILES]) for n in ("ex", "tb", "stf", "dead"))
        padf, padi = sb("padf", [P, NE]), sb("padi", [P, NE], I32)

        ps_s1 = [ctx.enter_context(nc.psum_tensor(f"ps_s1{i}", [P, QT, S], F32)) for i in range(2)]
        ps_st = [ctx.enter_context(nc.psum_tensor(f"ps_st{i}", [P, 2, QT, S], F32)) for i in range(2)]
        ps_pv = ctx.enter_context(nc.psum_tensor("ps_pv", [P, 512], F32))
        ps_mi = ctx.enter_context(nc.psum_tensor("ps_mi", [P, 512], F32))
        ps_mib = ps_mi[:, :].bitcast(BF16)

        names = """x_in c_in w_in b_in w1_in w2_in fill_out wog_z wog_r set_ps set_r cast_r vx_init fill_r init_r ln1 ln1c
            xn_r xnc xt_ps xnT_r qk_ps qk_hi_r sq_r qk_lo_r var_ps var_hi_r var_lo_r rows_out
            s1_ps max_r m_r mc mt_ps mt_r mrow_in st_ps exp_r pv_ps ot_r db_ps rd_r on_r v_ps v_r
            wo_ps x2_r x2c y0_r n2c xrow_r x2keep id_r idc x2t_ps x2nT_r rt_ps lg_r rtc v8_r keep_r taken_r pos_ps pos_r posc slot_r
            tsum_r scat shared_out cnt_ps endc pad_i_r pads_out split_r passed""".split()
        s = {n: sem("s_" + n) for n in names}
        s_ld = [sem(f"s_ld{g}") for g in range(G)]

        FIRST, LAST = -2, B + 3

        def has(i, lag):
            return 0 <= i - lag < B if isinstance(i, int) else True

        def pass2_at(i, u):
            return (i - 1, u - 3, 1) if u >= 3 else (i - 2, u + 5, 2)

        def pv_at(i, u):
            return (i - 1, u - 4, 1) if u >= 4 else (i - 2, u + 4, 2)

        def run(eng, iteration):
            for i in range(FIRST, 6):
                iteration(i, i % 2)
            with eng.Fori(6, B - 2, 2) as i:
                iteration(i, 0)
                iteration(i + 1, 1)
            for i in range(B - 2, LAST):
                iteration(i, i % 2)

        with nc.Block() as block:
            @block.sync
            def _(sp):
                sp.dma_start(cst[:, :], consts).then_inc(s["c_in"], 16)
                for n, w in enumerate((Wq, Wk, Wv, Wo)):
                    sp.dma_start(wraw[:, n, :], w).then_inc(s["w_in"], 16)
                for n in range(4):
                    sp.dma_start(xs[:, 8 * n:8 * n + 8, :], x.rearrange("b (q p) e -> p (b q) e", p=P)[:, 8 * n:8 * n + 8, :]).then_inc(s["x_in"], 16)
                sp.dma_start(wg[:, :], Wg).then_inc(s["w_in"], 16)
                sp.dma_start(b1r[0:NE * FC, :], b1.rearrange("e (f p) -> (e f) p", p=P)).then_inc(s["b_in"], 16)
                sp.dma_start(b1r[NE * FC:, :], bs1.rearrange("(f p) -> f p", p=P)).then_inc(s["b_in"], 16)
                sp.dma_start(b2r[:, 0:NE * E], b2.rearrange("(o e) h -> o (e h)", o=1)).then_inc(s["b_in"], 16)
                sp.dma_start(b2r[:, NE * E:], bs2.rearrange("(o h) -> o h", o=1)).then_inc(s["b_in"], 16)
                sp.wait_ge(s["fill_r"], 3)
                for i in range(2):
                    sp.dma_start(dq[i].rearrange("(g j) r t -> (j r) g t", g=G), fill[:, 0, :, :]).then_inc(s["fill_out"], 16)
                    sp.dma_start(dk[i].rearrange("(g j) r t -> (j r) g t", g=G), fill[:, 0, :, :]).then_inc(s["fill_out"], 16)
                sp.wait_ge(s["fill_out"], 64)
                for i in range(2):
                    sp.dma_start(dk[i][:, 27:29, :], fill[0:2 * H, 1, 0, :]).then_inc(s["fill_out"], 16)
                sp.dma_start(xrows[DUMMY:DUMMY + P, :], pad_row[:, :]).then_inc(s["fill_out"], 16)
                sp.wait_ge(s["fill_out"], 64 + 16 * 3)
                sp.dma_start(w1f[:, 0:NE, :], W1.rearrange("e h f -> h e f")).then_inc(s["w1_in"], 16)
                sp.dma_start(w1f[:, NE, :], Ws1).then_inc(s["w1_in"], 16)
                w2v = w2[:, :].rearrange("p (e f h) -> p e f h", e=NE + 1, f=FC)
                for e in range(NE):
                    sp.dma_start(w2v[:, e, :, :], W2[e].rearrange("(f p) h -> p f h", p=P)).then_inc(s["w2_in"], 16)
                sp.dma_start(w2v[:, NE, :, :], Ws2.rearrange("(f p) h -> p f h", p=P)).then_inc(s["w2_in"], 16)

                def load(b, par, g):
                    wait(sp, s["st_ps"], UNITS * (b - 2) + 2 * g + 2)
                    for sbuf, dram in ((qa, dq), (ka, dk)):
                        sp.dma_start(sbuf[par][:, g, :], dram[par][HG * g:HG * (g + 1)].rearrange("j r t -> (j r) t")).then_inc(s_ld[g], 16)

                def iteration(i, par):
                    nxt = 1 - par
                    if has(i, -1):
                        b = i + 1
                        wait_apart(sp, s["passed"], *((s_ld[g], 32 * (b - 1)) for g in range(G)))
                        sp.wait_ge(s["qk_lo_r"], b + 1)
                        for side, dram, parts in ((0, dq, (qk_hi, qk_hi, qk_lo)), (1, dk, (qk_hi, qk_lo, qk_hi))):
                            for n, part in enumerate(parts):
                                sp.dma_start(dram[nxt][:, 9 * n:9 * n + D, :], part[:, side, :]).then_inc(s["rows_out"], 16)
                    if has(i, 1):
                        sp.wait_ge(s["mt_r"], i)
                        for c in range(2):
                            for g in range(G):
                                r = c * H + g * HG
                                sp.dma_start(qa[nxt][27 + c::ROWS, g, :], mT[r:r + HG, :]).then_inc(s["mrow_in"], 16)
                    if has(i, -1):
                        sp.wait_ge(s["var_lo_r"], b + 1)
                        for side, dram, parts in ((0, dq, (var_hi, var_hi, var_lo)), (1, dk, (var_hi, var_lo, var_hi))):
                            for n, part in enumerate(parts):
                                sp.dma_start(dram[nxt][:, 9 * n + D, :], part[:, side, :]).then_inc(s["rows_out"], 16)
                    if has(i, 0):
                        load(i, par, 2)
                        load(i, par, 3)
                    if has(i, 3):
                        b = i - 3
                        wait_apart(sp, s["passed"], (s["xrow_r"], b + 1), (s["id_r"], b + 1), (s["shared_out"], 16 * b))
                        sp.dma_start(xrows[bass.ds(b * S + SHARED_ROW, S), :].rearrange("(q p) w -> p q w", p=P),
                                     xrow[nxt][:, :, 2, :]).then_inc(s["shared_out"], 16)
                    if has(i, -1):
                        sp.wait_ge(s["rows_out"], 16 * 12 * (i + 2))
                        load(i + 1, nxt, 0)
                        load(i + 1, nxt, 1)

                run(sp, iteration)
                sp.wait_ge(s["shared_out"], 16 * B)
                sp.wait_ge(s["w2_in"], 16 * (NE + 1))

            @block.gpsimd
            def _(pool):
                nc.gpsimd.memset(wog[:, :, :, :], 0.0).then_inc(s["wog_z"], 1)
                nc.gpsimd.memset(fill[:, 0, :, :], 0.0).then_inc(s["fill_r"], 1)
                nc.gpsimd.memset(fill[:, 1, :, :], 1.0).then_inc(s["fill_r"], 1)
                nc.gpsimd.memset(pad_row[:, 0:E], 0.0)
                nc.gpsimd.memset(pad_row[:, E:].bitcast(I32), SKIP).then_inc(s["fill_r"], 1)
                for i in range(2):
                    nc.gpsimd.memset(vx[i][:, :, :, :], 0.0).then_inc(s["init_r"], 1)
                pool.wait_ge(s["init_r"], 2)
                for i in range(2):
                    last = nc.gpsimd.memset(vx[i][:, :, :, D:D + 1], 1.0)
                last.then_inc(s["vx_init"], 1)

                def layer_norm_in(b, par):
                    if isinstance(b, int) and b == 0:
                        pool.wait_ge(s["ln1"], 1)
                    wait(pool, s["xt_ps"], b)
                    at = bass.ds(QT * b, QT)
                    c = Chain(pool, s["xnc"], 1, b)
                    c(nc.gpsimd.tensor_tensor(xn[:, :, :], xs[:, at, :], y1[:, at].unsqueeze(2).to_broadcast([P, QT, E]), ALU.mult))
                    nc.gpsimd.tensor_tensor(xn[:, :, :], xn[:, :, :], nmr1[:, at].unsqueeze(2).to_broadcast([P, QT, E]), ALU.add).then_inc(s["xn_r"], 1)

                def normalise(b, g):
                    pool.wait_ge(s["rd_r"], G * b + g + 1)
                    if g == 0:
                        wait(pool, s["wo_ps"], b)
                    nc.gpsimd.tensor_tensor(onT[:, g, :], oT[:, g, :], rden[:, g, :], ALU.mult).then_inc(s["on_r"], 1)

                def rows_of_tokens(b, par):
                    pool.wait_ge(s["y0_r"], b + 1)
                    c = Chain(pool, s["n2c"], 14, b, s["passed"])
                    for _ in range(3):
                        c(nc.gpsimd.tensor_tensor(t2[:, :], y2[:, :], y2[:, :], ALU.mult))
                        c(nc.gpsimd.tensor_tensor(t2[:, :], t2[:, :], ve2[:, :], ALU.mult))
                        c(nc.gpsimd.tensor_scalar(t2[:, :], t2[:, :], -0.5, 1.5, ALU.mult, ALU.add))
                        c(nc.gpsimd.tensor_tensor(y2[:, :], y2[:, :], t2[:, :], ALU.mult))
                    c(nc.gpsimd.tensor_tensor(t2[:, :], mv2[:, :, 0], y2[:, :], ALU.mult))
                    c(nc.gpsimd.tensor_scalar(nmr2[:, :], t2[:, :], -1.0, 0.0, ALU.mult, ALU.add))
                    c.done()
                    wait_apart(pool, s["passed"], (s["scat"], 16 * QT * TOPK * (b - 1)), (s["shared_out"], 16 * (b - 1)))
                    for q in range(QT):
                        last = nc.gpsimd.tensor_scalar(xrow[par][:, q, :, 0:E], x2[:, q, :].unsqueeze(1).to_broadcast([P, 3, E]),
                                                       y2[:, q:q + 1], nmr2[:, q:q + 1], ALU.mult, ALU.add)
                    last.then_inc(s["xrow_r"], 1)
                    nc.gpsimd.tensor_copy(xs[:, bass.ds(QT * b, QT), :], x2[:, :, :]).then_inc(s["x2keep"], 1)

                def scatter(b, par):
                    pool.wait_ge(s["v8_r"], b + 1)
                    nc.gpsimd.tensor_copy(logits[:, bass.ds(QT * b, QT), :], lg[:, :, :])
                    nc.gpsimd.tensor_copy(top8[:, bass.ds(QT * b, QT), :], v8[:, :, :]).then_inc(s["keep_r"], 1)
                    wait_apart(pool, s["passed"], (s["slot_r"], b + 1), (s["id_r"], b + 1), (s["xrow_r"], b + 1),
                               (s["scat"], 16 * QT * TOPK * b))
                    for q in range(QT):
                        for k in range(TOPK):
                            n = q * TOPK + k
                            nc.gpsimd.indirect_dma_start(out=xrows, out_offset=bass.IndirectOffsetOnAxis(ap=slot[par][:, n:n + 1], axis=0),
                                                         in_=xrow[par][:, q, k, :], in_offset=None,
                                                         bounds_check=XROWS - 1, oob_is_err=False).then_inc(s["scat"], 16)

                def split_w1(e):
                    c = Chain(pool, s["split_r"], 2, e)
                    c(nc.gpsimd.tensor_copy(w1h[:, F * e:F * (e + 1)], w1f[:, e, :]))
                    c(nc.gpsimd.tensor_tensor(w1l[:, F * e:F * (e + 1)], w1f[:, e, :], w1h[:, F * e:F * (e + 1)], ALU.subtract))

                def iteration(i, par):
                    nxt = 1 - par
                    if has(i, 2):
                        normalise(i - 2, 1)
                        normalise(i - 2, 2)
                    if has(i, -2):
                        layer_norm_in(i + 2, par)
                    if has(i, 2):
                        normalise(i - 2, 3)
                    if has(i, 3):
                        scatter(i - 3, nxt)
                    if has(i, 2):
                        rows_of_tokens(i - 2, par)
                    if has(i, 1):
                        normalise(i - 1, 0)
                    if isinstance(i, int) and -1 <= i <= 1:
                        if i == -1:
                            pool.wait_ge(s["w1_in"], 32)
                        for e in range(3 * (i + 1), 3 * (i + 2)):
                            split_w1(e)

                run(pool, iteration)
                pool.wait_ge(s["pad_i_r"], 1)
                pool.wait_ge(s["fill_r"], 3)
                for e in range(NE):
                    nc.gpsimd.indirect_dma_start(out=xrows, out_offset=bass.IndirectOffsetOnAxis(ap=padi[:, e:e + 1], axis=0),
                                                 in_=pad_row[:, :], in_offset=None,
                                                 bounds_check=XROWS - 1, oob_is_err=False).then_inc(s["pads_out"], 16)
                pool.wait_ge(s["pads_out"], 16 * NE)
                pool.wait_ge(s["scat"], 16 * QT * TOPK * B)

            @block.scalar
            def _(act):
                def iteration(i, par):
                    nxt = 1 - par
                    for u in range(UNITS):
                        if u == 0 and has(i, -1):
                            b = i + 1
                            act.wait_ge(s["var_ps"], b + 1)
                            wait(act, s["rows_out"], 16 * 12 * b)
                            nc.scalar.activation(var_hi[:, :, :], ps_mi[0:H, :].rearrange("p (a t) -> p a t", a=2), ACT.Copy).then_inc(s["var_hi_r"], 1)
                        if u == 2 and has(i, 3):
                            b = i - 3
                            act.wait_ge(s["x2t_ps"], b + 1)
                            wait(act, s["rt_ps"], b)
                            nc.scalar.activation(x2nT[:, :], ps_mi[:, 0:S], ACT.Copy).then_inc(s["x2nT_r"], 1)
                        if u == 6 and has(i, -2):
                            b = i + 2
                            act.wait_ge(s["xt_ps"], b + 1)
                            wait(act, s["v_ps"], b - 1)
                            nc.scalar.activation(xnT[par][:, :], ps_mi[:, 0:S], ACT.Copy).then_inc(s["xnT_r"], 1)
                        if u == 7 and has(i, -2):
                            b = i + 2
                            act.wait_ge(s["qk_ps"], b + 1)
                            wait(act, s["rows_out"], 16 * 12 * b)
                            src = ps_mi[:, :].rearrange("p (a t) -> p a t", a=2)
                            nc.scalar.activation(qk_hi[:, :, :], src, ACT.Copy).then_inc(s["qk_hi_r"], 1)
                            wait(act, s["var_ps"], b)
                            nc.scalar.activation(qk_sq[:, :, :], src, ACT.Square).then_inc(s["sq_r"], 1)
                        b, k, lag = pass2_at(i, u)
                        if has(i, lag):
                            act.wait_ge(s["st_ps"], UNITS * b + k + 1)
                            wait(act, s["pv_ps"], UNITS * b + k - 1)
                            nc.scalar.activation(probs[k % 2][:, :, :, :].rearrange("p a q t -> p (a q t)"),
                                                 ps_st[k % 2][:, :, :, :].rearrange("p a q t -> p (a q t)"), ACT.Exp).then_inc(s["exp_r"], 1)
                        b, k, lag = pv_at(i, u)
                        if has(i, lag) and k % 2:
                            g = k // 2
                            act.wait_ge(s["pv_ps"], UNITS * b + k + 1)
                            wait(act, s["on_r"], G * (b - 1) + g + 1)
                            nc.scalar.activation(oT[:, g, :], ps_pv[:, 0:S], ACT.Copy).then_inc(s["ot_r"], 1)
                        if u == 0 and has(i, 1):
                            b = i - 1
                            act.wait_ge(s["mt_ps"], b + 1)
                            wait(act, s["mrow_in"], 16 * 2 * G * b)
                            nc.scalar.activation(mT[:, :], ps_mib[0:2 * H, 0:S], ACT.Copy).then_inc(s["mt_r"], 1)
                        if u == 5 and has(i, 0):
                            act.wait_ge(s["v_ps"], i + 1)
                            wait(act, s["pv_ps"], UNITS * (i - 1))
                            if isinstance(i, int) and i == 0:
                                act.wait_ge(s["vx_init"], 1)
                            for q in range(QT):
                                last = nc.scalar.activation(vx[par][:, q, :, 0:D], ps_mi[:, q * E:(q + 1) * E].rearrange("p (h d) -> p h d", d=D), ACT.Copy)
                            last.then_inc(s["v_r"], 1)

                run(act, iteration)

            @block.tensor
            def _(pe):
                pe.wait_ge(s["c_in"], 16)
                pe.wait_ge(s["w_in"], 16 * 5)
                nc.tensor.matmul(ps_s1[0][:, 0, 0:E], wraw[:, 0, :], con("centre_q"), start=True, stop=True)
                nc.tensor.matmul(ps_s1[0][:, 0, E:2 * E], wraw[:, 1, :], con("centre"), start=True, stop=True)
                nc.tensor.matmul(ps_s1[0][:, 1, 0:E], wraw[:, 2, :], con("ident"), start=True, stop=True).then_inc(s["set_ps"], 1)
                pe.wait_ge(s["wog_r"], 1)
                for g in range(G):
                    last = nc.tensor.matmul(ps_s1[1][:, g // 2, (g % 2) * E:(g % 2 + 1) * E], wog[:, g, :, :].rearrange("p j r -> p (j r)"), con("ident"), start=True, stop=True)
                last.then_inc(s["set_ps"], 1)
                pe.wait_ge(s["b_in"], 64)
                nb = (NE + 1) * FC
                nc.tensor.transpose(ps_pv[:, 0:nb], b1r[:, :], con("ident", nb)[:, 0:nb]).then_inc(s["set_ps"], 1)
                pe.wait_ge(s["wog_r"], 2)
                for a in range(3):
                    n = min(512, (NE + 1) * E - 512 * a)
                    dst = (ps_st[0][:, 0, :, :], ps_st[0][:, 1, :, :], ps_st[1][:, 0, :, :])[a].rearrange("p q t -> p (q t)")[:, 0:n]
                    last = nc.tensor.matmul(dst, ones_f[:, :], b2r[:, 512 * a:512 * a + n], start=True, stop=True)
                last.then_inc(s["set_ps"], 1)
                pe.wait_ge(s["set_r"], 1)

                prev = [None]

                def misc(sem_name, value):
                    if prev[0] is not None:
                        pe.wait_ge(s[prev[0][0]], prev[0][1])
                    prev[0] = (sem_name, value)

                def denominators(b, g):
                    pe.wait_ge(s["ot_r"], G * b + g + 1)
                    misc("rd_r", G * b + g + 1)
                    nc.tensor.matmul(ps_mi[:, 0:S], con("sel"), oT[:, g, :], start=True, stop=True).then_inc(s["db_ps"], 1)

                def step_a(i, par, u):
                    if u == 0 and has(i, -1):
                        b = i + 1
                        pe.wait_ge(s["sq_r"], b + 1)
                        misc("var_lo_r", b + 1)
                        nc.tensor.matmul(ps_mi[0:H, 0:S], con("ind_q"), qk_sq[:, 0, :], start=True, stop=True)
                        nc.tensor.matmul(ps_mi[0:H, S:2 * S], con("ind_k"), qk_sq[:, 1, :], start=True, stop=True).then_inc(s["var_ps"], 1)
                    if u == 1 and has(i, 2):
                        denominators(i - 2, 1)
                    if u == 2 and has(i, 3):
                        b = i - 3
                        pe.wait_ge(s["xrow_r"], b + 1)
                        misc("x2nT_r", b + 1)
                        for q in range(QT):
                            last = nc.tensor.transpose(ps_mi[:, q * P:(q + 1) * P], xrow[1 - par][:, q, 0, 0:E], con("ident"))
                        last.then_inc(s["x2t_ps"], 1)
                    if u == 4 and has(i, 3):
                        b = i - 3
                        pe.wait_ge(s["taken_r"], b + 1)
                        pe.wait_ge(s["tsum_r"], b + 1)
                        misc("pos_r", b + 1)
                        nc.tensor.matmul(ps_mi[:, 0:NE], tri_b[:, :], taken[:, 0, :], start=True, stop=False)
                        nc.tensor.matmul(ps_mi[:, 0:NE], ones_b[:, :], taken_sum[:, :], start=False, stop=True)
                        nc.tensor.matmul(ps_mi[:, NE:2 * NE], tri_b[:, :], taken[:, 1, :], start=True, stop=False)
                        nc.tensor.matmul(ps_mi[:, NE:2 * NE], ones_b[:, :], taken[:, 0, :], start=False, stop=False)
                        nc.tensor.matmul(ps_mi[:, NE:2 * NE], ones_b[:, :], taken_sum[:, :], start=False, stop=True).then_inc(s["pos_ps"], 1)
                    if u == 6 and has(i, -2):
                        b = i + 2
                        pe.wait_ge(s["xn_r"], b + 1)
                        misc("xnT_r", b + 1)
                        for q in range(QT):
                            last = nc.tensor.transpose(ps_mi[:, q * P:(q + 1) * P], xn[:, q, :], con("ident"))
                        last.then_inc(s["xt_ps"], 1)
                    if u == 7 and has(i, -2):
                        b = i + 2
                        pe.wait_ge(s["xnT_r"], b + 1)
                        misc("qk_lo_r", b + 1)
                        nc.tensor.matmul(ps_mi[:, 0:S], wqT[:, :], xnT[par][:, :], start=True, stop=True)
                        nc.tensor.matmul(ps_mi[:, S:2 * S], wkT[:, :], xnT[par][:, :], start=True, stop=True).then_inc(s["qk_ps"], 1)

                def step_b(i, par, u):
                    if u == 0 and has(i, 1):
                        b = i - 1
                        pe.wait_ge(s["m_r"], b + 1)
                        misc("mt_r", b + 1)
                        for q in range(QT):
                            last = nc.tensor.transpose(ps_mib[0:2 * H, q * P:(q + 1) * P], m_parts[:, q, :, :].rearrange("p c h -> p (c h)"), ident_b[:, :])
                        last.then_inc(s["mt_ps"], 1)
                    if u == 2 and has(i, 2):
                        denominators(i - 2, 2)
                    if u == 3 and has(i, 3):
                        b = i - 3
                        pe.wait_ge(s["x2nT_r"], b + 1)
                        misc("lg_r", b + 1)
                        for q in range(QT):
                            last = nc.tensor.matmul(ps_mi[:, q * NE:(q + 1) * NE], x2nT[:, q * P:(q + 1) * P], wg[:, :], start=True, stop=True)
                        last.then_inc(s["rt_ps"], 1)
                    if u == 4 and has(i, 2):
                        denominators(i - 2, 3)
                    if u == 5 and has(i, 0):
                        pe.wait_ge(s["xnT_r"], i + 1)
                        misc("v_r", i + 1)
                        for q in range(QT):
                            last = nc.tensor.matmul(ps_mi[:, q * E:(q + 1) * E], xnT[par][:, q * P:(q + 1) * P], wvT[:, :], start=True, stop=True)
                        last.then_inc(s["v_ps"], 1)
                    if u == 6 and has(i, 2):
                        b = i - 2
                        pe.wait_ge(s["on_r"], G * (b + 1))
                        misc("x2_r", b + 1)
                        for q in range(QT):
                            for g in range(G):
                                last = nc.tensor.matmul(ps_mi[:, q * E:(q + 1) * E], onT[:, g, q * P:(q + 1) * P], woT[:, g, :], start=g == 0, stop=g == G - 1)
                        last.then_inc(s["wo_ps"], 1)
                    if u == 7 and has(i, 1):
                        denominators(i - 1, 0)

                def iteration(i, par):
                    if not isinstance(i, int) or has(i, 2):
                        prev[0] = ("rd_r", (i - 2) * G + 1)
                    for u in range(UNITS):
                        if has(i, 0):
                            for a in range(2):
                                h = 2 * u + a
                                g, j = h // HG, h % HG
                                if h % HG == 0:
                                    pe.wait_ge(s_ld[g], 32 * (i + 1))
                                wait(pe, s["max_r"], i * H + h - 1)
                                r = slice(ROWS * j, ROWS * (j + 1))
                                for q in range(QT):
                                    last = nc.tensor.matmul(ps_s1[h % 2][:, q, :], qa[par][r, g, q * P:(q + 1) * P], ka[par][r, g, :], start=True, stop=True)
                                last.then_inc(s["s1_ps"], 1)
                        step_a(i, par, u)
                        b, k, lag = pass2_at(i, u)
                        if has(i, lag):
                            bp = (par + lag) % 2
                            if k == 0:
                                pe.wait_ge(s["mrow_in"], 16 * 2 * G * (b + 1))
                            wait(pe, s["exp_r"], UNITS * b + k - 1)
                            for a in range(2):
                                h = 2 * k + a
                                g, j = h // HG, h % HG
                                r = slice(ROWS * j, ROWS * (j + 1))
                                for q in range(QT):
                                    last = nc.tensor.matmul(ps_st[k % 2][:, a, q, :], ka[bp][r, g, q * P:(q + 1) * P], qa[bp][r, g, :], start=True, stop=True)
                            last.then_inc(s["st_ps"], 1)
                        b, k, lag = pv_at(i, u)
                        if has(i, lag):
                            bp = (par + lag) % 2
                            if k == 0:
                                pe.wait_ge(s["v_r"], b + 1)
                            pe.wait_ge(s["exp_r"], UNITS * b + k + 1)
                            if k % 2 == 0:
                                wait(pe, s["ot_r"], G * b + k // 2)
                            for a in range(2):
                                h = 2 * k + a
                                j = h % HG
                                for q in range(QT):
                                    last = nc.tensor.matmul(ps_pv[ROWS * j:ROWS * (j + 1), 0:S], vx[bp][:, q, h, :], probs[k % 2][:, a, q, :],
                                                            start=q == 0, stop=q == QT - 1, tile_position=(0, ROWS * j))
                            last.then_inc(s["pv_ps"], 1)
                        step_b(i, par, u)

                run(pe, iteration)
                pe.wait_ge(s["tsum_r"], B + 1)
                misc("", 0)
                nc.tensor.matmul(ps_mi[:, 0:NE], ones_b[:, :], taken_sum[:, :], start=True, stop=True).then_inc(s["cnt_ps"], 1)

            @block.vector
            def _(dve):
                dve.wait_ge(s["c_in"], 16)
                nc.vector.tensor_copy(ident_b[:, :], con("ident"))
                nc.vector.tensor_copy(tri_b[:, :], con("tri"))
                nc.vector.memset(ones_b[:, :], 1.0)
                nc.vector.memset(taken_sum[:, :], 0.0)
                nc.vector.tensor_copy(idrun[:, :], con("ids")).then_inc(s["tsum_r"], 1)
                dve.wait_ge(s["w_in"], 16 * 5)
                dve.wait_ge(s["wog_z"], 1)
                for g in range(G):
                    last = nc.vector.tensor_copy(wog[:, g, :, 0:D], wraw[:, 3, g * HG * D:(g + 1) * HG * D].rearrange("p (j d) -> p j d", d=D))
                last.then_inc(s["wog_r"], 1)
                nc.vector.memset(ones_f[:, :], 1.0).then_inc(s["wog_r"], 1)
                for t in range(NT):
                    if t % 8 == 0:
                        dve.wait_ge(s["x_in"], 64)
                    last = nc.vector.bn_stats(st1[:, t, :], xs[:, t, :])
                c = Chain(dve, s["ln1c"], 19, 0)
                c(last)
                for t in range(NT):
                    last = nc.vector.bn_aggr(mv1[:, t, :], st1[:, t, :])
                c(last)
                c(nc.vector.tensor_scalar(ve1[:, :], mv1[:, :, 1], EPS, None, ALU.add))
                c(nc.vector.tensor_scalar(t1[:, :].bitcast(I32), ve1[:, :].bitcast(I32), 1, None, ALU.logical_shift_right))
                c(nc.vector.tensor_scalar(y1[:, 0:NT].bitcast(I32), t1[:, :].bitcast(I32), -1.0, MAGIC, ALU.mult, ALU.add))
                for _ in range(3):
                    c(nc.vector.tensor_tensor(t1[:, :], y1[:, 0:NT], y1[:, 0:NT], ALU.mult))
                    c(nc.vector.tensor_tensor(t1[:, :], t1[:, :], ve1[:, :], ALU.mult))
                    c(nc.vector.tensor_scalar(t1[:, :], t1[:, :], -0.5, 1.5, ALU.mult, ALU.add))
                    c(nc.vector.tensor_tensor(y1[:, 0:NT], y1[:, 0:NT], t1[:, :], ALU.mult))
                c(nc.vector.tensor_tensor(t1[:, :], mv1[:, :, 0], y1[:, 0:NT], ALU.mult))
                c(nc.vector.tensor_scalar(nmr1[:, 0:NT], t1[:, :], -1.0, None, ALU.mult))
                c.done()
                nc.vector.memset(cnt[:, :], 0.0).then_inc(s["ln1"], 1)
                dve.wait_ge(s["set_ps"], 4)
                nc.vector.tensor_copy(wqT[:, :], ps_s1[0][:, 0, 0:E])
                nc.vector.tensor_copy(wkT[:, :], ps_s1[0][:, 0, E:])
                nc.vector.tensor_copy(wvT[:, :], ps_s1[0][:, 1, 0:E])
                nc.vector.tensor_copy(woT[:, :, :].rearrange("p g e -> p (g e)"), ps_s1[1][:, :, :].rearrange("p q t -> p (q t)"))
                nc.vector.tensor_copy(b1t[:, :], ps_pv[:, 0:(NE + 1) * FC])
                nc.vector.tensor_copy(b2bc[:, 0:1024], ps_st[0][:, :, :, :].rearrange("p a q t -> p (a q t)"))
                nc.vector.tensor_copy(b2bc[:, 1024:], ps_st[1][:, 0, 0, 0:E]).then_inc(s["set_r"], 1)

                def reciprocals(b, g):
                    dve.wait_ge(s["db_ps"], G * b + g + 1)
                    wait(dve, s["on_r"], G * (b - 1) + g + 1)
                    nc.vector.reciprocal(rden[:, g, :], ps_mi[:, 0:S]).then_inc(s["rd_r"], 1)

                def residual(b, par):
                    dve.wait_ge(s["wo_ps"], b + 1)
                    wait(dve, s["x2keep"], b)
                    nc.vector.tensor_tensor(x2[:, :, :], ps_mi[:, 0:QT * E].rearrange("p (q e) -> p q e", q=QT), xs[:, bass.ds(QT * b, QT), :], ALU.add).then_inc(s["x2_r"], 1)
                    dve.wait_ge(s["x2_r"], b + 1)
                    c = Chain(dve, s["x2c"], 4, b, s["passed"])
                    for q in range(QT):
                        last = nc.vector.bn_stats(st2[:, q, :], x2[:, q, :])
                    c(last)
                    for q in range(QT):
                        last = nc.vector.bn_aggr(mv2[:, q, :], st2[:, q, :])
                    c(last)
                    c(nc.vector.tensor_scalar(ve2[:, :], mv2[:, :, 1], EPS, None, ALU.add))
                    c(nc.vector.tensor_scalar(t2[:, :].bitcast(I32), ve2[:, :].bitcast(I32), 1, None, ALU.logical_shift_right))
                    nc.vector.tensor_scalar(y2[:, :].bitcast(I32), t2[:, :].bitcast(I32), -1.0, MAGIC, ALU.mult, ALU.add).then_inc(s["y0_r"], 1)
                    wait(dve, s["scat"], 16 * QT * TOPK * (b - 1))
                    wait(dve, s["shared_out"], 16 * (b - 1))
                    nc.vector.tensor_copy(xrow[par][:, :, :, E:].bitcast(I32).rearrange("p q k o -> p (q k) o"), idrun[:, :].unsqueeze(2)).then_inc(s["id_r"], 1)
                    nc.vector.tensor_scalar(idrun[:, :], idrun[:, :], float(3 * S), None, ALU.add).then_inc(s["idc"], 1)
                    dve.wait_ge(s["idc"], b + 1)

                def route(b):
                    dve.wait_ge(s["rt_ps"], b + 1)
                    wait(dve, s["keep_r"], b)
                    nc.vector.tensor_copy(lg[:, :, :], ps_mi[:, 0:QT * NE].rearrange("p (q e) -> p q e", q=QT)).then_inc(s["lg_r"], 1)
                    wait_apart(dve, s["passed"], (s["lg_r"], b + 1))
                    for q in range(QT):
                        last = nc.vector.max(v8[:, q, :], lg[:, q, :])
                    last.then_inc(s["v8_r"], 1)
                    wait_apart(dve, s["passed"], (s["v8_r"], b + 1))
                    c = Chain(dve, s["rtc"], 3, b)
                    for q in range(QT):
                        last = nc.vector.max_index(i8[:, q, :], v8[:, q, :], lg[:, q, :])
                    c(last)
                    c(nc.vector.tensor_copy(idxf[:, :, :], i8[:, :, 0:TOPK]))
                    n = QT * TOPK
                    c(nc.vector.tensor_tensor(onehot[:, :, :, :].rearrange("p q k e -> p (q k) e"), con("iota8").unsqueeze(1).to_broadcast([P, n, NE]),
                                              idxf[:, :, :].rearrange("p q k -> p (q k)").unsqueeze(2).to_broadcast([P, n, NE]), ALU.is_equal))
                    nc.vector.tensor_tensor(taken[:, :, :], onehot[:, :, 0, :], onehot[:, :, 1, :], ALU.add).then_inc(s["taken_r"], 1)

                def places(b, par):
                    dve.wait_ge(s["pos_ps"], b + 1)
                    nc.vector.tensor_tensor(place[:, :, :], ps_mi[:, 0:QT * NE].rearrange("p (q e) -> p q e", q=QT),
                                            con("region").unsqueeze(1).to_broadcast([P, QT, NE]), ALU.add).then_inc(s["pos_r"], 1)
                    dve.wait_ge(s["pos_r"], b + 1)
                    c = Chain(dve, s["posc"], 3, b)
                    c(nc.vector.tensor_tensor(placed[:, :, :, :], onehot[:, :, :, :], place[:, :, :].unsqueeze(2).to_broadcast([P, QT, TOPK, NE]), ALU.mult))
                    c(nc.vector.tensor_reduce(slotf[:, :], placed[:, :, :, :].rearrange("p q k e -> p (q k) e"), AX.X, ALU.add))
                    wait(dve, s["scat"], 16 * QT * TOPK * (b - 1))
                    nc.vector.tensor_copy(slot[par][:, :], slotf[:, :]).then_inc(s["slot_r"], 1)
                    c(nc.vector.tensor_tensor(taken_sum[:, :], taken_sum[:, :], taken[:, 0, :], ALU.add))
                    c.done()
                    nc.vector.tensor_tensor(taken_sum[:, :], taken_sum[:, :], taken[:, 1, :], ALU.add).then_inc(s["tsum_r"], 1)

                def iteration(i, par):
                    for u in range(UNITS):
                        if has(i, 0):
                            if u == 0:
                                wait(dve, s["m_r"], i)
                            for a in range(2):
                                h = 2 * u + a
                                dve.wait_ge(s["s1_ps"], i * H + h + 1)
                                nc.vector.tensor_reduce(negmax[:, :, h:h + 1], ps_s1[h % 2][:, :, :], AX.X, ALU.max, negate=True).then_inc(s["max_r"], 1)
                        if u == 0 and has(i, -1):
                            dve.wait_ge(s["var_hi_r"], i + 2)
                            nc.vector.tensor_tensor(var_lo[:, :, :], ps_mi[0:H, :].rearrange("p (a t) -> p a t", a=2), var_hi[:, :, :], ALU.subtract).then_inc(s["var_lo_r"], 1)
                        if u == 1 and has(i, 2):
                            reciprocals(i - 2, 1)
                        if u == 2 and has(i, 2):
                            reciprocals(i - 2, 2)
                        if u == 3 and has(i, 3):
                            route(i - 3)
                        if u == 4 and has(i, 3):
                            places(i - 3, 1 - par)
                        if u == 4 and has(i, 2):
                            reciprocals(i - 2, 3)
                        if u == 6 and has(i, 2):
                            residual(i - 2, par)
                        if u == 7 and has(i, -2):
                            dve.wait_ge(s["sq_r"], i + 3)
                            nc.vector.tensor_tensor(qk_lo[:, :, :], ps_mi[:, :].rearrange("p (a t) -> p a t", a=2), qk_hi[:, :, :], ALU.subtract).then_inc(s["qk_lo_r"], 1)
                        if u == 7 and has(i, 1):
                            reciprocals(i - 1, 0)
                    if has(i, 0):
                        wait(dve, s["mt_ps"], i)
                        dve.wait_ge(s["max_r"], (i + 1) * H)
                        c = Chain(dve, s["mc"], 1, i)
                        c(nc.vector.tensor_copy(m_parts[:, :, 0, :], negmax[:, :, :]))
                        nc.vector.tensor_tensor(m_parts[:, :, 1, :], negmax[:, :, :], m_parts[:, :, 0, :], ALU.subtract).then_inc(s["m_r"], 1)

                run(dve, iteration)

                dve.wait_ge(s["cnt_ps"], 1)
                c = Chain(dve, s["endc"], 19, 0)
                c(nc.vector.tensor_copy(cnt[:, :], ps_mi[:, 0:NE]))
                c(nc.vector.tensor_tensor(padf[:, :], cnt[:, :], con("region"), ALU.add))
                c(nc.vector.tensor_scalar(padf[:, :], padf[:, :], con("part"), None, ALU.add))
                nc.vector.tensor_copy(padi[:, :], padf[:, :]).then_inc(s["pad_i_r"], 1)
                c(nc.vector.tensor_tensor(cmp_[:, :, :], cnt[:, :].unsqueeze(2).to_broadcast([P, NE, 32]), con("steps").unsqueeze(1).to_broadcast([P, NE, 32]), ALU.is_gt))
                c(nc.vector.tensor_reduce(ntile[:, :], cmp_[:, :, :], AX.X, ALU.add))
                c(nc.vector.tensor_tensor(low[:, :, :], con("lower").rearrange("p (a b) -> p a b", b=NE), ntile[:, :].unsqueeze(1).to_broadcast([P, NE, NE]), ALU.mult))
                c(nc.vector.tensor_reduce(tbase[:, :], low[:, :, :], AX.X, ALU.add))
                c(nc.vector.tensor_tensor(total[:, :], tbase[:, NE - 1:NE], ntile[:, NE - 1:NE], ALU.add))
                c(nc.vector.tensor_tensor(ge[:, :, :], con("tiles").unsqueeze(2).to_broadcast([P, RT_TILES, NE]), tbase[:, :].unsqueeze(1).to_broadcast([P, RT_TILES, NE]), ALU.is_ge))
                c(nc.vector.tensor_reduce(ex[:, :], ge[:, :, :], AX.X, ALU.add))
                c(nc.vector.tensor_tensor(gt_[:, :, :], ge[:, :, :], tbase[:, :].unsqueeze(1).to_broadcast([P, RT_TILES, NE]), ALU.mult))
                c(nc.vector.tensor_reduce(tb[:, :], gt_[:, :, :], AX.X, ALU.max))
                c(nc.vector.tensor_scalar(ex[:, :], ex[:, :], -1.0, None, ALU.add))
                c(nc.vector.tensor_tensor(tb[:, :], con("tiles"), tb[:, :], ALU.subtract))
                c(nc.vector.tensor_scalar(tb[:, :], tb[:, :], float(P), None, ALU.mult))
                c(nc.vector.scalar_tensor_tensor(stf[:, :], ex[:, :], float(REGION), tb[:, :], ALU.mult, ALU.add))
                c(nc.vector.tensor_scalar(dead[:, :], con("tiles"), total[:, 0:1], None, ALU.is_ge))
                c(nc.vector.scalar_tensor_tensor(tb[:, :], stf[:, :], -float(DUMMY), dead[:, :], ALU.add, ALU.mult))
                c(nc.vector.tensor_tensor(stf[:, :], stf[:, :], tb[:, :], ALU.subtract))
                c.done()
                nc.vector.tensor_copy(starts[:, NT:TILES], stf[:, :])
                nc.vector.tensor_copy(experts[:, NT:TILES], ex[:, :])
                nc.vector.tensor_copy(starts[:, 0:NT], con("shared_starts"))
                nc.vector.memset(experts[:, 0:NT], SHARED).then_inc(s["endc"], 1)
                dve.wait_ge(s["endc"], 20)

        experts_phase(nc, ctx, sb, sem, locals())


def experts_phase(nc, ctx, sb, sem, v):
    xs, w1h, w1l, w2, b1t, b2bc = (v[n] for n in ("xs", "w1h", "w1l", "w2", "b1t", "b2bc"))
    logits, top8, starts, experts, xrows, orows, out = (v[n] for n in ("logits", "top8", "starts", "experts", "xrows", "orows", "out"))
    ident, ps_pv, ps_mi, ps_s1, ps_st = v["con"]("ident"), v["ps_pv"], v["ps_mi"], v["ps_s1"], v["ps_st"]
    XB = 4
    xg = [sb(f"xg{i}", [P, XW]) for i in range(XB)]
    xT = [sb(f"xT{i}", [P, 2, P], BF16) for i in range(2)]
    hid = [sb(f"hid{i}", [P, FC, P]) for i in range(2)]
    yb = [sb(f"yb{i}", [P, E]) for i in range(XB)]
    dl = sb("dl", [P, NT, NE + 1])
    el = sb("el", [P, NT, NE + 1])
    esum, wt = sb("esum", [P, NT]), sb("wt", [P, 2, NT])
    CH = 4
    og = [sb(f"og{i}", [P, CH, 3, E]) for i in range(2)]
    ob = [sb(f"ob{i}", [P, CH, E]) for i in range(2)]
    ps_t = [ps_pv, ps_mi]
    ps_h = [ps_s1[i][:, :, :].rearrange("p q t -> p (q t)").rearrange("p (f t) -> p f t", f=FC) for i in range(2)]
    ps_y = [ps_st[i][:, 0, 0, 0:E] for i in range(2)]
    s = {n: sem("f_" + n) for n in "xt_ps xhi_r xlo_r h_ps h_r y_ps y_r wt_d wt_e wtc o_c o_r".split()}
    s_in, s_out = ([sem(f"f_{n}{j}") for j in range(XB)] for n in ("in", "out"))
    s_og, s_fin = ([sem(f"f_{n}{j}") for j in range(2)] for n in ("og", "fin"))
    NCH = NT // CH
    passed = v["s"]["passed"]

    with nc.Block() as block:
        @block.sync
        def _(sp):
            def fetch(r, j):
                wait_apart(sp, passed, (s_out[j], 16 * r))
                row = sp.value_load(starts[0:1, bass.ds(r * XB + j, 1)], min_val=0, max_val=XROWS - P)
                sp.dma_start(xg[j][:, :], xrows[bass.ds(row, P), :]).then_inc(s_in[j], 16)

            for j in range(XB):
                fetch(0, j)
            with sp.Fori(1, TILES // XB) as r:
                for j in range(XB):
                    fetch(r, j)
            for j in range(XB):
                sp.wait_ge(s_out[j], 16 * (TILES // XB))
            ov = orows.rearrange("(t p k) e -> p t k e", p=P, k=3)
            outv = out.rearrange("b (q p) e -> p (b q) e", p=P)

            def store(n):
                sp.wait_ge(s["o_r"], n + 1)
                sp.dma_start(outv[:, CH * n:CH * (n + 1), :], ob[n % 2][:, :, :]).then_inc(s_fin[n % 2], 16)

            for n in range(NCH):
                if n >= 2:
                    store(n - 2)
                sp.dma_start(og[n % 2][:, :, :, :], ov[:, CH * n:CH * (n + 1), :, :]).then_inc(s_og[n % 2], 16)
            store(NCH - 2)
            store(NCH - 1)
            for n in range(2):
                sp.wait_ge(s_fin[n], 16 * NCH // 2)

        @block.tensor
        def _(pe):
            def turn(r, j):
                t = r * XB + j
                pe.wait_ge(s_in[j], 16 * (r + 1))
                wait(pe, s["xlo_r"], t - 1)
                nc.tensor.transpose(ps_t[j % 2][:, 0:P], xg[j][:, 0:E], ident).then_inc(s["xt_ps"], 1)

            def up(t, par):
                e = pe.value_load(experts[0:1, bass.ds(t, 1)], min_val=0, max_val=NE)
                pe.wait_ge(s["xlo_r"], t + 1)
                wait(pe, s["h_r"], t - 1)
                for f in range(FC):
                    at = bass.ds(e * F + f * P, P)
                    nc.tensor.matmul(ps_h[par][:, f, :], w1h[:, at], xT[par][:, 0, :], start=True, stop=False)
                    nc.tensor.matmul(ps_h[par][:, f, :], w1h[:, at], xT[par][:, 1, :], start=False, stop=False)
                    last = nc.tensor.matmul(ps_h[par][:, f, :], w1l[:, at], xT[par][:, 0, :], start=False, stop=True)
                last.then_inc(s["h_ps"], 1)

            def down(t, par):
                e = pe.value_load(experts[0:1, bass.ds(t, 1)], min_val=0, max_val=NE)
                pe.wait_ge(s["h_r"], t + 1)
                wait(pe, s["y_r"], t - 1)
                for f in range(FC):
                    last = nc.tensor.matmul(ps_y[par], hid[par][:, f, :], w2[:, bass.ds(e * F + f * E, E)], start=f == 0, stop=f == FC - 1)
                last.then_inc(s["y_ps"], 1)

            def step(r, j):
                t = r * XB + j
                static = isinstance(r, int)
                if not static or t + 2 < TILES:
                    turn(r + (j + 2) // XB, (j + 2) % XB)
                if not static or t + 1 < TILES:
                    up(t + 1, (j + 1) % 2)
                down(t, j % 2)

            turn(0, 0)
            turn(0, 1)
            up(0, 0)
            for j in range(XB):
                step(0, j)
            with pe.Fori(1, TILES // XB - 1) as r:
                for j in range(XB):
                    step(r, j)
            for j in range(XB):
                step(TILES // XB - 1, j)

        @block.scalar
        def _(act):
            act.wait_ge(s["wt_d"], 1)
            nc.scalar.activation(el[:, :, :], dl[:, :, :], ACT.Exp).then_inc(s["wt_e"], 1)

            def silu(t, par):
                e = act.value_load(experts[0:1, bass.ds(t, 1)], min_val=0, max_val=NE)
                act.wait_ge(s["h_ps"], t + 1)
                wait(act, s["y_ps"], t - 1)
                for f in range(FC):
                    last = nc.scalar.activation(hid[par][:, f, :], ps_h[par][:, f, :], ACT.Silu, bias=b1t[:, bass.ds(e * FC + f, 1)])
                last.then_inc(s["h_r"], 1)

            silu(0, 0)
            silu(1, 1)
            with act.Fori(2, TILES, 2) as t:
                silu(t, 0)
                silu(t + 1, 1)

        @block.vector
        def _(dve):
            nc.vector.tensor_tensor(dl[:, :, 0:NE], logits[:, 0:NT, :], top8[:, 0:NT, 0:1].to_broadcast([P, NT, NE]), ALU.subtract)
            nc.vector.tensor_tensor(dl[:, :, NE:], top8[:, 0:NT, 1:2], top8[:, 0:NT, 0:1], ALU.subtract).then_inc(s["wt_d"], 1)
            dve.wait_ge(s["wt_e"], 1)
            c = Chain(dve, s["wtc"], 5, 0)
            c(nc.vector.tensor_reduce(esum[:, :], el[:, :, 0:NE], AX.X, ALU.add))
            c(nc.vector.scalar_tensor_tensor(esum[:, :], esum[:, :], EPS_W, el[:, :, NE], ALU.mult, ALU.add))
            c(nc.vector.tensor_scalar(esum[:, :], esum[:, :], 1.0, None, ALU.add))
            c(nc.vector.reciprocal(wt[:, 0, :], esum[:, :]))
            c(nc.vector.tensor_tensor(wt[:, 1, :], wt[:, 0, :], el[:, :, NE], ALU.mult))
            c.done()

            def parts(t, par):
                dve.wait_ge(s["xt_ps"], t + 1)
                wait(dve, s["h_ps"], t - 1)
                nc.vector.tensor_copy(xT[par][:, 0, :], ps_t[par][:, 0:P]).then_inc(s["xhi_r"], 1)
                dve.wait_ge(s["xhi_r"], t + 1)
                nc.vector.tensor_tensor(xT[par][:, 1, :], ps_t[par][:, 0:P], xT[par][:, 0, :], ALU.subtract).then_inc(s["xlo_r"], 1)

            def bias(r, j):
                t = r * XB + j
                e = dve.value_load(experts[0:1, bass.ds(t, 1)], min_val=0, max_val=NE)
                dve.wait_ge(s["y_ps"], t + 1)
                wait(dve, s_out[j], 16 * r)
                nc.vector.tensor_tensor(yb[j][:, :], ps_y[j % 2], b2bc[:, bass.ds(e * E, E)], ALU.add).then_inc(s["y_r"], 1)

            parts(0, 0)
            parts(1, 1)
            for j in range(XB):
                parts(j + 2, j % 2)
                bias(0, j)
            with dve.Fori(1, TILES // XB - 1) as r:
                for j in range(XB):
                    parts(r * XB + j + 2, j % 2)
                    bias(r, j)
            for j in range(XB):
                if j < XB - 2:
                    parts(TILES - XB + j + 2, j % 2)
                bias(TILES // XB - 1, j)

            for n in range(NCH):
                dve.wait_ge(s_og[n % 2], 16 * (n // 2 + 1))
                if n >= 2:
                    dve.wait_ge(s_fin[n % 2], 16 * (n // 2))
                o, g = ob[n % 2], og[n % 2]
                c = Chain(dve, s["o_c"], 2, n)
                c(nc.vector.scalar_tensor_tensor(o[:, :, :], g[:, :, 2, :], SHARED_SCALE, xs[:, CH * n:CH * (n + 1), :], ALU.mult, ALU.add))
                for k in range(TOPK):
                    for q in range(CH):
                        last = nc.vector.scalar_tensor_tensor(o[:, q, :], g[:, q, k, :], wt[:, k, CH * n + q:CH * n + q + 1], o[:, q, :], ALU.mult, ALU.add)
                    if k == 0:
                        c(last)
                last.then_inc(s["o_r"], 1)

        @block.gpsimd
        def _(pool):
            def send(r, j):
                wait_apart(pool, passed, (s["y_r"], r * XB + j + 1))
                nc.gpsimd.indirect_dma_start(out=orows, out_offset=bass.IndirectOffsetOnAxis(ap=xg[j][:, E:XW].bitcast(I32), axis=0),
                                             in_=yb[j][:, :], in_offset=None, bounds_check=OROWS - 1, oob_is_err=False).then_inc(s_out[j], 16)

            with pool.Fori(0, TILES // XB) as r:
                for j in range(XB):
                    send(r, j)


_INS = ["L0_attn_x", "L0_attn_Wq", "L0_attn_Wk", "L0_attn_Wv", "L0_attn_Wo", "L0_ffn_Wg", "L0_ffn_W1", "L0_ffn_b1",
        "L0_ffn_W2", "L0_ffn_b2", "L0_ffn_Ws1", "L0_ffn_bs1", "L0_ffn_Ws2", "L0_ffn_bs2"]


def kernel(**inputs):
    import concourse.bacc as _bacc
    from concourse.bass_utils import run_bass_kernel_spmd as _run

    nc = _bacc.Bacc("TRN2", target_bir_lowering=False, num_devices=1)
    arrays, args = {}, []
    for name in _INS:
        a = np.ascontiguousarray(inputs[name])
        arrays[name] = a
        args.append(nc.dram_tensor(name, a.shape, mybir.dt.from_np(a.dtype), kind="ExternalInput").ap())
    arrays["consts"] = constants()
    args.append(nc.dram_tensor("consts", [P, NCONST], F32, kind="ExternalInput").ap())
    args.append(nc.dram_tensor("result", [B, S, E], F32, kind="ExternalOutput").ap())
    block_kernel(nc, *args)
    r = _run(nc, [arrays], core_ids=[0])
    return r.results[0]["result"]
```

```python
from contextlib import ExitStack

import numpy as np
import concourse.bass as bass
from concourse import mybir

F32 = mybir.dt.float32
BF16 = mybir.dt.bfloat16
I32 = mybir.dt.int32
U32 = mybir.dt.uint32
ALU = mybir.AluOpType
ACT = mybir.ActivationFunctionType
AX = mybir.AxisListType

P = 128
B, S, E = 16, 256, 128
H = 16
D = E // H
QT = S // P
NT = B * QT
G = 4
HG = H // G
UNITS = H // 2
ROWS = 32
NE, F = 8, 512
FC = F // P
SHARED = NE
TOPK = 2
EPS = 1e-5
EPS_W = 1e-9
SHARED_SCALE = 0.1
TT = 256
TQ = TT // P
NS = B * S // TT
REGION = B * S + TT
DUMMY = NE * REGION
XROWS = DUMMY + TT
XW = E + 1
ROUTED_TILES = (TOPK * B * S + NE * (TT - 1)) // TT
XB = 8
TILES = -(-ROUTED_TILES // XB) * XB
XT = 4
OROWS = TOPK * B * S
REC_L, REC_W2, REC_B1, REC_B2, REC = F // 2, F, 2 * F, 2 * F + FC, 2 * F + FC + E
SKIP = 1 << 20
MAGIC = float(0x5F3759DF)

_COLS = [("ident", P), ("centre", P), ("centre_q", P), ("ind_q", H), ("ind_k", H), ("tri", P),
         ("iota8", NE), ("region", NE), ("ids", QT * TOPK), ("steps", NS), ("lower", NE * NE), ("tiles", TILES),
         ("part", TQ)]
COL = {}
for _n, _w in _COLS:
    COL[_n] = (sum(w for _, w in _COLS[:len(COL)]), _w)
NCONST = sum(w for _, w in _COLS)


def constants():
    c = np.zeros((P, NCONST), np.float32)

    def put(name, a):
        o, w = COL[name]
        c[:, o:o + w] = a

    same = (np.arange(P)[:, None] // D == np.arange(P)[None, :] // D).astype(np.float32)
    centre = np.eye(P, dtype=np.float32) - same / D
    ind = (np.arange(P)[:, None] // D == np.arange(H)[None, :]).astype(np.float32)
    put("ident", np.eye(P))
    put("centre", centre)
    put("centre_q", centre / D)
    put("ind_q", ind * (D / (D - 1)))
    put("ind_k", ind / (D - 1))
    put("tri", np.arange(P)[:, None] < np.arange(P)[None, :])
    put("iota8", np.arange(NE)[None, :])
    put("region", np.arange(NE)[None, :] * REGION)
    q, k = np.arange(QT)[None, :, None], np.arange(TOPK)[None, None, :]
    put("ids", (TOPK * (q * P + np.arange(P)[:, None, None]) + k).reshape(P, QT * TOPK))
    put("steps", np.arange(NS)[None, :] * TT)
    put("lower", (np.arange(NE)[None, :] < np.arange(NE)[:, None]).reshape(1, -1))
    put("tiles", np.arange(TILES)[None, :])
    put("part", np.arange(P)[:, None] + P * np.arange(TQ)[None, :])
    return c


def wait(eng, sem, value):
    if isinstance(value, int) and value <= 0:
        return
    eng.wait_ge(sem, value)


def wait_apart(eng, passed, *waits):
    for sem, value in waits:
        wait(eng, sem, value)
        eng.sem_inc(passed, 1)


class Chain:

    def __init__(self, eng, sem, steps, rnd, passed=None):
        self.eng, self.sem, self.steps, self.base, self.n, self.passed = eng, sem, steps, steps * rnd, 0, passed

    def __call__(self, ins):
        self.n += 1
        assert self.n <= self.steps
        ins.then_inc(self.sem, 1)
        if self.passed is None:
            self.eng.wait_ge(self.sem, self.base + self.n)
        else:
            wait_apart(self.eng, self.passed, (self.sem, self.base + self.n))

    def done(self):
        assert self.n == self.steps, (self.n, self.steps)


def block_kernel(nc, x, Wq, Wk, Wv, Wo, Wg, W1, b1, W2, b2, Ws1, bs1, Ws2, bs2, consts, out):
    ctx = ExitStack()
    with ctx:
        def sb(name, shape, dt=F32):
            return ctx.enter_context(nc.sbuf_tensor(name, shape, dt))

        def sem(name):
            return ctx.enter_context(nc.semaphore(name))

        dq = [nc.dram_tensor(f"dq{i}", [H, ROWS, S], BF16, kind="Internal").ap() for i in range(2)]
        dk = [nc.dram_tensor(f"dk{i}", [H, ROWS, S], BF16, kind="Internal").ap() for i in range(2)]
        xrows = nc.dram_tensor("xrows", [XROWS, XW], F32, kind="Internal").ap()
        orows = nc.dram_tensor("orows", [OROWS, E], F32, kind="Internal").ap()

        xs = sb("xs", [P, NT + 2, E])
        cst = sb("cst", [P, NCONST])
        records = sb("records", [P, NE + 1, REC])
        w1f = sb("w1f", [P, NE + 1, F])
        x2nT_all = w1f[:, :, :].rearrange("p e f -> p (e f)")
        logits = sb("logits", [P, NT + 2, NE])
        top8 = sb("top8", [P, NT + 2, 8])
        pad_row = sb("pad_row", [P, XW])
        starts = sb("starts", [P, TILES + XB], I32)
        experts = sb("experts", [P, TILES + XB], I32)

        def con(name, rows=P):
            o, w = COL[name]
            return cst[0:rows, o:o + w]

        phase1 = ExitStack()

        def sb1(name, shape, dt=F32):
            return phase1.enter_context(nc.sbuf_tensor(name, shape, dt))

        wraw = sb1("wraw", [P, 4, E])
        wqT, wkT, wvT = sb1("wqT", [P, E]), sb1("wkT", [P, E]), sb1("wvT", [P, E])
        woT = sb1("woT", [P, E])
        wg = sb1("wg", [P, NE])
        b1r = sb1("b1r", [(NE + 1) * FC, P])
        b2r = sb1("b2r", [1, (NE + 1) * E])
        ones_f = sb1("ones_f", [1, P])
        ident_b, tri_b, ones_b = sb1("ident_b", [P, P], BF16), sb1("tri_b", [P, P], BF16), sb1("ones_b", [P, P], BF16)
        fill = sb1("fill", [P, 2, G, S], BF16)
        st1 = sb1("st1", [P, NT, 6])
        mv1 = sb1("mv1", [P, NT, 2])
        ve1, y1, t1 = sb1("ve1", [P, NT]), sb1("y1", [P, NT + 2]), sb1("t1", [P, NT])
        nmr1 = sb1("nmr1", [P, NT + 2])
        xn = sb1("xn", [P, QT, E])
        xnT = [sb1(f"xnT{i}", [P, S]) for i in range(2)]
        qk_parts = sb1("qk_parts", [P, 6, S], BF16)
        qk_hi, qk_hi2, qk_lo = qk_parts[:, 0:5:4, :], qk_parts[:, 1:6:4, :], qk_parts[:, 2:4, :]
        qk_sq = sb1("qk_sq", [P, 2, S])
        var_hi, var_lo = sb1("var_hi", [H, 2, S], BF16), sb1("var_lo", [H, 2, S], BF16)
        qa = [sb1(f"qa{i}", [P, G, S], BF16) for i in range(2)]
        ka = [sb1(f"ka{i}", [P, G, HG, S], BF16) for i in range(2)]
        vx = [sb1(f"vx{i}", [P, QT, H, ROWS]) for i in range(2)]
        negmax = sb1("negmax", [P, QT, H])
        m_parts = sb1("m_parts", [P, QT, G, 2, HG], BF16)
        mT = sb1("mT", [2 * HG, G, S], BF16)
        probs = [sb1(f"probs{i}", [P, HG, QT, S]) for i in range(2)]
        oT = sb1("oT", [P, G, S])
        rden = sb1("rden", [P, G, QT, HG])
        on = sb1("on", [P, QT, E])
        onT = sb1("onT", [P, S])
        x2 = sb1("x2", [P, QT, E])
        st2, mv2 = sb1("st2", [P, QT, 6]), sb1("mv2", [P, QT, 2])
        ve2, y2, t2, nmr2 = sb1("ve2", [P, QT]), sb1("y2", [P, QT]), sb1("t2", [P, QT]), sb1("nmr2", [P, QT])
        xrow = [sb1(f"xrow{i}", [P, QT, TOPK, XW]) for i in range(2)]
        idrun = sb1("idrun", [P, QT * TOPK])
        x2nT = sb1("x2nT", [P, S])
        lg, v8 = sb1("lg", [P, QT, NE]), sb1("v8", [P, QT, 8])
        i8 = sb1("i8", [P, QT, 8], U32)
        idxf = sb1("idxf", [P, QT, TOPK])
        onehot = sb1("onehot", [P, QT, TOPK, NE])
        taken = sb1("taken", [P, QT, NE], BF16)
        taken_sum = sb1("taken_sum", [P, NE], BF16)
        place = sb1("place", [P, QT, NE])
        placed = sb1("placed", [P, QT, TOPK, NE])
        slotf = sb1("slotf", [P, QT * TOPK])
        slot = [sb1(f"slot{i}", [P, QT * TOPK], I32) for i in range(2)]

        ps = ctx.enter_context(nc.psum_tensor("ps", [P, 8, 512], F32))
        ps_s1 = [ps[:, q, :].rearrange("p (a t) -> p a t", a=2) for q in range(QT)]
        ps_st = [ps[:, 2 + a, :] for a in range(2)]
        ps_pv = ps[:, 4, :]
        STEPS = "VAR MT OTT1 OTT2 X2T RT OTT3 V POS T ONT QK WO OTT0".split()
        mi = {n: ps[:, 5 + k % 3, :] for k, n in enumerate(STEPS)}

        names = """x_in c_in w_in b_in w1_in w2_in fill_out set_ps set_r vx_init ka_zero fill_r init_r ln1 ln1c ones_r
            xn_r xnc xt_ps xnT_r qk_ps qk_hi_r sq_r qk_lo_r var_ps var_hi_r var_lo_r rows_out
            max_r m_r mc mt_ps mt_r mrow_in s1_ps st_ps exp_r pv_ps ot_r ott_ps rd_r on_r ont_ps onT_r v_ps v_r
            wo_ps x2_r x2c y0_r n2c xrow_r x2keep id_r idc x2t_ps x2nT_r xkeep rt_ps lg_r rtc v8_r keep_r taken_r pos_ps pos_r posc slot_r
            tsum_r scat cnt_ps pads_out split_r passed""".split()
        s = {n: sem("s_" + n) for n in names}
        s_ld = [sem(f"s_ld{half}") for half in range(2)]
        LOADS, ROWS_OUT, MROWS = 16 * (1 + HG), 16 * 6, 16 * 2

        FIRST, LAST = -2, B + 3

        def has(i, lag):
            return 0 <= i - lag < B if isinstance(i, int) else True

        def pass2_at(i, u):
            return (i - 1, u - 2, 1) if u >= 2 else (i - 2, u + 6, 2)

        def pv_at(i, u):
            k = (u - 3) % UNITS
            b, lag = (i - 1, 1) if u >= 3 else (i - 2, 2)
            return b, (k // 2 if k % 2 else None), lag

        def run(eng, iteration):
            for i in range(FIRST, 6):
                iteration(i, i % 2)
            with eng.Fori(6, B - 2, 2) as i:
                iteration(i, 0)
                iteration(i + 1, 1)
            for i in range(B - 2, LAST):
                iteration(i, i % 2)

        with nc.Block() as block:
            @block.sync
            def _(sp):
                sp.dma_start(cst[:, :], consts).then_inc(s["c_in"], 16)
                for n, w in enumerate((Wq, Wk, Wv, Wo)):
                    sp.dma_start(wraw[:, n, :], w).then_inc(s["w_in"], 16)
                for n in range(4):
                    sp.dma_start(xs[:, 8 * n:8 * n + 8, :], x.rearrange("b (q p) e -> p (b q) e", p=P)[:, 8 * n:8 * n + 8, :]).then_inc(s["x_in"], 16)
                sp.dma_start(wg[:, :], Wg).then_inc(s["w_in"], 16)
                sp.dma_start(b1r[0:NE * FC, :], b1.rearrange("e (f p) -> (e f) p", p=P)).then_inc(s["b_in"], 16)
                sp.dma_start(b1r[NE * FC:, :], bs1.rearrange("(f p) -> f p", p=P)).then_inc(s["b_in"], 16)
                sp.dma_start(b2r[:, 0:NE * E], b2.rearrange("(o e) h -> o (e h)", o=1)).then_inc(s["b_in"], 16)
                sp.dma_start(b2r[:, NE * E:], bs2.rearrange("(o h) -> o h", o=1)).then_inc(s["b_in"], 16)
                sp.wait_ge(s["fill_r"], 3)
                for i in range(2):
                    sp.dma_start(dq[i].rearrange("(g j) r t -> (j r) g t", g=G), fill[:, 0, :, :]).then_inc(s["fill_out"], 16)
                    sp.dma_start(dk[i].rearrange("(g j) r t -> (j r) g t", g=G), fill[:, 0, :, :]).then_inc(s["fill_out"], 16)
                sp.wait_ge(s["fill_out"], 64)
                for i in range(2):
                    sp.dma_start(dk[i][:, 3 * D + 3:3 * D + 5, :], fill[0:2 * H, 1, 0, :]).then_inc(s["fill_out"], 16)
                for q in range(TQ):
                    sp.dma_start(xrows[DUMMY + q * P:DUMMY + (q + 1) * P, :], pad_row[:, :]).then_inc(s["fill_out"], 16)
                sp.wait_ge(s["fill_out"], 64 + 16 * (2 + TQ))
                sp.dma_start(w1f[:, 0:NE, :], W1.rearrange("e h f -> h e f")).then_inc(s["w1_in"], 16)
                sp.dma_start(w1f[:, NE, :], Ws1).then_inc(s["w1_in"], 16)
                w2v = records[:, :, REC_W2:REC_B1].rearrange("p e (f h) -> p e f h", f=FC)
                for e in range(NE):
                    sp.dma_start(w2v[:, e, :, :], W2[e].rearrange("(f p) h -> p f h", p=P)).then_inc(s["w2_in"], 16)
                sp.dma_start(w2v[:, NE, :, :], Ws2.rearrange("(f p) h -> p f h", p=P)).then_inc(s["w2_in"], 16)

                def load(b, par, half):
                    wait(sp, s["st_ps"], H * (b - 2) + 8 * half + 8)
                    at = slice(2 * half, 2 * half + 2)
                    sp.dma_start(qa[par][:, at, :], dq[par].rearrange("(g j) r t -> (j r) g t", g=G)[:, at, :]).then_inc(s_ld[half], 16)
                    if isinstance(b, int) and b == 0 and half == 0:
                        sp.wait_ge(s["ka_zero"], 1)
                    for j in range(HG):
                        sp.dma_start(ka[par][ROWS * j:ROWS * (j + 1), at, j, :], dk[par].rearrange("(g j) r t -> j r g t", g=G)[j][:, at, :]).then_inc(s_ld[half], 16)

                def iteration(i, par):
                    nxt = 1 - par
                    if has(i, -1):
                        b = i + 1
                        wait_apart(sp, s["passed"], *((s_ld[half], LOADS * (b - 1)) for half in range(2)))
                        sp.wait_ge(s["qk_lo_r"], b + 1)
                        for side, dram in ((0, dq), (1, dk)):
                            sp.dma_start(dram[nxt][:, 0:3 * D, :].rearrange("h (d n) t -> h d (n t)", n=3),
                                         qk_parts[:, 3 * side:3 * side + 3, :].rearrange("p n t -> p (n t)")).then_inc(s["rows_out"], 16)
                    if has(i, 1):
                        sp.wait_ge(s["mt_r"], i)
                        for c in range(2):
                            sp.dma_start(qa[nxt][3 * D + 3 + c::ROWS, :, :], mT[HG * c:HG * (c + 1), :, :]).then_inc(s["mrow_in"], 16)
                    if has(i, -1):
                        sp.wait_ge(s["var_lo_r"], b + 1)
                        for side, dram, hi, lo in ((0, dq, 0, 2), (1, dk, 1, 0)):
                            rows = dram[nxt][:, 3 * D:3 * D + 3, :]
                            sp.dma_start(rows[:, hi:hi + 2, :], var_hi[:, side, :].unsqueeze(1).to_broadcast([H, 2, S])).then_inc(s["rows_out"], 16)
                            sp.dma_start(rows[:, lo, :], var_lo[:, side, :]).then_inc(s["rows_out"], 16)
                    if has(i, 0):
                        load(i, par, 1)
                    if has(i, -1):
                        sp.wait_ge(s["rows_out"], ROWS_OUT * (i + 2))
                        load(i + 1, nxt, 0)

                run(sp, iteration)
                sp.wait_ge(s["w2_in"], 16 * (NE + 1))

            @block.gpsimd
            def _(pool):
                nc.gpsimd.memset(fill[:, 0, :, :], 0.0).then_inc(s["fill_r"], 1)
                nc.gpsimd.memset(fill[:, 1, :, :], 1.0).then_inc(s["fill_r"], 1)
                nc.gpsimd.memset(pad_row[:, 0:E], 0.0)
                nc.gpsimd.memset(pad_row[:, E:].bitcast(I32), SKIP).then_inc(s["fill_r"], 1)
                for i in range(2):
                    last = nc.gpsimd.memset(ka[i][:, :, :, :], 0.0)
                last.then_inc(s["ka_zero"], 1)
                for i in range(2):
                    nc.gpsimd.memset(vx[i][:, :, :, :], 0.0).then_inc(s["init_r"], 1)
                pool.wait_ge(s["init_r"], 2)
                for i in range(2):
                    last = nc.gpsimd.memset(vx[i][:, :, :, D:D + 1], 1.0)
                last.then_inc(s["vx_init"], 1)

                def layer_norm_in(b, par):
                    if isinstance(b, int) and b == 0:
                        pool.wait_ge(s["ln1"], 1)
                    wait(pool, s["xt_ps"], b)
                    at = bass.ds(QT * b, QT)
                    c = Chain(pool, s["xnc"], 1, b)
                    c(nc.gpsimd.tensor_tensor(xn[:, :, :], xs[:, at, :], y1[:, at].unsqueeze(2).to_broadcast([P, QT, E]), ALU.mult))
                    nc.gpsimd.tensor_tensor(xn[:, :, :], xn[:, :, :], nmr1[:, at].unsqueeze(2).to_broadcast([P, QT, E]), ALU.add).then_inc(s["xn_r"], 1)

                def rows_of_tokens(b, par):
                    pool.wait_ge(s["y0_r"], b + 1)
                    c = Chain(pool, s["n2c"], 14, b, s["passed"])
                    for _ in range(3):
                        c(nc.gpsimd.tensor_tensor(t2[:, :], y2[:, :], y2[:, :], ALU.mult))
                        c(nc.gpsimd.tensor_tensor(t2[:, :], t2[:, :], ve2[:, :], ALU.mult))
                        c(nc.gpsimd.tensor_scalar(t2[:, :], t2[:, :], -0.5, 1.5, ALU.mult, ALU.add))
                        c(nc.gpsimd.tensor_tensor(y2[:, :], y2[:, :], t2[:, :], ALU.mult))
                    c(nc.gpsimd.tensor_tensor(t2[:, :], mv2[:, :, 0], y2[:, :], ALU.mult))
                    c(nc.gpsimd.tensor_scalar(nmr2[:, :], t2[:, :], -1.0, 0.0, ALU.mult, ALU.add))
                    c.done()
                    wait_apart(pool, s["passed"], (s["scat"], 16 * QT * TOPK * (b - 1)))
                    for q in range(QT):
                        last = nc.gpsimd.tensor_scalar(xrow[par][:, q, :, 0:E], x2[:, q, :].unsqueeze(1).to_broadcast([P, TOPK, E]),
                                                       y2[:, q:q + 1], nmr2[:, q:q + 1], ALU.mult, ALU.add)
                    last.then_inc(s["xrow_r"], 1)
                    nc.gpsimd.tensor_copy(xs[:, bass.ds(QT * b, QT), :], x2[:, :, :]).then_inc(s["x2keep"], 1)

                def keep_columns(b):
                    pool.wait_ge(s["x2nT_r"], b + 1)
                    if isinstance(b, int) and b == 0:
                        pool.wait_ge(s["split_r"], 2 * (NE + 1))
                    nc.gpsimd.tensor_copy(x2nT_all[:, bass.ds(S * b, S)], x2nT[:, :]).then_inc(s["xkeep"], 1)

                def scatter(b, par):
                    pool.wait_ge(s["v8_r"], b + 1)
                    nc.gpsimd.tensor_copy(logits[:, bass.ds(QT * b, QT), :], lg[:, :, :])
                    nc.gpsimd.tensor_copy(top8[:, bass.ds(QT * b, QT), :], v8[:, :, :]).then_inc(s["keep_r"], 1)
                    wait_apart(pool, s["passed"], (s["slot_r"], b + 1), (s["id_r"], b + 1), (s["xrow_r"], b + 1),
                               (s["scat"], 16 * QT * TOPK * b))
                    for q in range(QT):
                        for k in range(TOPK):
                            n = q * TOPK + k
                            nc.gpsimd.indirect_dma_start(out=xrows, out_offset=bass.IndirectOffsetOnAxis(ap=slot[par][:, n:n + 1], axis=0),
                                                         in_=xrow[par][:, q, k, :], in_offset=None,
                                                         bounds_check=XROWS - 1, oob_is_err=False).then_inc(s["scat"], 16)

                def split_w1(e):
                    c = Chain(pool, s["split_r"], 2, e)
                    high, low = records[:, e, 0:REC_L].bitcast(BF16), records[:, e, REC_L:REC_W2].bitcast(BF16)
                    c(nc.gpsimd.tensor_copy(high, w1f[:, e, :]))
                    c(nc.gpsimd.tensor_tensor(low, w1f[:, e, :], high, ALU.subtract))

                def iteration(i, par):
                    nxt = 1 - par
                    if has(i, -2):
                        layer_norm_in(i + 2, par)
                    if has(i, 3):
                        rows_of_tokens(i - 3, nxt)
                        keep_columns(i - 3)
                        scatter(i - 3, nxt)
                    if isinstance(i, int) and -1 <= i <= 1:
                        if i == -1:
                            pool.wait_ge(s["w1_in"], 32)
                        for e in range(3 * (i + 1), 3 * (i + 2)):
                            split_w1(e)

                run(pool, iteration)

            @block.scalar
            def _(act):
                def iteration(i, par):
                    nxt = 1 - par
                    for u in range(UNITS):
                        if u == 0 and has(i, -1):
                            b = i + 1
                            act.wait_ge(s["var_ps"], b + 1)
                            wait(act, s["rows_out"], ROWS_OUT * b)
                            nc.scalar.activation(var_hi[:, :, :], mi["VAR"][0:H, :].rearrange("p (a t) -> p a t", a=2), ACT.Copy).then_inc(s["var_hi_r"], 1)
                        if u == 3 and has(i, 3):
                            b = i - 3
                            act.wait_ge(s["x2t_ps"], b + 1)
                            wait(act, s["rt_ps"], b)
                            wait(act, s["xkeep"], b)
                            nc.scalar.activation(x2nT[:, :], mi["X2T"][:, 0:S], ACT.Copy).then_inc(s["x2nT_r"], 1)
                        if u == 6 and has(i, 2):
                            b = i - 2
                            act.wait_ge(s["ont_ps"], b + 1)
                            wait(act, s["wo_ps"], b)
                            nc.scalar.activation(onT[:, :], mi["ONT"][:, 0:S], ACT.Copy).then_inc(s["onT_r"], 1)
                        b, k, lag = pass2_at(i, u)
                        if has(i, lag):
                            g = k // 2
                            for a in range(2):
                                act.wait_ge(s["st_ps"], H * b + 2 * k + a + 1)
                                if a == 0:
                                    wait(act, s["pv_ps"], G * b + g - 1)
                                nc.scalar.activation(probs[g % 2][:, 2 * (k % 2) + a, :, :].rearrange("p q t -> p (q t)"), ps_st[a], ACT.Exp).then_inc(s["exp_r"], 1)
                        b, g, lag = pv_at(i, u)
                        if g is not None and has(i, lag):
                            act.wait_ge(s["pv_ps"], G * b + g + 1)
                            wait(act, s["ott_ps"], G * (b - 1) + g + 1)
                            nc.scalar.activation(oT[:, g, :], ps_pv[:, 0:S], ACT.Copy).then_inc(s["ot_r"], 1)
                        if u == 0 and has(i, 1):
                            b = i - 1
                            act.wait_ge(s["mt_ps"], b + 1)
                            wait(act, s["mrow_in"], MROWS * b)
                            nc.scalar.activation(mT[:, :, :].rearrange("p g t -> p (g t)"), mi["MT"].bitcast(BF16)[0:2 * HG, :], ACT.Copy).then_inc(s["mt_r"], 1)
                        if u == 4 and has(i, 0):
                            act.wait_ge(s["v_ps"], i + 1)
                            wait(act, s["pv_ps"], G * (i - 1))
                            if isinstance(i, int) and i == 0:
                                act.wait_ge(s["vx_init"], 1)
                            for q in range(QT):
                                last = nc.scalar.activation(vx[par][:, q, :, 0:D], mi["V"][:, q * E:(q + 1) * E].rearrange("p (h d) -> p h d", d=D), ACT.Copy)
                            last.then_inc(s["v_r"], 1)
                        if u == 5 and has(i, -2):
                            b = i + 2
                            act.wait_ge(s["xt_ps"], b + 1)
                            wait(act, s["v_ps"], b - 1)
                            nc.scalar.activation(xnT[par][:, :], mi["T"][:, 0:S], ACT.Copy).then_inc(s["xnT_r"], 1)
                        if u == 6 and has(i, -2):
                            b = i + 2
                            act.wait_ge(s["qk_ps"], b + 1)
                            wait(act, s["rows_out"], ROWS_OUT * b)
                            src = mi["QK"].rearrange("p (a t) -> p a t", a=2)
                            nc.scalar.activation(qk_hi, src, ACT.Copy).then_inc(s["qk_hi_r"], 1)
                            wait(act, s["var_ps"], b)
                            nc.scalar.activation(qk_sq[:, :, :], src, ACT.Square).then_inc(s["sq_r"], 1)

                run(act, iteration)

            @block.tensor
            def _(pe):
                pe.wait_ge(s["c_in"], 16)
                pe.wait_ge(s["w_in"], 16 * 5)
                nc.tensor.matmul(ps_s1[0][:, 0, 0:E], wraw[:, 0, :], con("centre_q"), start=True, stop=True)
                nc.tensor.matmul(ps_s1[0][:, 0, E:2 * E], wraw[:, 1, :], con("centre"), start=True, stop=True)
                nc.tensor.matmul(ps_s1[0][:, 1, 0:E], wraw[:, 2, :], con("ident"), start=True, stop=True)
                nc.tensor.matmul(ps_s1[0][:, 1, E:2 * E], wraw[:, 3, :], con("ident"), start=True, stop=True).then_inc(s["set_ps"], 1)
                pe.wait_ge(s["b_in"], 64)
                nb = (NE + 1) * FC
                nc.tensor.transpose(ps_pv[:, 0:nb], b1r[:, :], con("ident", nb)[:, 0:nb]).then_inc(s["set_ps"], 1)
                pe.wait_ge(s["ones_r"], 1)
                for a in range(3):
                    n = min(512, (NE + 1) * E - 512 * a)
                    last = nc.tensor.matmul(ps[:, 5 + a, 0:n], ones_f[:, :], b2r[:, 512 * a:512 * a + n], start=True, stop=True)
                last.then_inc(s["set_ps"], 1)
                pe.wait_ge(s["set_r"], 1)

                prev = [None] * 3

                def misc(step, sem_name, value):
                    k = STEPS.index(step) % 3
                    if prev[k] is not None:
                        pe.wait_ge(s[prev[k][0]], prev[k][1])
                    prev[k] = (sem_name, value)
                    return mi[step]

                def heads_out(b, g):
                    pe.wait_ge(s["ot_r"], G * b + g + 1)
                    bank = misc(f"OTT{g}", "on_r", G * b + g + 1)
                    for q in range(QT):
                        last = nc.tensor.transpose(bank[:, q * P:(q + 1) * P], oT[:, g, q * P:(q + 1) * P], con("ident"))
                    last.then_inc(s["ott_ps"], 1)

                def step_a(i, par, u):
                    if u == 0 and has(i, -1):
                        b = i + 1
                        pe.wait_ge(s["sq_r"], b + 1)
                        bank = misc("VAR", "var_lo_r", b + 1)
                        nc.tensor.matmul(bank[0:H, 0:S], con("ind_q"), qk_sq[:, 0, :], start=True, stop=True)
                        nc.tensor.matmul(bank[0:H, S:2 * S], con("ind_k"), qk_sq[:, 1, :], start=True, stop=True).then_inc(s["var_ps"], 1)
                    if u == 1 and has(i, 2):
                        heads_out(i - 2, 1)
                    if u == 3 and has(i, 3):
                        b = i - 3
                        pe.wait_ge(s["xrow_r"], b + 1)
                        bank = misc("X2T", "x2nT_r", b + 1)
                        for q in range(QT):
                            last = nc.tensor.transpose(bank[:, q * P:(q + 1) * P], xrow[1 - par][:, q, 0, 0:E], con("ident"))
                        last.then_inc(s["x2t_ps"], 1)
                    if u == 4 and has(i, 2):
                        heads_out(i - 2, 3)
                    if u == 5 and has(i, 3):
                        b = i - 3
                        pe.wait_ge(s["taken_r"], b + 1)
                        pe.wait_ge(s["tsum_r"], b + 1)
                        bank = misc("POS", "pos_r", b + 1)
                        nc.tensor.matmul(bank[:, 0:NE], tri_b[:, :], taken[:, 0, :], start=True, stop=False)
                        nc.tensor.matmul(bank[:, 0:NE], ones_b[:, :], taken_sum[:, :], start=False, stop=True)
                        nc.tensor.matmul(bank[:, NE:2 * NE], tri_b[:, :], taken[:, 1, :], start=True, stop=False)
                        nc.tensor.matmul(bank[:, NE:2 * NE], ones_b[:, :], taken[:, 0, :], start=False, stop=False)
                        nc.tensor.matmul(bank[:, NE:2 * NE], ones_b[:, :], taken_sum[:, :], start=False, stop=True).then_inc(s["pos_ps"], 1)
                    if u == 6 and has(i, 2):
                        b = i - 2
                        pe.wait_ge(s["on_r"], G * (b + 1))
                        bank = misc("ONT", "onT_r", b + 1)
                        for q in range(QT):
                            last = nc.tensor.transpose(bank[:, q * P:(q + 1) * P], on[:, q, :], con("ident"))
                        last.then_inc(s["ont_ps"], 1)
                    if u == 7 and has(i, 2):
                        b = i - 2
                        pe.wait_ge(s["onT_r"], b + 1)
                        bank = misc("WO", "x2_r", b + 1)
                        for q in range(QT):
                            last = nc.tensor.matmul(bank[:, q * E:(q + 1) * E], onT[:, q * P:(q + 1) * P], woT[:, :], start=True, stop=True)
                        last.then_inc(s["wo_ps"], 1)

                def step_b(i, par, u):
                    if u == 0 and has(i, 1):
                        b = i - 1
                        pe.wait_ge(s["m_r"], b + 1)
                        bank = misc("MT", "mt_r", b + 1)
                        for g in range(G):
                            for q in range(QT):
                                last = nc.tensor.transpose(bank.bitcast(BF16)[0:2 * HG, g * S + q * P:g * S + (q + 1) * P],
                                                           m_parts[:, q, g, :, :].rearrange("p c j -> p (c j)"), ident_b[:, :])
                        last.then_inc(s["mt_ps"], 1)
                    if u == 2 and has(i, 2):
                        heads_out(i - 2, 2)
                    if u == 3 and has(i, 3):
                        b = i - 3
                        pe.wait_ge(s["x2nT_r"], b + 1)
                        bank = misc("RT", "lg_r", b + 1)
                        for q in range(QT):
                            last = nc.tensor.matmul(bank[:, q * NE:(q + 1) * NE], x2nT[:, q * P:(q + 1) * P], wg[:, :], start=True, stop=True)
                        last.then_inc(s["rt_ps"], 1)
                    if u == 4 and has(i, 0):
                        pe.wait_ge(s["xnT_r"], i + 1)
                        bank = misc("V", "v_r", i + 1)
                        for q in range(QT):
                            last = nc.tensor.matmul(bank[:, q * E:(q + 1) * E], xnT[par][:, q * P:(q + 1) * P], wvT[:, :], start=True, stop=True)
                        last.then_inc(s["v_ps"], 1)
                    if u == 5 and has(i, -2):
                        b = i + 2
                        pe.wait_ge(s["xn_r"], b + 1)
                        bank = misc("T", "xnT_r", b + 1)
                        for q in range(QT):
                            last = nc.tensor.transpose(bank[:, q * P:(q + 1) * P], xn[:, q, :], con("ident"))
                        last.then_inc(s["xt_ps"], 1)
                    if u == 6 and has(i, -2):
                        b = i + 2
                        pe.wait_ge(s["xnT_r"], b + 1)
                        bank = misc("QK", "qk_lo_r", b + 1)
                        nc.tensor.matmul(bank[:, 0:S], wqT[:, :], xnT[par][:, :], start=True, stop=True)
                        nc.tensor.matmul(bank[:, S:2 * S], wkT[:, :], xnT[par][:, :], start=True, stop=True).then_inc(s["qk_ps"], 1)
                    if u == 7 and has(i, 1):
                        heads_out(i - 1, 0)

                def iteration(i, par):
                    if not isinstance(i, int) or i == B - 2:
                        prev[:] = ("x2_r", i - 2), ("on_r", (i - 2) * G + 1), ("qk_lo_r", i + 2)
                    for u in range(UNITS):
                        if has(i, 0):
                            g = u // 2
                            if u % 4 == 0:
                                pe.wait_ge(s_ld[u // 4], LOADS * (i + 1))
                            j = 2 * (u % 2)
                            for q in range(QT):
                                wait(pe, s["max_r"], QT * (UNITS * i + u - 1) + q + 1)
                                nc.tensor.matmul(ps_s1[q][:, :, :], qa[par][:, g, q * P:(q + 1) * P], ka[par][:, g, j:j + 2, :],
                                                 start=True, stop=True).then_inc(s["s1_ps"], 1)
                        step_a(i, par, u)
                        b, k, lag = pass2_at(i, u)
                        if has(i, lag):
                            bp = (par + lag) % 2
                            if k == 0:
                                pe.wait_ge(s["mrow_in"], MROWS * (b + 1))
                            for a in range(2):
                                h = 2 * k + a
                                g, j = h // HG, h % HG
                                wait(pe, s["exp_r"], H * b + h - 1)
                                for q in range(QT):
                                    last = nc.tensor.matmul(ps_st[a][:, q * S:(q + 1) * S], ka[bp][:, g, j, q * P:(q + 1) * P], qa[bp][:, g, :], start=True, stop=True)
                                last.then_inc(s["st_ps"], 1)
                        b, g, lag = pv_at(i, u)
                        if g is not None and has(i, lag):
                            bp = (par + lag) % 2
                            if g == 0:
                                pe.wait_ge(s["v_r"], b + 1)
                            pe.wait_ge(s["exp_r"], H * b + HG * (g + 1))
                            wait(pe, s["ot_r"], G * b + g)
                            for q in range(QT):
                                for j in range(HG):
                                    last = nc.tensor.matmul(ps_pv[ROWS * j:ROWS * (j + 1), 0:S], vx[bp][:, q, HG * g + j, :], probs[g % 2][:, j, q, :],
                                                            start=q == 0, stop=q == QT - 1, tile_position=(0, ROWS * j))
                            last.then_inc(s["pv_ps"], 1)
                        step_b(i, par, u)

                run(pe, iteration)
                pe.wait_ge(s["tsum_r"], B + 1)
                nc.tensor.matmul(misc("VAR", "", 0)[:, 0:NE], ones_b[:, :], taken_sum[:, :], start=True, stop=True).then_inc(s["cnt_ps"], 1)

            @block.vector
            def _(dve):
                dve.wait_ge(s["c_in"], 16)
                nc.vector.tensor_copy(ident_b[:, :], con("ident"))
                nc.vector.tensor_copy(tri_b[:, :], con("tri"))
                nc.vector.memset(ones_b[:, :], 1.0)
                nc.vector.memset(taken_sum[:, :], 0.0)
                nc.vector.tensor_copy(idrun[:, :], con("ids")).then_inc(s["tsum_r"], 1)
                dve.wait_ge(s["w_in"], 16 * 5)
                nc.vector.memset(ones_f[:, :], 1.0).then_inc(s["ones_r"], 1)
                for t in range(NT):
                    if t % 8 == 0:
                        dve.wait_ge(s["x_in"], 64)
                    last = nc.vector.bn_stats(st1[:, t, :], xs[:, t, :])
                c = Chain(dve, s["ln1c"], 18, 0)
                c(last)
                for t in range(NT):
                    last = nc.vector.bn_aggr(mv1[:, t, :], st1[:, t, :])
                c(last)
                c(nc.vector.tensor_scalar(ve1[:, :], mv1[:, :, 1], EPS, None, ALU.add))
                c(nc.vector.tensor_scalar(t1[:, :].bitcast(I32), ve1[:, :].bitcast(I32), 1, None, ALU.logical_shift_right))
                c(nc.vector.tensor_scalar(y1[:, 0:NT].bitcast(I32), t1[:, :].bitcast(I32), -1.0, MAGIC, ALU.mult, ALU.add))
                for _ in range(3):
                    c(nc.vector.tensor_tensor(t1[:, :], y1[:, 0:NT], y1[:, 0:NT], ALU.mult))
                    c(nc.vector.tensor_tensor(t1[:, :], t1[:, :], ve1[:, :], ALU.mult))
                    c(nc.vector.tensor_scalar(t1[:, :], t1[:, :], -0.5, 1.5, ALU.mult, ALU.add))
                    c(nc.vector.tensor_tensor(y1[:, 0:NT], y1[:, 0:NT], t1[:, :], ALU.mult))
                c(nc.vector.tensor_tensor(t1[:, :], mv1[:, :, 0], y1[:, 0:NT], ALU.mult))
                c.done()
                nc.vector.tensor_scalar(nmr1[:, 0:NT], t1[:, :], -1.0, None, ALU.mult).then_inc(s["ln1"], 1)
                dve.wait_ge(s["set_ps"], 3)
                nc.vector.tensor_copy(wqT[:, :], ps_s1[0][:, 0, 0:E])
                nc.vector.tensor_copy(wkT[:, :], ps_s1[0][:, 0, E:])
                nc.vector.tensor_copy(wvT[:, :], ps_s1[0][:, 1, 0:E])
                nc.vector.tensor_copy(woT[:, :], ps_s1[0][:, 1, E:])
                nc.vector.tensor_copy(records[:, :, REC_B1:REC_B2], ps_pv[:, 0:(NE + 1) * FC].rearrange("p (e f) -> p e f", f=FC))
                nc.vector.tensor_copy(records[:, 0:NE, REC_B2:], ps[:, 5:7, :].rearrange("p a (e h) -> p (a e) h", h=E))
                nc.vector.tensor_copy(records[:, NE, REC_B2:], ps[:, 7, 0:E]).then_inc(s["set_r"], 1)

                def normalise(b, g):
                    dve.wait_ge(s["ott_ps"], G * b + g + 1)
                    sums = mi[f"OTT{g}"][:, 0:S].rearrange("p (q j r) -> p q j r", q=QT, r=ROWS)
                    nc.vector.reciprocal(rden[:, g, :, :].unsqueeze(3), sums[:, :, :, D:D + 1]).then_inc(s["rd_r"], 1)
                    dve.wait_ge(s["rd_r"], G * b + g + 1)
                    if g == 0:
                        wait(dve, s["ont_ps"], b)
                    nc.vector.tensor_tensor(on[:, :, HG * D * g:HG * D * (g + 1)].rearrange("p q (j d) -> p q j d", d=D), sums[:, :, :, 0:D],
                                            rden[:, g, :, :].unsqueeze(3).to_broadcast([P, QT, HG, D]), ALU.mult).then_inc(s["on_r"], 1)

                def residual(b):
                    dve.wait_ge(s["wo_ps"], b + 1)
                    wait(dve, s["x2keep"], b)
                    nc.vector.tensor_tensor(x2[:, :, :], mi["WO"][:, 0:QT * E].rearrange("p (q e) -> p q e", q=QT), xs[:, bass.ds(QT * b, QT), :], ALU.add).then_inc(s["x2_r"], 1)

                def statistics(b, par):
                    dve.wait_ge(s["x2_r"], b + 1)
                    c = Chain(dve, s["x2c"], 4, b, s["passed"])
                    for q in range(QT):
                        last = nc.vector.bn_stats(st2[:, q, :], x2[:, q, :])
                    c(last)
                    for q in range(QT):
                        last = nc.vector.bn_aggr(mv2[:, q, :], st2[:, q, :])
                    c(last)
                    c(nc.vector.tensor_scalar(ve2[:, :], mv2[:, :, 1], EPS, None, ALU.add))
                    c(nc.vector.tensor_scalar(t2[:, :].bitcast(I32), ve2[:, :].bitcast(I32), 1, None, ALU.logical_shift_right))
                    nc.vector.tensor_scalar(y2[:, :].bitcast(I32), t2[:, :].bitcast(I32), -1.0, MAGIC, ALU.mult, ALU.add).then_inc(s["y0_r"], 1)
                    wait(dve, s["scat"], 16 * QT * TOPK * (b - 1))
                    nc.vector.tensor_copy(xrow[par][:, :, :, E:].bitcast(I32).rearrange("p q k o -> p (q k) o"), idrun[:, :].unsqueeze(2)).then_inc(s["id_r"], 1)
                    nc.vector.tensor_scalar(idrun[:, :], idrun[:, :], float(TOPK * S), None, ALU.add).then_inc(s["idc"], 1)
                    dve.wait_ge(s["idc"], b + 1)

                def route(b):
                    dve.wait_ge(s["rt_ps"], b + 1)
                    wait(dve, s["keep_r"], b)
                    nc.vector.tensor_copy(lg[:, :, :], mi["RT"][:, 0:QT * NE].rearrange("p (q e) -> p q e", q=QT)).then_inc(s["lg_r"], 1)
                    wait_apart(dve, s["passed"], (s["lg_r"], b + 1))
                    for q in range(QT):
                        last = nc.vector.max(v8[:, q, :], lg[:, q, :])
                    last.then_inc(s["v8_r"], 1)
                    wait_apart(dve, s["passed"], (s["v8_r"], b + 1))
                    c = Chain(dve, s["rtc"], 3, b)
                    for q in range(QT):
                        last = nc.vector.max_index(i8[:, q, :], v8[:, q, :], lg[:, q, :])
                    c(last)
                    c(nc.vector.tensor_copy(idxf[:, :, :], i8[:, :, 0:TOPK]))
                    n = QT * TOPK
                    c(nc.vector.tensor_tensor(onehot[:, :, :, :].rearrange("p q k e -> p (q k) e"), con("iota8").unsqueeze(1).to_broadcast([P, n, NE]),
                                              idxf[:, :, :].rearrange("p q k -> p (q k)").unsqueeze(2).to_broadcast([P, n, NE]), ALU.is_equal))
                    nc.vector.tensor_tensor(taken[:, :, :], onehot[:, :, 0, :], onehot[:, :, 1, :], ALU.add).then_inc(s["taken_r"], 1)

                def places(b, par):
                    dve.wait_ge(s["pos_ps"], b + 1)
                    nc.vector.tensor_tensor(place[:, :, :], mi["POS"][:, 0:QT * NE].rearrange("p (q e) -> p q e", q=QT),
                                            con("region").unsqueeze(1).to_broadcast([P, QT, NE]), ALU.add).then_inc(s["pos_r"], 1)
                    dve.wait_ge(s["pos_r"], b + 1)
                    c = Chain(dve, s["posc"], 3, b)
                    c(nc.vector.tensor_tensor(placed[:, :, :, :], onehot[:, :, :, :], place[:, :, :].unsqueeze(2).to_broadcast([P, QT, TOPK, NE]), ALU.mult))
                    c(nc.vector.tensor_reduce(slotf[:, :], placed[:, :, :, :].rearrange("p q k e -> p (q k) e"), AX.X, ALU.add))
                    wait(dve, s["scat"], 16 * QT * TOPK * (b - 1))
                    nc.vector.tensor_copy(slot[par][:, :], slotf[:, :]).then_inc(s["slot_r"], 1)
                    c(nc.vector.tensor_tensor(taken_sum[:, :], taken_sum[:, :], taken[:, 0, :], ALU.add))
                    c.done()
                    nc.vector.tensor_tensor(taken_sum[:, :], taken_sum[:, :], taken[:, 1, :], ALU.add).then_inc(s["tsum_r"], 1)

                def iteration(i, par):
                    for u in range(UNITS):
                        if has(i, 0):
                            if u == 0:
                                wait(dve, s["m_r"], i)
                            for q in range(QT):
                                dve.wait_ge(s["s1_ps"], QT * (UNITS * i + u) + q + 1)
                                nc.vector.tensor_reduce(negmax[:, q, 2 * u:2 * u + 2], ps_s1[q][:, :, :], AX.X, ALU.max, negate=True).then_inc(s["max_r"], 1)
                        if u == 1 and has(i, -1):
                            dve.wait_ge(s["var_hi_r"], i + 2)
                            nc.vector.tensor_tensor(var_lo[:, :, :], mi["VAR"][0:H, :].rearrange("p (a t) -> p a t", a=2), var_hi[:, :, :], ALU.subtract).then_inc(s["var_lo_r"], 1)
                        if u == 1 and has(i, 2):
                            normalise(i - 2, 1)
                        if u == 2 and has(i, 2):
                            normalise(i - 2, 2)
                        if u == 3 and has(i, 3):
                            route(i - 3)
                        if u == 4 and has(i, 2):
                            normalise(i - 2, 3)
                        if u == 5 and has(i, 3):
                            places(i - 3, 1 - par)
                    if has(i, 0):
                        wait(dve, s["mt_ps"], i)
                        dve.wait_ge(s["max_r"], (i + 1) * UNITS * QT)
                        c = Chain(dve, s["mc"], 1, i)
                        neg = negmax[:, :, :].rearrange("p q (g j) -> p q g j", g=G)
                        c(nc.vector.tensor_copy(m_parts[:, :, :, 0, :], neg))
                        nc.vector.tensor_tensor(m_parts[:, :, :, 1, :], neg, m_parts[:, :, :, 0, :], ALU.subtract).then_inc(s["m_r"], 1)
                    if has(i, 2):
                        residual(i - 2)
                    if has(i, 1):
                        normalise(i - 1, 0)
                    if has(i, -2):
                        dve.wait_ge(s["sq_r"], i + 3)
                        nc.vector.tensor_copy(qk_hi2, qk_hi)
                        nc.vector.tensor_tensor(qk_lo, mi["QK"].rearrange("p (a t) -> p a t", a=2), qk_hi, ALU.subtract).then_inc(s["qk_lo_r"], 1)
                    if has(i, 2):
                        statistics(i - 2, par)

                run(dve, iteration)

        phase1.close()
        experts_phase(nc, ctx, sb, sem, locals())


def experts_phase(nc, ctx, sb, sem, v):
    xs, records, x2nT_all, logits, top8 = (v[n] for n in ("xs", "records", "x2nT_all", "logits", "top8"))
    starts, experts, xrows, orows, out = (v[n] for n in ("starts", "experts", "xrows", "orows", "out"))
    con, ps, pad_row = (v[n] for n in ("con", "ps", "pad_row"))
    passed, pads_out, cnt_ps = (v["s"][n] for n in ("passed", "pads_out", "cnt_ps"))
    ident = con("ident")
    cnt = sb("cnt", [P, NE])
    full = sb("full", [P, NE, NS])
    ntile, tbase, total = sb("ntile", [P, NE]), sb("tbase", [P, NE]), sb("total", [P, 1])
    low = sb("low", [P, NE, NE])
    ge = sb("ge", [P, TILES, NE])
    gt_ = sb("gt_", [P, TILES, NE])
    ex, tb, stf, dead = (sb(n, [P, TILES]) for n in ("ex", "tb", "stf", "dead"))
    pad_end, padf, padi = sb("pad_end", [P, NE]), sb("padf", [P, TQ, NE]), sb("padi", [P, TQ * NE], I32)
    rec = [sb(f"rec{i}", [P, REC]) for i in range(XT)]
    xg = [sb(f"xg{i}", [P, TQ, XW]) for i in range(XB)]
    xT = [sb(f"xT{i}", [P, 2, TT], BF16) for i in range(XT)]
    hid = [sb(f"hid{i}", [P, FC, TT]) for i in range(2)]
    yb = [sb(f"yb{i}", [P, TQ, E]) for i in range(XB)]
    ysh = sb("ysh", [P, TQ, E])
    dl = sb("dl", [P, NT, NE + 1])
    el = sb("el", [P, NT, NE + 1])
    esum, wt = sb("esum", [P, NT]), sb("wt", [P, 2, NT])
    CH = 4
    og = [sb(f"og{i}", [P, CH, TOPK, E]) for i in range(2)]
    ob = [sb(f"ob{i}", [P, CH, E]) for i in range(2)]
    ps_h = [ps[:, 2 * i:2 * i + 2, :].rearrange("p b (f t) -> p (b f) t", f=FC // 2) for i in range(2)]
    ps_t = [ps[:, 4 + i, :] for i in range(2)]
    ps_y = [ps[:, 6 + i, 0:TQ * E].rearrange("p (q e) -> p q e", q=TQ) for i in range(2)]
    list_r = sem("f_list_r")
    s = {n: sem("f_" + n) for n in "xt_ps listc pad_i_r rec_r xhi_r xlo_r h_ps h_r y_ps y_r ysh_r wt_d wt_e wtc o_c o_r".split()}
    s_in, s_out = ([sem(f"f_{n}{j}") for j in range(XB)] for n in ("in", "out"))
    s_og, s_fin = ([sem(f"f_{n}{j}") for j in range(2)] for n in ("og", "fin"))
    NCH = NT // CH
    ROUNDS = TILES // XB

    with nc.Block() as block:
        @block.sync
        def _(sp):
            def fetch(r, j):
                wait_apart(sp, passed, (s_out[j], 16 * TQ * r))
                row = sp.value_load(starts[0:1, bass.ds(r * XB + j, 1)], min_val=0, max_val=XROWS - TT)
                sp.dma_start(xg[j][:, :, :], xrows[bass.ds(row, TT), :].rearrange("(q p) w -> p q w", p=P)).then_inc(s_in[j], 16)

            sp.wait_ge(list_r, 1)
            sp.wait_ge(pads_out, 16 * NE * TQ)
            for j in range(XB):
                fetch(0, j)
            with sp.Fori(1, ROUNDS) as r:
                for j in range(XB):
                    fetch(r, j)
            for j in range(XB):
                sp.wait_ge(s_out[j], 16 * TQ * ROUNDS)
            ov = orows.rearrange("(t p k) e -> p t k e", p=P, k=TOPK)
            outv = out.rearrange("b (q p) e -> p (b q) e", p=P)

            def store(n):
                sp.wait_ge(s["o_r"], n + 1)
                sp.dma_start(outv[:, CH * n:CH * (n + 1), :], ob[n % 2][:, :, :]).then_inc(s_fin[n % 2], 16)

            for n in range(NCH):
                if n >= 2:
                    store(n - 2)
                sp.dma_start(og[n % 2][:, :, :, :], ov[:, CH * n:CH * (n + 1), :, :]).then_inc(s_og[n % 2], 16)
            store(NCH - 2)
            store(NCH - 1)
            for n in range(2):
                sp.wait_ge(s_fin[n], 16 * NCH // 2)

        @block.tensor
        def _(pe):
            def turn(r, j):
                t = r * XB + j
                pe.wait_ge(s_in[j], 16 * (r + 1))
                wait(pe, s["xlo_r"], t + NS - 1)
                for q in range(TQ):
                    last = nc.tensor.transpose(ps_t[j % 2][:, q * P:(q + 1) * P], xg[j][:, q, 0:E], ident)
                last.then_inc(s["xt_ps"], 1)

            def up(n, m, w):
                pe.wait_ge(s["xlo_r"], n + 1)
                wait(pe, s["h_r"], n - 1)
                high, low = w[:, 0:REC_L].bitcast(BF16), w[:, REC_L:REC_W2].bitcast(BF16)
                for f in range(FC):
                    at = slice(f * P, (f + 1) * P)
                    nc.tensor.matmul(ps_h[m % 2][:, f, :], high[:, at], xT[m][:, 0, :], start=True, stop=False)
                    nc.tensor.matmul(ps_h[m % 2][:, f, :], high[:, at], xT[m][:, 1, :], start=False, stop=False)
                    last = nc.tensor.matmul(ps_h[m % 2][:, f, :], low[:, at], xT[m][:, 0, :], start=False, stop=True)
                last.then_inc(s["h_ps"], 1)

            def down(n, m, w):
                pe.wait_ge(s["h_r"], n + 1)
                wait(pe, s["y_r"], n - 1)
                for q in range(TQ):
                    for f in range(FC):
                        last = nc.tensor.matmul(ps_y[m % 2][:, q, :], hid[m % 2][:, f, q * P:(q + 1) * P],
                                                w[:, REC_W2 + f * E:REC_W2 + (f + 1) * E], start=f == 0, stop=f == FC - 1)
                last.then_inc(s["y_ps"], 1)

            shared = records[:, SHARED, :]
            up(0, 0, shared)
            up(1, 1, shared)

            def shared_step(n, m):
                up(n + 1, (m + 1) % XT, shared)
                down(n - 1, (m - 1) % XT, shared)

            for n in range(1, XT + 1):
                shared_step(n, n % XT)
            with pe.Fori(XT + 1, NS - 3, XT) as n:
                for j in range(XT):
                    shared_step(n + j, (j + 1) % XT)
            shared_step(NS - 3, (NS - 3) % XT)
            turn(0, 0)
            shared_step(NS - 2, (NS - 2) % XT)
            turn(0, 1)
            up(NS, 0, rec[0])
            down(NS - 2, (NS - 2) % XT, shared)

            def step(r, j):
                t = r * XB + j
                static = isinstance(r, int)
                if not static or t + 2 < TILES:
                    turn(r + (j + 2) // XB, (j + 2) % XB)
                if not static or t + 1 < TILES:
                    up(t + 1 + NS, (j + 1) % XT, rec[(j + 1) % XT])
                down(t - 1 + NS, (j - 1) % XT, shared if static and t == 0 else rec[(j - 1) % XT])

            for j in range(XB):
                step(0, j)
            with pe.Fori(1, ROUNDS - 1) as r:
                for j in range(XB):
                    step(r, j)
            for j in range(XB):
                step(ROUNDS - 1, j)
            down(TILES - 1 + NS, (TILES - 1) % XT, rec[(TILES - 1) % XT])

        @block.scalar
        def _(act):
            act.wait_ge(s["wt_d"], 1)
            nc.scalar.activation(el[:, :, :], dl[:, :, :], ACT.Exp).then_inc(s["wt_e"], 1)

            def silu(n, m, w):
                act.wait_ge(s["h_ps"], n + 1)
                wait(act, s["y_ps"], n - 1)
                for f in range(FC):
                    last = nc.scalar.activation(hid[m % 2][:, f, :], ps_h[m % 2][:, f, :], ACT.Silu, bias=w[:, REC_B1 + f:REC_B1 + f + 1])
                last.then_inc(s["h_r"], 1)

            for n in range(XT):
                silu(n, n, records[:, SHARED, :])
            with act.Fori(XT, NS, XT) as n:
                for j in range(XT):
                    silu(n + j, j, records[:, SHARED, :])
            with act.Fori(0, TILES, XT) as t:
                for j in range(XT):
                    silu(t + j + NS, j, rec[j])

        @block.vector
        def _(dve):
            def parts(n, m, src):
                wait(dve, s["h_ps"], n - XT + 1)
                nc.vector.tensor_copy(xT[m][:, 0, :], src).then_inc(s["xhi_r"], 1)
                dve.wait_ge(s["xhi_r"], n + 1)
                nc.vector.tensor_tensor(xT[m][:, 1, :], src, xT[m][:, 0, :], ALU.subtract).then_inc(s["xlo_r"], 1)

            def shared_parts(n, m):
                parts(n, m, x2nT_all[:, bass.ds(n * TT, TT)])

            def shared_out(n, par):
                dve.wait_ge(s["y_ps"], n + 1)
                wait(dve, s["ysh_r"], 2 * n)
                nc.vector.tensor_tensor(ysh[:, :, :], ps_y[par], records[:, SHARED:SHARED + 1, REC_B2:].to_broadcast([P, TQ, E]), ALU.add).then_inc(s["y_r"], 1)
                dve.wait_ge(s["y_r"], n + 1)
                at = bass.ds(n * TQ, TQ)
                nc.vector.scalar_tensor_tensor(xs[:, at, :], ysh[:, :, :], SHARED_SCALE, xs[:, at, :], ALU.mult, ALU.add).then_inc(s["ysh_r"], 2)

            for n in range(3):
                shared_parts(n, n)
            nc.vector.tensor_tensor(dl[:, :, 0:NE], logits[:, 0:NT, :], top8[:, 0:NT, 0:1].to_broadcast([P, NT, NE]), ALU.subtract)
            nc.vector.tensor_tensor(dl[:, :, NE:], top8[:, 0:NT, 1:2], top8[:, 0:NT, 0:1], ALU.subtract).then_inc(s["wt_d"], 1)
            dve.wait_ge(cnt_ps, 1)
            c = Chain(dve, s["listc"], 19, 0)
            c(nc.vector.tensor_copy(cnt[:, :], v["mi"]["VAR"][:, 0:NE]))
            c(nc.vector.tensor_tensor(pad_end[:, :], cnt[:, :], con("region"), ALU.add))
            c(nc.vector.tensor_tensor(padf[:, :, :], pad_end[:, :].unsqueeze(1).to_broadcast([P, TQ, NE]), con("part").unsqueeze(2).to_broadcast([P, TQ, NE]), ALU.add))
            nc.vector.tensor_copy(padi[:, :], padf[:, :, :].rearrange("p q e -> p (q e)")).then_inc(s["pad_i_r"], 1)
            c(nc.vector.tensor_tensor(full[:, :, :], cnt[:, :].unsqueeze(2).to_broadcast([P, NE, NS]), con("steps").unsqueeze(1).to_broadcast([P, NE, NS]), ALU.is_gt))
            c(nc.vector.tensor_reduce(ntile[:, :], full[:, :, :], AX.X, ALU.add))
            c(nc.vector.tensor_tensor(low[:, :, :], con("lower").rearrange("p (a b) -> p a b", b=NE), ntile[:, :].unsqueeze(1).to_broadcast([P, NE, NE]), ALU.mult))
            c(nc.vector.tensor_reduce(tbase[:, :], low[:, :, :], AX.X, ALU.add))
            c(nc.vector.tensor_tensor(total[:, :], tbase[:, NE - 1:NE], ntile[:, NE - 1:NE], ALU.add))
            c(nc.vector.tensor_tensor(ge[:, :, :], con("tiles").unsqueeze(2).to_broadcast([P, TILES, NE]), tbase[:, :].unsqueeze(1).to_broadcast([P, TILES, NE]), ALU.is_ge))
            c(nc.vector.tensor_reduce(ex[:, :], ge[:, :, :], AX.X, ALU.add))
            c(nc.vector.tensor_tensor(gt_[:, :, :], ge[:, :, :], tbase[:, :].unsqueeze(1).to_broadcast([P, TILES, NE]), ALU.mult))
            c(nc.vector.tensor_reduce(tb[:, :], gt_[:, :, :], AX.X, ALU.max))
            c(nc.vector.tensor_scalar(ex[:, :], ex[:, :], -1.0, None, ALU.add))
            c(nc.vector.tensor_tensor(tb[:, :], con("tiles"), tb[:, :], ALU.subtract))
            c(nc.vector.tensor_scalar(tb[:, :], tb[:, :], float(TT), None, ALU.mult))
            c(nc.vector.scalar_tensor_tensor(stf[:, :], ex[:, :], float(REGION), tb[:, :], ALU.mult, ALU.add))
            c(nc.vector.tensor_scalar(dead[:, :], con("tiles"), total[:, 0:1], None, ALU.is_ge))
            c(nc.vector.scalar_tensor_tensor(tb[:, :], stf[:, :], -float(DUMMY), dead[:, :], ALU.add, ALU.mult))
            c(nc.vector.tensor_tensor(stf[:, :], stf[:, :], tb[:, :], ALU.subtract))
            c.done()
            nc.vector.tensor_copy(starts[:, 0:TILES], stf[:, :])
            nc.vector.tensor_copy(experts[:, 0:TILES], ex[:, :]).then_inc(list_r, 1)

            def shared_step(n, m):
                shared_parts(n + 2, (m + 2) % XT)
                shared_out(n - 1, (m - 1) % 2)

            for n in range(1, XT + 1):
                shared_step(n, n % XT)
            with dve.Fori(XT + 1, NS - 3, XT) as n:
                for j in range(XT):
                    shared_step(n + j, (j + 1) % XT)
            shared_step(NS - 3, (NS - 3) % XT)

            def routed_parts(t, j):
                e = dve.value_load(experts[0:1, bass.ds(t, 1)], min_val=0, max_val=NE - 1)
                wait(dve, s["y_r"], t + NS - XT + 1)
                nc.vector.tensor_copy(rec[j % XT][:, :], records[:, bass.ds(e, 1), :].rearrange("p o w -> p (o w)")).then_inc(s["rec_r"], 1)
                dve.wait_ge(s["xt_ps"], t + 1)
                parts(t + NS, j % XT, ps_t[j % 2][:, 0:TT])

            def bias(r, j):
                t = r * XB + j
                dve.wait_ge(s["y_ps"], t + NS + 1)
                wait(dve, s_out[j], 16 * TQ * r)
                nc.vector.tensor_tensor(yb[j][:, :, :], ps_y[j % 2], rec[j % XT][:, REC_B2:].unsqueeze(1).to_broadcast([P, TQ, E]), ALU.add).then_inc(s["y_r"], 1)

            dve.wait_ge(list_r, 1)
            for n in range(NS - 2, NS):
                routed_parts(n - (NS - 2), n - (NS - 2))
                shared_out(n - 1, (n - 1) % 2)
            dve.wait_ge(s["wt_e"], 1)
            c = Chain(dve, s["wtc"], 5, 0)
            c(nc.vector.tensor_reduce(esum[:, :], el[:, :, 0:NE], AX.X, ALU.add))
            c(nc.vector.scalar_tensor_tensor(esum[:, :], esum[:, :], EPS_W, el[:, :, NE], ALU.mult, ALU.add))
            c(nc.vector.tensor_scalar(esum[:, :], esum[:, :], 1.0, None, ALU.add))
            c(nc.vector.reciprocal(wt[:, 0, :], esum[:, :]))
            c(nc.vector.tensor_tensor(wt[:, 1, :], wt[:, 0, :], el[:, :, NE], ALU.mult))
            c.done()

            def step(r, j):
                t = r * XB + j
                static = isinstance(r, int)
                if not static or t + 2 < TILES:
                    routed_parts(t + 2, (j + 2) % XB)
                if static and t == 0:
                    shared_out(NS - 1, (NS - 1) % 2)
                else:
                    bias(r + (j - 1) // XB, (j - 1) % XB)

            for j in range(XB):
                step(0, j)
            for j in range(XB):
                step(1, j)
            with dve.Fori(2, ROUNDS - 1) as r:
                for j in range(XB):
                    step(r, j)
            for j in range(XB):
                step(ROUNDS - 1, j)
            bias(ROUNDS - 1, XB - 1)

            for n in range(NCH):
                dve.wait_ge(s_og[n % 2], 16 * (n // 2 + 1))
                if n >= 2:
                    dve.wait_ge(s_fin[n % 2], 16 * (n // 2))
                o, g = ob[n % 2], og[n % 2]
                c = Chain(dve, s["o_c"], 1, n)
                for k in range(TOPK):
                    for q in range(CH):
                        base = o[:, q, :] if k else xs[:, CH * n + q, :]
                        last = nc.vector.scalar_tensor_tensor(o[:, q, :], g[:, q, k, :], wt[:, k, CH * n + q:CH * n + q + 1], base, ALU.mult, ALU.add)
                    if k == 0:
                        c(last)
                last.then_inc(s["o_r"], 1)

        @block.gpsimd
        def _(pool):
            pool.wait_ge(s["pad_i_r"], 1)
            for e in range(TQ * NE):
                nc.gpsimd.indirect_dma_start(out=xrows, out_offset=bass.IndirectOffsetOnAxis(ap=padi[:, e:e + 1], axis=0),
                                             in_=pad_row[:, :], in_offset=None,
                                             bounds_check=XROWS - 1, oob_is_err=False).then_inc(pads_out, 16)

            def send(r, j):
                wait_apart(pool, passed, (s["y_r"], r * XB + j + 1 + NS))
                for q in range(TQ):
                    nc.gpsimd.indirect_dma_start(out=orows, out_offset=bass.IndirectOffsetOnAxis(ap=xg[j][:, q, E:XW].bitcast(I32), axis=0),
                                                 in_=yb[j][:, q, :], in_offset=None, bounds_check=OROWS - 1, oob_is_err=False).then_inc(s_out[j], 16)

            with pool.Fori(0, ROUNDS) as r:
                for j in range(XB):
                    send(r, j)


_INS = ["L0_attn_x", "L0_attn_Wq", "L0_attn_Wk", "L0_attn_Wv", "L0_attn_Wo", "L0_ffn_Wg", "L0_ffn_W1", "L0_ffn_b1",
        "L0_ffn_W2", "L0_ffn_b2", "L0_ffn_Ws1", "L0_ffn_bs1", "L0_ffn_Ws2", "L0_ffn_bs2"]


def kernel(**inputs):
    import concourse.bacc as _bacc
    from concourse.bass_utils import run_bass_kernel_spmd as _run

    nc = _bacc.Bacc("TRN2", target_bir_lowering=False, num_devices=1)
    arrays, args = {}, []
    for name in _INS:
        a = np.ascontiguousarray(inputs[name])
        arrays[name] = a
        args.append(nc.dram_tensor(name, a.shape, mybir.dt.from_np(a.dtype), kind="ExternalInput").ap())
    arrays["consts"] = constants()
    args.append(nc.dram_tensor("consts", [P, NCONST], F32, kind="ExternalInput").ap())
    args.append(nc.dram_tensor("result", [B, S, E], F32, kind="ExternalOutput").ap())
    block_kernel(nc, *args)
    r = _run(nc, [arrays], core_ids=[0])
    return r.results[0]["result"]
```

```python
from contextlib import ExitStack

import numpy as np
import concourse.bass as bass
from concourse import mybir

F32 = mybir.dt.float32
BF16 = mybir.dt.bfloat16
I32 = mybir.dt.int32
U32 = mybir.dt.uint32
ALU = mybir.AluOpType
ACT = mybir.ActivationFunctionType
AX = mybir.AxisListType

P = 128
B, S, E = 16, 256, 128
H = 16
D = E // H
QT = S // P
NT = B * QT
G = 4
HG = H // G
UNITS = H // 2
ROWS = 32
NE, F = 8, 512
FC = F // P
SHARED = NE
TOPK = 2
EPS = 1e-5
EPS_W = 1e-9
SHARED_SCALE = 0.1
TT = 256
TQ = TT // P
NS = B * S // TT
REGION = B * S + TT
DUMMY = NE * REGION
XROWS = DUMMY + TT
XW = E + 1
ROUTED_TILES = (TOPK * B * S + NE * (TT - 1)) // TT
XB = 8
TILES = -(-ROUTED_TILES // XB) * XB
XT = 4
OROWS = TOPK * B * S
REC_L, REC_W2, REC_B1, REC_B2, REC = F // 2, F, 2 * F, 2 * F + FC, 2 * F + FC + E
SKIP = 1 << 20
MAGIC = float(0x5F3759DF)

_COLS = [("ident", P), ("centre", P), ("centre_q", P), ("ind_q", H), ("ind_k", H), ("tri", P),
         ("iota8", NE), ("region", NE), ("ids", QT * TOPK), ("steps", NS), ("lower", NE * NE), ("tiles", TILES),
         ("part", TQ)]
COL = {}
for _n, _w in _COLS:
    COL[_n] = (sum(w for _, w in _COLS[:len(COL)]), _w)
NCONST = sum(w for _, w in _COLS)


def constants():
    c = np.zeros((P, NCONST), np.float32)

    def put(name, a):
        o, w = COL[name]
        c[:, o:o + w] = a

    same = (np.arange(P)[:, None] // D == np.arange(P)[None, :] // D).astype(np.float32)
    centre = np.eye(P, dtype=np.float32) - same / D
    ind = (np.arange(P)[:, None] // D == np.arange(H)[None, :]).astype(np.float32)
    put("ident", np.eye(P))
    put("centre", centre)
    put("centre_q", centre / D)
    put("ind_q", ind * (D / (D - 1)))
    put("ind_k", ind / (D - 1))
    put("tri", np.arange(P)[:, None] < np.arange(P)[None, :])
    put("iota8", np.arange(NE)[None, :])
    put("region", np.arange(NE)[None, :] * REGION)
    q, k = np.arange(QT)[None, :, None], np.arange(TOPK)[None, None, :]
    put("ids", (TOPK * (q * P + np.arange(P)[:, None, None]) + k).reshape(P, QT * TOPK))
    put("steps", np.arange(NS)[None, :] * TT)
    put("lower", (np.arange(NE)[None, :] < np.arange(NE)[:, None]).reshape(1, -1))
    put("tiles", np.arange(TILES)[None, :])
    put("part", np.arange(P)[:, None] + P * np.arange(TQ)[None, :])
    return c


def wait(eng, sem, value):
    if isinstance(value, int) and value <= 0:
        return
    eng.wait_ge(sem, value)


def wait_apart(eng, passed, *waits):
    for sem, value in waits:
        wait(eng, sem, value)
        eng.sem_inc(passed, 1)


class Chain:

    def __init__(self, eng, sem, steps, rnd, passed=None):
        self.eng, self.sem, self.steps, self.base, self.n, self.passed = eng, sem, steps, steps * rnd, 0, passed

    def count(self, ins):
        self.n += 1
        assert self.n <= self.steps
        ins.then_inc(self.sem, 1)

    def ready(self):
        if self.passed is None:
            self.eng.wait_ge(self.sem, self.base + self.n)
        else:
            wait_apart(self.eng, self.passed, (self.sem, self.base + self.n))

    def __call__(self, ins):
        self.count(ins)
        self.ready()

    def done(self):
        assert self.n == self.steps, (self.n, self.steps)


def block_kernel(nc, x, Wq, Wk, Wv, Wo, Wg, W1, b1, W2, b2, Ws1, bs1, Ws2, bs2, consts, out):
    ctx = ExitStack()
    with ctx:
        def sb(name, shape, dt=F32):
            return ctx.enter_context(nc.sbuf_tensor(name, shape, dt))

        def sem(name):
            return ctx.enter_context(nc.semaphore(name))

        dq = [nc.dram_tensor(f"dq{i}", [H, ROWS, S], BF16, kind="Internal").ap() for i in range(2)]
        dk = [nc.dram_tensor(f"dk{i}", [H, ROWS, S], BF16, kind="Internal").ap() for i in range(2)]
        xrows = nc.dram_tensor("xrows", [XROWS, XW], F32, kind="Internal").ap()
        orows = nc.dram_tensor("orows", [OROWS, E], F32, kind="Internal").ap()

        xs = sb("xs", [P, NT + 2, E])
        cst = sb("cst", [P, NCONST])
        records = sb("records", [P, NE + 1, REC])
        w1f = sb("w1f", [P, NE + 1, F])
        x2nT_all = w1f[:, :, :].rearrange("p e f -> p (e f)")
        logits = sb("logits", [P, NT + 2, NE])
        top8 = sb("top8", [P, NT + 2, 8])
        pad_row = sb("pad_row", [P, TQ, XW])
        starts = sb("starts", [P, TILES + XB], I32)
        experts = sb("experts", [P, TILES + XB], I32)

        def con(name, rows=P):
            o, w = COL[name]
            return cst[0:rows, o:o + w]

        wraw = sb("wraw", [P, 4, E])
        wqT, wkT, wvT = sb("wqT", [P, E]), sb("wkT", [P, E]), sb("wvT", [P, E])
        woT = sb("woT", [P, E])
        wg = sb("wg", [P, NE])
        b1r = sb("b1r", [(NE + 1) * FC, P])
        b2r = sb("b2r", [1, (NE + 1) * E])
        ones_f = sb("ones_f", [1, P])
        ident_b, tri_b, ones_b = sb("ident_b", [P, P], BF16), sb("tri_b", [P, P], BF16), sb("ones_b", [P, P], BF16)
        fill = sb("fill", [P, 2, G, S], BF16)
        st1 = sb("st1", [P, NT, 6])
        mv1 = sb("mv1", [P, NT, 2])
        ve1, y1, t1 = sb("ve1", [P, NT]), sb("y1", [P, NT + 2]), sb("t1", [P, NT])
        nmr1 = sb("nmr1", [P, NT + 2])
        xn = sb("xn", [P, QT, E])
        xnT = [sb(f"xnT{i}", [P, S]) for i in range(2)]
        qk_parts = sb("qk_parts", [P, 4, S], BF16)
        qk_hi, qk_lo = qk_parts[:, 0:4:3, :], qk_parts[:, 1:3, :]
        qk_sq = sb("qk_sq", [P, 2, S])
        var_hi, var_lo = sb("var_hi", [H, 2, S], BF16), sb("var_lo", [H, 2, S], BF16)
        qa = [sb(f"qa{i}", [P, G, S], BF16) for i in range(2)]
        ka = [sb(f"ka{i}", [P, G, HG, S], BF16) for i in range(2)]
        vx = [sb(f"vx{i}", [P, QT, H, ROWS]) for i in range(2)]
        negmax = sb("negmax", [P, QT, H])
        m_parts = sb("m_parts", [P, QT, G, 2, HG], BF16)
        mT = sb("mT", [2 * HG, G, S], BF16)
        probs = [sb(f"probs{i}", [P, HG, QT, S]) for i in range(2)]
        oT = sb("oT", [P, G, S])
        rden = sb("rden", [P, G, QT, HG])
        on = sb("on", [P, QT, E])
        onT = sb("onT", [P, S])
        x2 = sb("x2", [P, QT, E])
        st2, mv2 = sb("st2", [P, QT, 6]), sb("mv2", [P, QT, 2])
        ve2, y2, t2, nmr2 = sb("ve2", [P, QT]), sb("y2", [P, QT]), sb("t2", [P, QT]), sb("nmr2", [P, QT])
        xrow = [sb(f"xrow{i}", [P, QT, TOPK, XW]) for i in range(2)]
        idrun = sb("idrun", [P, QT * TOPK])
        x2nT = sb("x2nT", [P, S])
        lg, v8 = sb("lg", [P, QT, NE]), sb("v8", [P, QT, 8])
        i8 = sb("i8", [P, QT, 8], U32)
        idxf = sb("idxf", [P, QT, TOPK])
        onehot = sb("onehot", [P, QT, TOPK, NE])
        taken = sb("taken", [P, QT, NE], BF16)
        taken_sum = sb("taken_sum", [P, NE], BF16)
        place = sb("place", [P, QT, NE])
        placed = sb("placed", [P, QT, TOPK, NE])
        slotf = sb("slotf", [P, QT * TOPK])
        slot = [sb(f"slot{i}", [P, QT * TOPK], I32) for i in range(2)]

        ps = ctx.enter_context(nc.psum_tensor("ps", [P, 8, 512], F32))
        ps_s1 = [ps[:, q, :].rearrange("p (a t) -> p a t", a=2) for q in range(QT)]
        ps_st = [ps[:, 2 + a, :] for a in range(2)]
        ps_pv = ps[:, 4, :]
        MISC = dict(OTT1=0, MT=1, VAR=2, OTT2=0, V=0, OTT3=2, T=0, X2T=1, QK=0, RT=1, ONT=2, WO=0, OTT0=1, POS=2)
        mi = {step: ps[:, 5 + bank, :] for step, bank in MISC.items()}

        names = """c_in w_in b_in w1_in w2_in fill_out set_ps set_r vx_init ka_zero fill_r init_r ln1 ln1c ones_r
            xn_r xnc xt_ps xnT_r qk_ps qk_hi_r sq_r qk_lo_r var_ps var_hi_r var_lo_r rows_out
            max_r m_r mc mt_ps mt_r mrow_in s1_ps st_ps exp_r pv_ps ot_r ott_ps rd_r on_r ont_ps onT_r v_ps v_r
            wo_ps x2_r x2c y0_r n2c xrow_r x2keep id_r idc x2t_ps x2nT_r xkeep rt_ps lg_r rtc v8_r keep_r taken_r pos_ps pos_r posc slot_r
            tsum_r scat cnt_ps pads_out split_r passed""".split()
        s = {n: sem("s_" + n) for n in names}
        s_ld = [sem(f"s_ld{half}") for half in range(2)]
        LOADS, ROWS_OUT, MROWS = 16 * (1 + HG), 16 * 8, 16 * 2

        CHUNKS = (0, 4), (4, NT)
        x_in = [sem(f"s_x_in{n}") for n in range(len(CHUNKS))]

        FIRST, LAST = -2, B + 4

        def has(i, lag):
            return 0 <= i - lag < B if isinstance(i, int) else True

        def pass2_at(i, u):
            return (i - 1, u - 2, 1) if u >= 2 else (i - 2, u + 6, 2)

        def pv_at(i, u):
            k = (u - 3) % UNITS
            b, lag = (i - 1, 1) if u >= 3 else (i - 2, 2)
            return b, (k // 2 if k % 2 else None), lag

        def run(eng, iteration, before=None):
            for i in range(FIRST, 6):
                if before and i in before:
                    before[i]()
                iteration(i, i % 2)
            with eng.Fori(6, B - 2, 2) as i:
                iteration(i, 0)
                iteration(i + 1, 1)
            for i in range(B - 2, LAST):
                if before and i in before:
                    before[i]()
                iteration(i, i % 2)

        shared_at = [(B + 1, u) for u in range(2, UNITS)] + [(B + 2, u) for u in (0, 1, 2, 4, 5)]

        def shared_here(i, u):
            return [shared_at.index((i, u))] if isinstance(i, int) and (i, u) in shared_at else []

        experts_programs = experts_phase(nc, sb, sem, locals())

        with nc.Block() as block:
            @block.sync
            def _(sp):
                sp.dma_start(cst[:, :], consts).then_inc(s["c_in"], 16)
                tokens = x.rearrange("b (q p) e -> p (b q) e", p=P)
                at = [slice(c[0], c[1]) for c in CHUNKS]
                sp.dma_start(xs[:, at[0], :], tokens[:, at[0], :]).then_inc(x_in[0], 16)
                for n, w in enumerate((Wq, Wk, Wv, Wo)):
                    sp.dma_start(wraw[:, n, :], w).then_inc(s["w_in"], 16)
                sp.dma_start(xs[:, at[1], :], tokens[:, at[1], :]).then_inc(x_in[1], 16)
                sp.dma_start(wg[:, :], Wg).then_inc(s["b_in"], 16)
                sp.dma_start(b1r[0:NE * FC, :], b1.rearrange("e (f p) -> (e f) p", p=P)).then_inc(s["b_in"], 16)
                sp.dma_start(b1r[NE * FC:, :], bs1.rearrange("(f p) -> f p", p=P)).then_inc(s["b_in"], 16)
                sp.dma_start(b2r[:, 0:NE * E], b2.rearrange("(o e) h -> o (e h)", o=1)).then_inc(s["b_in"], 16)
                sp.dma_start(b2r[:, NE * E:], bs2.rearrange("(o h) -> o h", o=1)).then_inc(s["b_in"], 16)
                sp.wait_ge(s["fill_r"], 3)
                for i in range(2):
                    sp.dma_start(dq[i].rearrange("(g j) r t -> (j r) g t", g=G), fill[:, 0, :, :]).then_inc(s["fill_out"], 16)
                    sp.dma_start(dk[i].rearrange("(g j) r t -> (j r) g t", g=G), fill[:, 0, :, :]).then_inc(s["fill_out"], 16)
                sp.wait_ge(s["fill_out"], 64)
                for i in range(2):
                    sp.dma_start(dk[i][:, 3 * D + 3:3 * D + 5, :], fill[0:2 * H, 1, 0, :]).then_inc(s["fill_out"], 16)
                sp.dma_start(xrows[DUMMY:, :].rearrange("(q p) w -> p q w", p=P), pad_row[:, :, :]).then_inc(s["fill_out"], 16)
                sp.wait_ge(s["fill_out"], 64 + 16 * 3)

                def load_w1():
                    sp.dma_start(w1f[:, 0:NE, :], W1.rearrange("e h f -> h e f")).then_inc(s["w1_in"], 16)
                    sp.dma_start(w1f[:, NE, :], Ws1).then_inc(s["w1_in"], 16)

                w2v = records[:, :, REC_W2:REC_B1].rearrange("p e (f h) -> p e f h", f=FC)

                def load_w2(e0, e1):
                    for e in range(e0, e1):
                        sp.dma_start(w2v[:, e, :, :], W2[e].rearrange("(f p) h -> p f h", p=P)).then_inc(s["w2_in"], 16)

                def load_last_w2():
                    sp.dma_start(w2v[:, NE, :, :], Ws2.rearrange("(f p) h -> p f h", p=P)).then_inc(s["w2_in"], 16)

                def load(b, par, half):
                    wait(sp, s["st_ps"], H * (b - 2) + 8 * half + 8)
                    at = slice(2 * half, 2 * half + 2)
                    sp.dma_start(qa[par][:, at, :], dq[par].rearrange("(g j) r t -> (j r) g t", g=G)[:, at, :]).then_inc(s_ld[half], 16)
                    if isinstance(b, int) and b == 0 and half == 0:
                        sp.wait_ge(s["ka_zero"], 1)
                    for j in range(HG):
                        sp.dma_start(ka[par][ROWS * j:ROWS * (j + 1), at, j, :], dk[par].rearrange("(g j) r t -> j r g t", g=G)[j][:, at, :]).then_inc(s_ld[half], 16)

                def iteration(i, par):
                    nxt = 1 - par
                    if has(i, -1):
                        b = i + 1
                        wait_apart(sp, s["passed"], *((s_ld[half], LOADS * (b - 1)) for half in range(2)))
                        sp.wait_ge(s["qk_lo_r"], b + 1)
                        for dram, part, at, again in ((dq, 0, 1, 0), (dk, 2, 0, 2)):
                            rows = dram[nxt][:, 0:3 * D, :].rearrange("h (d n) t -> h d n t", n=3)
                            sp.dma_start(rows[:, :, at:at + 2, :].rearrange("h d n t -> h d (n t)"),
                                         qk_parts[:, part:part + 2, :].rearrange("p n t -> p (n t)")).then_inc(s["rows_out"], 16)
                            sp.dma_start(rows[:, :, again, :], qk_hi[:, part // 2, :]).then_inc(s["rows_out"], 16)
                    if has(i, 1):
                        sp.wait_ge(s["mt_r"], i)
                        for c in range(2):
                            sp.dma_start(qa[nxt][3 * D + 3 + c::ROWS, :, :], mT[HG * c:HG * (c + 1), :, :]).then_inc(s["mrow_in"], 16)
                    if has(i, 0):
                        load(i, par, 1)
                    if has(i, -1):
                        sp.wait_ge(s["var_lo_r"], b + 1)
                        for side, dram, hi, lo in ((0, dq, 0, 2), (1, dk, 1, 0)):
                            rows = dram[nxt][:, 3 * D:3 * D + 3, :]
                            sp.dma_start(rows[:, hi:hi + 2, :], var_hi[:, side, :].unsqueeze(1).to_broadcast([H, 2, S])).then_inc(s["rows_out"], 16)
                            sp.dma_start(rows[:, lo, :], var_lo[:, side, :]).then_inc(s["rows_out"], 16)
                    if has(i, -1):
                        sp.wait_ge(s["rows_out"], ROWS_OUT * (i + 2))
                        load(i + 1, nxt, 0)

                run(sp, iteration, {0: load_w1, 2: lambda: load_w2(0, 2), 3: lambda: load_w2(2, 4), 4: lambda: load_w2(4, 6), 5: lambda: load_w2(6, NE), B - 2: load_last_w2})
                experts_programs["sync"](sp)

            @block.gpsimd
            def _(pool):
                nc.gpsimd.memset(fill[:, 0, :, :], 0.0).then_inc(s["fill_r"], 1)
                nc.gpsimd.memset(fill[:, 1, :, :], 1.0).then_inc(s["fill_r"], 1)
                nc.gpsimd.memset(pad_row[:, :, 0:E], 0.0)
                nc.gpsimd.memset(pad_row[:, :, E:].bitcast(I32), SKIP).then_inc(s["fill_r"], 1)

                def clear():
                    for i in range(2):
                        last = nc.gpsimd.memset(ka[i][:, :, :, :], 0.0)
                    last.then_inc(s["ka_zero"], 1)
                    for i in range(2):
                        nc.gpsimd.memset(vx[i][:, :, :, :], 0.0).then_inc(s["init_r"], 1)
                    pool.wait_ge(s["init_r"], 2)
                    for i in range(2):
                        last = nc.gpsimd.memset(vx[i][:, :, :, D:D + 1], 1.0)
                    last.then_inc(s["vx_init"], 1)

                def layer_norm_in(b, par):
                    if isinstance(b, int) and b in (0, 2):
                        pool.wait_ge(s["ln1"], {0: 1, 2: 2}[b])
                    wait(pool, s["xt_ps"], b)
                    at = bass.ds(QT * b, QT)
                    c = Chain(pool, s["xnc"], 1, b)
                    c(nc.gpsimd.tensor_tensor(xn[:, :, :], xs[:, at, :], y1[:, at].unsqueeze(2).to_broadcast([P, QT, E]), ALU.mult))
                    nc.gpsimd.tensor_tensor(xn[:, :, :], xn[:, :, :], nmr1[:, at].unsqueeze(2).to_broadcast([P, QT, E]), ALU.add).then_inc(s["xn_r"], 1)

                def rows_of_tokens(b, par):
                    pool.wait_ge(s["y0_r"], b + 1)
                    c = Chain(pool, s["n2c"], 14, b, s["passed"])
                    for _ in range(3):
                        c(nc.gpsimd.tensor_tensor(t2[:, :], y2[:, :], y2[:, :], ALU.mult))
                        c(nc.gpsimd.tensor_tensor(t2[:, :], t2[:, :], ve2[:, :], ALU.mult))
                        c(nc.gpsimd.tensor_scalar(t2[:, :], t2[:, :], -0.5, 1.5, ALU.mult, ALU.add))
                        c(nc.gpsimd.tensor_tensor(y2[:, :], y2[:, :], t2[:, :], ALU.mult))
                    c(nc.gpsimd.tensor_tensor(t2[:, :], mv2[:, :, 0], y2[:, :], ALU.mult))
                    c(nc.gpsimd.tensor_scalar(nmr2[:, :], t2[:, :], -1.0, 0.0, ALU.mult, ALU.add))
                    c.done()
                    wait_apart(pool, s["passed"], (s["scat"], 16 * QT * TOPK * (b - 1)))
                    for q in range(QT):
                        last = nc.gpsimd.tensor_scalar(xrow[par][:, q, :, 0:E], x2[:, q, :].unsqueeze(1).to_broadcast([P, TOPK, E]),
                                                       y2[:, q:q + 1], nmr2[:, q:q + 1], ALU.mult, ALU.add)
                    last.then_inc(s["xrow_r"], 1)
                    nc.gpsimd.tensor_copy(xs[:, bass.ds(QT * b, QT), :], x2[:, :, :]).then_inc(s["x2keep"], 1)

                def keep_columns(b):
                    pool.wait_ge(s["x2nT_r"], b + 1)
                    if isinstance(b, int) and b == 0:
                        pool.wait_ge(s["split_r"], 2 * (NE + 1))
                    nc.gpsimd.tensor_copy(x2nT_all[:, bass.ds(S * b, S)], x2nT[:, :]).then_inc(s["xkeep"], 1)

                def scatter(b, par):
                    pool.wait_ge(s["v8_r"], b + 1)
                    nc.gpsimd.tensor_copy(logits[:, bass.ds(QT * b, QT), :], lg[:, :, :])
                    nc.gpsimd.tensor_copy(top8[:, bass.ds(QT * b, QT), :], v8[:, :, :]).then_inc(s["keep_r"], 1)
                    wait_apart(pool, s["passed"], (s["slot_r"], b + 1), (s["id_r"], b + 1), (s["xrow_r"], b + 1),
                               (s["scat"], 16 * QT * TOPK * b))
                    for q in range(QT):
                        for k in range(TOPK):
                            n = q * TOPK + k
                            nc.gpsimd.indirect_dma_start(out=xrows, out_offset=bass.IndirectOffsetOnAxis(ap=slot[par][:, n:n + 1], axis=0),
                                                         in_=xrow[par][:, q, k, :], in_offset=None,
                                                         bounds_check=XROWS - 1, oob_is_err=False).then_inc(s["scat"], 16)

                def split_w1(e):
                    c = Chain(pool, s["split_r"], 2, e)
                    high, low = records[:, e, 0:REC_L].bitcast(BF16), records[:, e, REC_L:REC_W2].bitcast(BF16)
                    c(nc.gpsimd.tensor_copy(high, w1f[:, e, :]))
                    c(nc.gpsimd.tensor_tensor(low, w1f[:, e, :], high, ALU.subtract))

                def iteration(i, par):
                    nxt = 1 - par
                    if has(i, -2):
                        layer_norm_in(i + 2, par)
                    if has(i, 3):
                        rows_of_tokens(i - 3, nxt)
                    if has(i, 4):
                        scatter(i - 4, par)
                    if has(i, 3):
                        keep_columns(i - 3)
                    if isinstance(i, int) and 0 <= i <= 2:
                        if i == 0:
                            pool.wait_ge(s["w1_in"], 32)
                        for e in range(3 * i, 3 * (i + 1)):
                            split_w1(e)

                run(pool, iteration, {0: clear})
                experts_programs["gpsimd"](pool)

            @block.scalar
            def _(act):
                act.wait_ge(s["set_ps"], 1)
                for n, w in enumerate((wqT, wkT, wvT, woT)):
                    last = nc.scalar.activation(w[:, :], ps[:, 0, n * E:(n + 1) * E], ACT.Copy)
                last.then_inc(s["set_r"], 1)

                def biases():
                    act.wait_ge(s["set_ps"], 2)
                    nc.scalar.activation(records[:, :, REC_B1:REC_B2], ps[:, 0, 0:(NE + 1) * FC].rearrange("p (e f) -> p e f", f=FC), ACT.Copy)
                    nc.scalar.activation(records[:, 0:NE, REC_B2:], ps[:, 1:3, :].rearrange("p a (e h) -> p (a e) h", h=E), ACT.Copy)
                    nc.scalar.activation(records[:, NE, REC_B2:], ps[:, 3, 0:E], ACT.Copy).then_inc(s["set_r"], 1)

                shared, routed = experts_programs["scalar"](act)

                def iteration(i, par):
                    for u in range(UNITS):
                        if u == 1 and has(i, -1):
                            b = i + 1
                            act.wait_ge(s["var_ps"], b + 1)
                            wait(act, s["rows_out"], ROWS_OUT * b)
                            nc.scalar.activation(var_hi[:, :, :], mi["VAR"][0:H, :].rearrange("p (a t) -> p a t", a=2), ACT.Copy).then_inc(s["var_hi_r"], 1)
                        if u == 4 and has(i, 3):
                            b = i - 3
                            act.wait_ge(s["x2t_ps"], b + 1)
                            wait(act, s["rt_ps"], b)
                            wait(act, s["xkeep"], b)
                            nc.scalar.activation(x2nT[:, :], mi["X2T"][:, 0:S], ACT.Copy).then_inc(s["x2nT_r"], 1)
                        b, k, lag = pass2_at(i, u)
                        if has(i, lag):
                            g = k // 2
                            for a in range(2):
                                act.wait_ge(s["st_ps"], H * b + 2 * k + a + 1)
                                if a == 0:
                                    wait(act, s["pv_ps"], G * b + g - 1)
                                nc.scalar.activation(probs[g % 2][:, 2 * (k % 2) + a, :, :].rearrange("p q t -> p (q t)"), ps_st[a], ACT.Exp).then_inc(s["exp_r"], 1)
                        if u == 0 and has(i, 1):
                            b = i - 1
                            act.wait_ge(s["mt_ps"], b + 1)
                            wait(act, s["mrow_in"], MROWS * b)
                            nc.scalar.activation(mT[:, :, :].rearrange("p g t -> p (g t)"), mi["MT"].bitcast(BF16)[0:2 * HG, :], ACT.Copy).then_inc(s["mt_r"], 1)
                        if u == 5 and has(i, 2):
                            b = i - 2
                            act.wait_ge(s["ont_ps"], b + 1)
                            wait(act, s["wo_ps"], b)
                            nc.scalar.activation(onT[:, :], mi["ONT"][:, 0:S], ACT.Copy).then_inc(s["onT_r"], 1)
                        b, g, lag = pv_at(i, u)
                        if g is not None and has(i, lag):
                            act.wait_ge(s["pv_ps"], G * b + g + 1)
                            wait(act, s["ott_ps"], G * (b - 1) + g + 1)
                            nc.scalar.activation(oT[:, g, :], ps_pv[:, 0:S], ACT.Copy).then_inc(s["ot_r"], 1)
                        if u == 2 and has(i, 0):
                            act.wait_ge(s["v_ps"], i + 1)
                            wait(act, s["pv_ps"], G * (i - 1))
                            if isinstance(i, int) and i == 0:
                                act.wait_ge(s["vx_init"], 1)
                            for q in range(QT):
                                last = nc.scalar.activation(vx[par][:, q, :, 0:D], mi["V"][:, q * E:(q + 1) * E].rearrange("p (h d) -> p h d", d=D), ACT.Copy)
                            last.then_inc(s["v_r"], 1)
                        if u == 3 and has(i, -2):
                            b = i + 2
                            act.wait_ge(s["xt_ps"], b + 1)
                            wait(act, s["v_ps"], b - 1)
                            nc.scalar.activation(xnT[par][:, :], mi["T"][:, 0:S], ACT.Copy).then_inc(s["xnT_r"], 1)
                        if u == 4 and has(i, -2):
                            b = i + 2
                            act.wait_ge(s["qk_ps"], b + 1)
                            wait(act, s["rows_out"], ROWS_OUT * b)
                            src = mi["QK"].rearrange("p (a t) -> p a t", a=2)
                            nc.scalar.activation(qk_hi, src, ACT.Copy).then_inc(s["qk_hi_r"], 1)
                            wait(act, s["var_ps"], b)
                            nc.scalar.activation(qk_sq[:, :, :], src, ACT.Square).then_inc(s["sq_r"], 1)
                        for n in shared_here(i, u):
                            shared(n)

                run(act, iteration, {0: biases})
                for n in range(len(shared_at), NS):
                    shared(n)
                routed()

            @block.tensor
            def _(pe):
                pe.wait_ge(s["c_in"], 16)
                pe.wait_ge(s["w_in"], 16 * 4)
                for n, m in enumerate(("centre_q", "centre", "ident", "ident")):
                    last = nc.tensor.matmul(ps[:, 0, n * E:(n + 1) * E], wraw[:, n, :], con(m), start=True, stop=True)
                last.then_inc(s["set_ps"], 1)

                def biases():
                    pe.wait_ge(s["b_in"], 16 * 5)
                    pe.wait_ge(s["set_r"], 1)
                    nb = (NE + 1) * FC
                    nc.tensor.transpose(ps[:, 0, 0:nb], b1r[:, :], con("ident", nb)[:, 0:nb])
                    pe.wait_ge(s["ones_r"], 1)
                    for a in range(3):
                        n = min(512, (NE + 1) * E - 512 * a)
                        last = nc.tensor.matmul(ps[:, 1 + a, 0:n], ones_f[:, :], b2r[:, 512 * a:512 * a + n], start=True, stop=True)
                    last.then_inc(s["set_ps"], 1)
                    pe.wait_ge(s["set_r"], 2)

                pe.wait_ge(s["set_r"], 1)

                prev = [None] * 3

                def misc(step, sem_name, value):
                    k = MISC[step]
                    if prev[k] is not None:
                        pe.wait_ge(s[prev[k][0]], prev[k][1])
                    prev[k] = (sem_name, value)
                    return mi[step]

                def heads_out(b, g):
                    pe.wait_ge(s["ot_r"], G * b + g + 1)
                    bank = misc(f"OTT{g}", "on_r", G * b + g + 1)
                    for q in range(QT):
                        last = nc.tensor.transpose(bank[:, q * P:(q + 1) * P], oT[:, g, q * P:(q + 1) * P], con("ident"))
                    last.then_inc(s["ott_ps"], 1)

                def step_a(i, par, u):
                    if u == 0 and has(i, 2):
                        heads_out(i - 2, 1)
                    if u == 1 and has(i, -1):
                        b = i + 1
                        pe.wait_ge(s["sq_r"], b + 1)
                        bank = misc("VAR", "var_lo_r", b + 1)
                        nc.tensor.matmul(bank[0:H, 0:S], con("ind_q"), qk_sq[:, 0, :], start=True, stop=True)
                        nc.tensor.matmul(bank[0:H, S:2 * S], con("ind_k"), qk_sq[:, 1, :], start=True, stop=True).then_inc(s["var_ps"], 1)
                    if u == 3 and has(i, 2):
                        heads_out(i - 2, 3)
                    if u == 4 and has(i, 3):
                        b = i - 3
                        pe.wait_ge(s["xrow_r"], b + 1)
                        bank = misc("X2T", "x2nT_r", b + 1)
                        for q in range(QT):
                            last = nc.tensor.transpose(bank[:, q * P:(q + 1) * P], xrow[1 - par][:, q, 0, 0:E], con("ident"))
                        last.then_inc(s["x2t_ps"], 1)
                    if u == 5 and has(i, 3):
                        b = i - 3
                        pe.wait_ge(s["x2nT_r"], b + 1)
                        bank = misc("RT", "lg_r", b + 1)
                        for q in range(QT):
                            last = nc.tensor.matmul(bank[:, q * NE:(q + 1) * NE], x2nT[:, q * P:(q + 1) * P], wg[:, :], start=True, stop=True)
                        last.then_inc(s["rt_ps"], 1)
                    if u == 7 and has(i, 1):
                        heads_out(i - 1, 0)

                def step_b(i, par, u):
                    if u == 1 and has(i, 2):
                        heads_out(i - 2, 2)
                    if u == 2 and has(i, 0):
                        pe.wait_ge(s["xnT_r"], i + 1)
                        bank = misc("V", "v_r", i + 1)
                        for q in range(QT):
                            last = nc.tensor.matmul(bank[:, q * E:(q + 1) * E], xnT[par][:, q * P:(q + 1) * P], wvT[:, :], start=True, stop=True)
                        last.then_inc(s["v_ps"], 1)
                    if u == 3 and has(i, -2):
                        b = i + 2
                        pe.wait_ge(s["xn_r"], b + 1)
                        bank = misc("T", "xnT_r", b + 1)
                        for q in range(QT):
                            last = nc.tensor.transpose(bank[:, q * P:(q + 1) * P], xn[:, q, :], con("ident"))
                        last.then_inc(s["xt_ps"], 1)
                    if u == 4 and has(i, -2):
                        b = i + 2
                        pe.wait_ge(s["xnT_r"], b + 1)
                        bank = misc("QK", "qk_lo_r", b + 1)
                        nc.tensor.matmul(bank[:, 0:S], wqT[:, :], xnT[par][:, :], start=True, stop=True)
                        nc.tensor.matmul(bank[:, S:2 * S], wkT[:, :], xnT[par][:, :], start=True, stop=True).then_inc(s["qk_ps"], 1)
                    if u == 5 and has(i, 2):
                        b = i - 2
                        pe.wait_ge(s["on_r"], G * (b + 1))
                        bank = misc("ONT", "onT_r", b + 1)
                        for q in range(QT):
                            last = nc.tensor.transpose(bank[:, q * P:(q + 1) * P], on[:, q, :], con("ident"))
                        last.then_inc(s["ont_ps"], 1)
                    if u == 6 and has(i, 2):
                        b = i - 2
                        pe.wait_ge(s["onT_r"], b + 1)
                        bank = misc("WO", "x2_r", b + 1)
                        for q in range(QT):
                            last = nc.tensor.matmul(bank[:, q * E:(q + 1) * E], onT[:, q * P:(q + 1) * P], woT[:, :], start=True, stop=True)
                        last.then_inc(s["wo_ps"], 1)
                    if u == 7 and has(i, 3):
                        b = i - 3
                        pe.wait_ge(s["taken_r"], b + 1)
                        pe.wait_ge(s["tsum_r"], b + 1)
                        bank = misc("POS", "pos_r", b + 1)
                        nc.tensor.matmul(bank[:, 0:NE], tri_b[:, :], taken[:, 0, :], start=True, stop=False)
                        nc.tensor.matmul(bank[:, 0:NE], ones_b[:, :], taken_sum[:, :], start=False, stop=True)
                        nc.tensor.matmul(bank[:, NE:2 * NE], tri_b[:, :], taken[:, 1, :], start=True, stop=False)
                        nc.tensor.matmul(bank[:, NE:2 * NE], ones_b[:, :], taken[:, 0, :], start=False, stop=False)
                        nc.tensor.matmul(bank[:, NE:2 * NE], ones_b[:, :], taken_sum[:, :], start=False, stop=True).then_inc(s["pos_ps"], 1)

                def step_maxima(i, par, u):
                    if u == 0 and has(i, 1):
                        b = i - 1
                        pe.wait_ge(s["m_r"], b + 1)
                        bank = misc("MT", "mt_r", b + 1)
                        for g in range(G):
                            for q in range(QT):
                                last = nc.tensor.transpose(bank.bitcast(BF16)[0:2 * HG, g * S + q * P:g * S + (q + 1) * P],
                                                           m_parts[:, q, g, :, :].rearrange("p c j -> p (c j)"), ident_b[:, :])
                        last.then_inc(s["mt_ps"], 1)

                def iteration(i, par):
                    if not isinstance(i, int) or i == B - 2:
                        prev[:] = ("x2_r", i - 2), ("on_r", (i - 2) * G + 1), ("pos_r", i - 3)
                    for u in range(UNITS):
                        if has(i, 0):
                            g = u // 2
                            if u % 4 == 0:
                                pe.wait_ge(s_ld[u // 4], LOADS * (i + 1))
                            j = 2 * (u % 2)
                            for q in range(QT):
                                wait(pe, s["max_r"], QT * (UNITS * i + u - 1) + q + 1)
                                nc.tensor.matmul(ps_s1[q][:, :, :], qa[par][:, g, q * P:(q + 1) * P], ka[par][:, g, j:j + 2, :],
                                                 start=True, stop=True).then_inc(s["s1_ps"], 1)
                        step_a(i, par, u)
                        b, k, lag = pass2_at(i, u)
                        if has(i, lag):
                            bp = (par + lag) % 2
                            if k == 0:
                                pe.wait_ge(s["mrow_in"], MROWS * (b + 1))
                            for a in range(2):
                                h = 2 * k + a
                                g, j = h // HG, h % HG
                                wait(pe, s["exp_r"], H * b + h - 1)
                                for q in range(QT):
                                    last = nc.tensor.matmul(ps_st[a][:, q * S:(q + 1) * S], ka[bp][:, g, j, q * P:(q + 1) * P], qa[bp][:, g, :], start=True, stop=True)
                                last.then_inc(s["st_ps"], 1)
                        step_maxima(i, par, u)
                        b, g, lag = pv_at(i, u)
                        if g is not None and has(i, lag):
                            bp = (par + lag) % 2
                            if g == 0:
                                pe.wait_ge(s["v_r"], b + 1)
                            pe.wait_ge(s["exp_r"], H * b + HG * (g + 1))
                            wait(pe, s["ot_r"], G * b + g)
                            for q in range(QT):
                                for j in range(HG):
                                    last = nc.tensor.matmul(ps_pv[ROWS * j:ROWS * (j + 1), 0:S], vx[bp][:, q, HG * g + j, :], probs[g % 2][:, j, q, :],
                                                            start=q == 0, stop=q == QT - 1, tile_position=(0, ROWS * j))
                            last.then_inc(s["pv_ps"], 1)
                        step_b(i, par, u)
                        for n in shared_here(i, u):
                            shared(n)

                shared, routed = experts_programs["tensor"](pe)
                run(pe, iteration, {0: biases})
                pe.wait_ge(s["tsum_r"], B + 1)
                nc.tensor.matmul(misc("POS", "", 0)[:, 0:NE], ones_b[:, :], taken_sum[:, :], start=True, stop=True).then_inc(s["cnt_ps"], 1)
                for n in range(len(shared_at), NS):
                    shared(n)
                for k in range(2):
                    pe.wait_ge(s[prev[k][0]], prev[k][1])
                routed()

            @block.vector
            def _(dve):
                dve.wait_ge(s["c_in"], 16)
                nc.vector.tensor_copy(ident_b[:, :], con("ident"))
                nc.vector.tensor_copy(tri_b[:, :], con("tri"))
                nc.vector.memset(ones_b[:, :], 1.0)
                nc.vector.memset(taken_sum[:, :], 0.0)
                nc.vector.tensor_copy(idrun[:, :], con("ids")).then_inc(s["tsum_r"], 1)
                nc.vector.memset(ones_f[:, :], 1.0).then_inc(s["ones_r"], 1)

                ln1 = [Chain(dve, s["ln1c"], 18, n) for n in range(len(CHUNKS))]

                def moments_1(n):
                    dve.wait_ge(x_in[n], 16)
                    c = ln1[n]
                    for t in range(*CHUNKS[n]):
                        last = nc.vector.bn_stats(st1[:, t, :], xs[:, t, :])
                    c(last)
                    for t in range(*CHUNKS[n]):
                        last = nc.vector.bn_aggr(mv1[:, t, :], st1[:, t, :])
                    c(last)

                def scales_1(n):
                    c, r = ln1[n], slice(*CHUNKS[n])
                    c(nc.vector.tensor_scalar(ve1[:, r], mv1[:, r, 1], EPS, None, ALU.add))
                    c(nc.vector.tensor_scalar(t1[:, r].bitcast(I32), ve1[:, r].bitcast(I32), 1, None, ALU.logical_shift_right))
                    c(nc.vector.tensor_scalar(y1[:, r].bitcast(I32), t1[:, r].bitcast(I32), -1.0, MAGIC, ALU.mult, ALU.add))
                    for _ in range(3):
                        c(nc.vector.tensor_tensor(t1[:, r], y1[:, r], y1[:, r], ALU.mult))
                        c(nc.vector.tensor_tensor(t1[:, r], t1[:, r], ve1[:, r], ALU.mult))
                        c(nc.vector.tensor_scalar(t1[:, r], t1[:, r], -0.5, 1.5, ALU.mult, ALU.add))
                        c(nc.vector.tensor_tensor(y1[:, r], y1[:, r], t1[:, r], ALU.mult))
                    c(nc.vector.tensor_tensor(t1[:, r], mv1[:, r, 0], y1[:, r], ALU.mult))
                    c.done()
                    nc.vector.tensor_scalar(nmr1[:, r], t1[:, r], -1.0, None, ALU.mult).then_inc(s["ln1"], 1)

                moments_1(0)
                scales_1(0)
                moments_1(1)


                def normalise(b, g):
                    sums = mi[f"OTT{g}"][:, 0:S].rearrange("p (q j r) -> p q j r", q=QT, r=ROWS)

                    def denominators():
                        dve.wait_ge(s["ott_ps"], G * b + g + 1)
                        nc.vector.reciprocal(rden[:, g, :, :].unsqueeze(3), sums[:, :, :, D:D + 1]).then_inc(s["rd_r"], 1)

                    def product():
                        dve.wait_ge(s["rd_r"], G * b + g + 1)
                        if g == 0:
                            wait(dve, s["ont_ps"], b)
                        nc.vector.tensor_tensor(on[:, :, HG * D * g:HG * D * (g + 1)].rearrange("p q (j d) -> p q j d", d=D), sums[:, :, :, 0:D],
                                                rden[:, g, :, :].unsqueeze(3).to_broadcast([P, QT, HG, D]), ALU.mult).then_inc(s["on_r"], 1)
                    return denominators, product

                def residual(b):
                    dve.wait_ge(s["wo_ps"], b + 1)
                    wait(dve, s["x2keep"], b)
                    nc.vector.tensor_tensor(x2[:, :, :], mi["WO"][:, 0:QT * E].rearrange("p (q e) -> p q e", q=QT), xs[:, bass.ds(QT * b, QT), :], ALU.add).then_inc(s["x2_r"], 1)

                def statistics(b, par, taken_before=0):
                    c = Chain(dve, s["x2c"], 4, b, s["passed"])
                    c.n = taken_before

                    def sums():
                        wait_apart(dve, s["passed"], (s["x2_r"], b + 1))
                        for q in range(QT):
                            last = nc.vector.bn_stats(st2[:, q, :], x2[:, q, :])
                        c.count(last)

                    def moments():
                        c.ready()
                        for q in range(QT):
                            last = nc.vector.bn_aggr(mv2[:, q, :], st2[:, q, :])
                        c.count(last)

                    def var_eps():
                        c.ready()
                        c.count(nc.vector.tensor_scalar(ve2[:, :], mv2[:, :, 1], EPS, None, ALU.add))

                    def halved():
                        c.ready()
                        c.count(nc.vector.tensor_scalar(t2[:, :].bitcast(I32), ve2[:, :].bitcast(I32), 1, None, ALU.logical_shift_right))

                    def guess():
                        c.ready()
                        c.done()
                        nc.vector.tensor_scalar(y2[:, :].bitcast(I32), t2[:, :].bitcast(I32), -1.0, MAGIC, ALU.mult, ALU.add).then_inc(s["y0_r"], 1)

                    def numbers():
                        wait(dve, s["scat"], 16 * QT * TOPK * (b - 1))
                        wait(dve, s["idc"], b)
                        nc.vector.tensor_copy(xrow[par][:, :, :, E:].bitcast(I32).rearrange("p q k o -> p (q k) o"), idrun[:, :].unsqueeze(2)).then_inc(s["id_r"], 1)
                        dve.wait_ge(s["id_r"], b + 1)
                        nc.vector.tensor_scalar(idrun[:, :], idrun[:, :], float(TOPK * S), None, ALU.add).then_inc(s["idc"], 1)
                    return sums, moments, var_eps, halved, guess, numbers

                def route(b):
                    c = Chain(dve, s["rtc"], 3, b)

                    def logits_read():
                        dve.wait_ge(s["rt_ps"], b + 1)
                        wait(dve, s["keep_r"], b)
                        nc.vector.tensor_copy(lg[:, :, :], mi["RT"][:, 0:QT * NE].rearrange("p (q e) -> p q e", q=QT)).then_inc(s["lg_r"], 1)

                    def largest():
                        wait_apart(dve, s["passed"], (s["lg_r"], b + 1))
                        for q in range(QT):
                            last = nc.vector.max(v8[:, q, :], lg[:, q, :])
                        last.then_inc(s["v8_r"], 1)

                    def their_experts():
                        wait_apart(dve, s["passed"], (s["v8_r"], b + 1))
                        for q in range(QT):
                            last = nc.vector.max_index(i8[:, q, :], v8[:, q, :], lg[:, q, :])
                        c.count(last)

                    def as_float():
                        c.ready()
                        c.count(nc.vector.tensor_copy(idxf[:, :, :], i8[:, :, 0:TOPK]))

                    def one_hot():
                        c.ready()
                        n = QT * TOPK
                        c.count(nc.vector.tensor_tensor(onehot[:, :, :, :].rearrange("p q k e -> p (q k) e"), con("iota8").unsqueeze(1).to_broadcast([P, n, NE]),
                                                         idxf[:, :, :].rearrange("p q k -> p (q k)").unsqueeze(2).to_broadcast([P, n, NE]), ALU.is_equal))

                    def both():
                        c.ready()
                        c.done()
                        nc.vector.tensor_tensor(taken[:, :, :], onehot[:, :, 0, :], onehot[:, :, 1, :], ALU.add).then_inc(s["taken_r"], 1)
                    return logits_read, largest, their_experts, as_float, one_hot, both

                def places(b, par):
                    c = Chain(dve, s["posc"], 3, b)

                    def before():
                        dve.wait_ge(s["pos_ps"], b + 1)
                        nc.vector.tensor_tensor(place[:, :, :], mi["POS"][:, 0:QT * NE].rearrange("p (q e) -> p q e", q=QT),
                                                con("region").unsqueeze(1).to_broadcast([P, QT, NE]), ALU.add).then_inc(s["pos_r"], 1)

                    def chosen():
                        dve.wait_ge(s["pos_r"], b + 1)
                        c.count(nc.vector.tensor_tensor(placed[:, :, :, :], onehot[:, :, :, :], place[:, :, :].unsqueeze(2).to_broadcast([P, QT, TOPK, NE]), ALU.mult))

                    def slots():
                        c.ready()
                        c.count(nc.vector.tensor_reduce(slotf[:, :], placed[:, :, :, :].rearrange("p q k e -> p (q k) e"), AX.X, ALU.add))

                    def slots_out():
                        c.ready()
                        wait(dve, s["scat"], 16 * QT * TOPK * (b - 1))
                        nc.vector.tensor_copy(slot[par][:, :], slotf[:, :]).then_inc(s["slot_r"], 1)
                        c.count(nc.vector.tensor_tensor(taken_sum[:, :], taken_sum[:, :], taken[:, 0, :], ALU.add))

                    def counted():
                        c.ready()
                        c.done()
                        nc.vector.tensor_tensor(taken_sum[:, :], taken_sum[:, :], taken[:, 1, :], ALU.add).then_inc(s["tsum_r"], 1)
                    return before, chosen, slots, slots_out, counted

                def var_low(b):
                    dve.wait_ge(s["var_hi_r"], b + 1)
                    nc.vector.tensor_tensor(var_lo[:, :, :], mi["VAR"][0:H, :].rearrange("p (a t) -> p a t", a=2), var_hi[:, :, :], ALU.subtract).then_inc(s["var_lo_r"], 1)

                def qk_low(b):
                    dve.wait_ge(s["sq_r"], b + 1)
                    nc.vector.tensor_tensor(qk_lo, mi["QK"].rearrange("p (a t) -> p a t", a=2), qk_hi, ALU.subtract).then_inc(s["qk_lo_r"], 1)

                def iteration(i, par):
                    at = {(u, q): [] for u in range(UNITS) for q in range(QT)}

                    def put(works, *positions):
                        for work, pos in zip(works, positions, strict=True):
                            at[positions[0] if isinstance(i, int) and i > B else pos].append(work)

                    if has(i, 4):
                        put(places(i - 4, par), (0, 0), (0, 1), (1, 0), (1, 1), (2, 0))
                    if has(i, 3):
                        _, _, *rest = statistics(i - 3, 1 - par, taken_before=2)
                        put(rest, (0, 0), (0, 1), (1, 0), (4, 1))
                        put(route(i - 3), (5, 0), (5, 1), (6, 0), (6, 0), (6, 1), (6, 1))
                    if has(i, -1):
                        put((lambda: var_low(i + 1),), (2, 0))
                    if has(i, -2):
                        put((lambda: qk_low(i + 2),), (5, 1))
                    if has(i, 2):
                        put(normalise(i - 2, 1), (0, 1), (1, 0))
                        put(normalise(i - 2, 2), (2, 0), (2, 1))
                        put(normalise(i - 2, 3), (3, 1), (4, 0))
                        put((lambda: residual(i - 2),), (7, 0))
                        stats = statistics(i - 2, par)
                        put(stats[0:1], (7, 1))
                    for u in range(UNITS):
                        for q in range(QT):
                            if has(i, 0):
                                if u == 0 and q == 0:
                                    wait(dve, s["m_r"], i)
                                dve.wait_ge(s["s1_ps"], QT * (UNITS * i + u) + q + 1)
                                nc.vector.tensor_reduce(negmax[:, q, 2 * u:2 * u + 2], ps_s1[q], AX.X, ALU.max, negate=True).then_inc(s["max_r"], 1)
                            for work in at[u, q]:
                                work()
                        for n in shared_here(i, u):
                            shared(n)
                    late = list(normalise(i - 1, 0)) if has(i, 1) else []
                    if has(i, 0):
                        wait(dve, s["mt_ps"], i)
                        dve.wait_ge(s["max_r"], (i + 1) * UNITS * QT)
                        c = Chain(dve, s["mc"], 1, i)
                        neg = negmax[:, :, :].rearrange("p q (g j) -> p q g j", g=G)
                        c.count(nc.vector.tensor_copy(m_parts[:, :, :, 0, :], neg))
                        if late:
                            late.pop(0)()
                        c.ready()
                        nc.vector.tensor_tensor(m_parts[:, :, :, 1, :], neg, m_parts[:, :, :, 0, :], ALU.subtract).then_inc(s["m_r"], 1)
                    for work in late:
                        work()
                    if has(i, 2):
                        stats[1]()

                shared, tile_list, routed = experts_programs["vector"](dve)
                run(dve, iteration, {0: lambda: scales_1(1)})
                n = len(shared_at)
                for steps in tile_list:
                    steps()
                    shared(n)
                    n += 1
                for n in range(n, NS):
                    shared(n)
                routed()



def experts_phase(nc, sb, sem, v):
    xs, records, x2nT_all, logits, top8 = (v[n] for n in ("xs", "records", "x2nT_all", "logits", "top8"))
    starts, experts, xrows, orows, out = (v[n] for n in ("starts", "experts", "xrows", "orows", "out"))
    con, ps, pad_row, a = (v[n] for n in ("con", "ps", "pad_row", "s"))
    passed, pads_out = a["passed"], a["pads_out"]
    ident = con("ident")
    cnt = sb("cnt", [P, NE])
    full = sb("full", [P, NE, NS])
    ntile, tbase, total = sb("ntile", [P, NE]), sb("tbase", [P, NE]), sb("total", [P, 1])
    low = sb("low", [P, NE, NE])
    ge = sb("ge", [P, TILES, NE])
    gt_ = sb("gt_", [P, TILES, NE])
    ex, tb, stf, dead = (sb(n, [P, TILES]) for n in ("ex", "tb", "stf", "dead"))
    padf, padi = sb("padf", [P, NE]), sb("padi", [P, NE], I32)
    xT = [sb(f"xT{i}", [P, 2, TT], BF16) for i in range(XT)]
    ysh = sb("ysh", [P, TQ, E])
    dl = sb("dl", [P, NT, NE + 1])
    el = sb("el", [P, NT, NE + 1])
    esum, wt = sb("esum", [P, NT]), sb("wt", [P, 2, NT])
    hid = [v["fill"][:, :, :, :].rearrange("p a g t -> p (a g t)").bitcast(F32).rearrange("p (f t) -> p f t", f=FC), sb("hid1", [P, FC, TT])]
    left = ([v["probs"][i][:, :, :, :].rearrange("p j q t -> p (j q t)") for i in range(2)]
            + [v["ka"][i][:, :, :, :].rearrange("p g j t -> p (g j t)").bitcast(F32) for i in range(2)])
    rec = [space[:, 0:REC] for space in left]
    xg = [left[i // 2][:, REC + i % 2 * TQ * XW:REC + (i % 2 + 1) * TQ * XW].rearrange("p (q w) -> p q w", q=TQ) for i in range(XB)]
    yb = [v["vx"][i // 4][:, :, :, :].rearrange("p q h r -> p (q h r)")[:, i % 4 * TQ * E:(i % 4 + 1) * TQ * E].rearrange("p (q e) -> p q e", q=TQ) for i in range(XB)]
    CH, OG = 4, 4
    og = [space[:, 0:CH * TOPK * E].rearrange("p (c k e) -> p c k e", c=CH, k=TOPK) for space in left]
    ob = [space[:, CH * TOPK * E:CH * (TOPK + 1) * E].rearrange("p (c e) -> p c e", c=CH) for space in left]
    ps_h = [ps[:, 2 * i:2 * i + 2, :].rearrange("p b (f t) -> p (b f) t", f=FC // 2) for i in range(2)]
    ps_y = ps[:, 4, 0:TQ * E].rearrange("p (q e) -> p q e", q=TQ)
    ps_t = [ps[:, 5 + i, :] for i in range(2)]
    list_r = sem("f_list_r")
    s = {n: sem("f_" + n) for n in "xt_ps listc pad_i_r rec_r xhi_r xlo_r h_ps h_r y_ps y_r ysh_r wt_d wt_e wtc wt_r o_c og_w o_r".split()}
    s_in, s_out = ([sem(f"f_{n}{j}") for j in range(XB)] for n in ("in", "out"))
    s_og, s_fin = ([sem(f"f_{n}{j}") for j in range(OG)] for n in ("og", "fin"))
    NCH = NT // CH
    ROUNDS = TILES // XB

    def sync(sp):
        def fetch(r, j):
            wait_apart(sp, passed, (s_out[j], 16 * TQ * r))
            row = sp.value_load(starts[0:1, bass.ds(r * XB + j, 1)], min_val=0, max_val=XROWS - TT)
            sp.dma_start(xg[j][:, :, :], xrows[bass.ds(row, TT), :].rearrange("(q p) w -> p q w", p=P)).then_inc(s_in[j], 16)

        sp.wait_ge(s["pad_i_r"], 1)
        for e in range(NE):
            row = sp.value_load(padi[0:1, e:e + 1], min_val=0, max_val=DUMMY - TT)
            sp.dma_start(xrows[bass.ds(row, TT), :].rearrange("(q p) w -> p q w", p=P), pad_row[:, :, :]).then_inc(pads_out, 16)
        sp.wait_ge(list_r, 1)
        sp.wait_ge(pads_out, 16 * NE)
        sp.wait_ge(a["scat"], 16 * QT * TOPK * B)
        for j in range(XB):
            fetch(0, j)
        with sp.Fori(1, ROUNDS) as r:
            for j in range(XB):
                fetch(r, j)
        for j in range(XB):
            sp.wait_ge(s_out[j], 16 * TQ * ROUNDS)
        ov = orows.rearrange("(t p k) e -> p t k e", p=P, k=TOPK)
        outv = out.rearrange("b (q p) e -> p (b q) e", p=P)

        def results(n):
            sp.dma_start(og[n % OG][:, :, :, :], ov[:, CH * n:CH * (n + 1), :, :]).then_inc(s_og[n % OG], 16)

        for n in range(OG):
            results(n)
        for n in range(NCH):
            sp.wait_ge(s["o_r"], n + 1)
            sp.dma_start(outv[:, CH * n:CH * (n + 1), :], ob[n % OG][:, :, :]).then_inc(s_fin[n % OG], 16)
            if n + OG < NCH:
                results(n + OG)
        for n in range(OG):
            sp.wait_ge(s_fin[n], 16 * NCH // OG)

    def tensor(pe):
        def turn(r, j):
            t = r * XB + j
            pe.wait_ge(s_in[j], 16 * (r + 1))
            wait(pe, s["xlo_r"], t + NS - 1)
            for q in range(TQ):
                last = nc.tensor.transpose(ps_t[j % 2][:, q * P:(q + 1) * P], xg[j][:, q, 0:E], ident)
            last.then_inc(s["xt_ps"], 1)

        def up(n, m, w):
            pe.wait_ge(s["xlo_r"], n + 1)
            wait(pe, s["h_r"], n - 1)
            high, low = w[:, 0:REC_L].bitcast(BF16), w[:, REC_L:REC_W2].bitcast(BF16)
            for f in range(FC):
                at = slice(f * P, (f + 1) * P)
                nc.tensor.matmul(ps_h[m % 2][:, f, :], high[:, at], xT[m][:, 0, :], start=True, stop=False)
                nc.tensor.matmul(ps_h[m % 2][:, f, :], high[:, at], xT[m][:, 1, :], start=False, stop=False)
                last = nc.tensor.matmul(ps_h[m % 2][:, f, :], low[:, at], xT[m][:, 0, :], start=False, stop=True)
            last.then_inc(s["h_ps"], 1)

        def down(n, m, w):
            pe.wait_ge(s["h_r"], n + 1)
            wait(pe, s["y_r"], n)
            for q in range(TQ):
                for f in range(FC):
                    last = nc.tensor.matmul(ps_y[:, q, :], hid[m % 2][:, f, q * P:(q + 1) * P],
                                            w[:, REC_W2 + f * E:REC_W2 + (f + 1) * E], start=f == 0, stop=f == FC - 1)
            last.then_inc(s["y_ps"], 1)

        def shared(n):
            if n == 0:
                pe.wait_ge(a["split_r"], 2 * (NE + 1))
                pe.wait_ge(a["max_r"], UNITS * QT * B)
                pe.wait_ge(a["exp_r"], H * B)
            up(n, n % XT, records[:, SHARED, :])
            if n == 2:
                pe.wait_ge(a["w2_in"], 16 * (NE + 1))
                pe.wait_ge(a["ot_r"], G * B)
            if n >= 2:
                down(n - 2, (n - 2) % XT, records[:, SHARED, :])

        def first():
            turn(0, 0)
            turn(0, 1)
            up(NS, 0, rec[0])
            down(NS - 2, (NS - 2) % XT, records[:, SHARED, :])

        def step(r, j):
            t = r * XB + j
            static = isinstance(r, int)
            if not static or t + 2 < TILES:
                turn(r + (j + 2) // XB, (j + 2) % XB)
            if not static or t + 1 < TILES:
                up(t + 1 + NS, (j + 1) % XT, rec[(j + 1) % XT])
            down(t - 1 + NS, (j - 1) % XT, records[:, SHARED, :] if static and t == 0 else rec[(j - 1) % XT])

        def routed():
            first()
            for j in range(XB):
                step(0, j)
            with pe.Fori(1, ROUNDS - 1) as r:
                for j in range(XB):
                    step(r, j)
            for j in range(XB):
                step(ROUNDS - 1, j)
            down(TILES - 1 + NS, (TILES - 1) % XT, rec[(TILES - 1) % XT])
        return shared, routed

    def scalar(act):
        def silu(n, m, w):
            act.wait_ge(s["h_ps"], n + 1)
            wait(act, s["y_ps"], n - 1)
            for f in range(FC):
                last = nc.scalar.activation(hid[m % 2][:, f, :], ps_h[m % 2][:, f, :], ACT.Silu, bias=w[:, REC_B1 + f:REC_B1 + f + 1])
            last.then_inc(s["h_r"], 1)

        def shared(n):
            if n == 0:
                act.wait_ge(a["set_r"], 2)
            silu(n, n, records[:, SHARED, :])

        def routed():
            with act.Fori(0, TILES, XT) as t:
                for j in range(XT):
                    silu(t + j + NS, j, rec[j])
            act.wait_ge(s["wt_d"], 1)
            nc.scalar.activation(el[:, :, :], dl[:, :, :], ACT.Exp).then_inc(s["wt_e"], 1)
            act.wait_ge(s["wt_r"], 1)
            for n in range(NCH):
                act.wait_ge(s_og[n % OG], 16 * (n // OG + 1))
                for q in range(CH):
                    row = og[n % OG][:, q, 1, :]
                    last = nc.scalar.activation(row, row, ACT.Copy, scale=wt[:, 1, CH * n + q:CH * n + q + 1])
                last.then_inc(s["og_w"], 1)
        return shared, routed

    def vector(dve):
        def parts(n, m, src):
            wait(dve, s["h_ps"], n - XT + 1)
            nc.vector.tensor_copy(xT[m][:, 0, :], src).then_inc(s["xhi_r"], 1)
            dve.wait_ge(s["xhi_r"], n + 1)
            nc.vector.tensor_tensor(xT[m][:, 1, :], src, xT[m][:, 0, :], ALU.subtract).then_inc(s["xlo_r"], 1)

        def shared_parts(n, m):
            parts(n, m, x2nT_all[:, bass.ds(n * TT, TT)])

        def shared_out(n, par):
            dve.wait_ge(s["y_ps"], n + 1)
            wait(dve, s["ysh_r"], 2 * n)
            nc.vector.tensor_tensor(ysh[:, :, :], ps_y, records[:, SHARED:SHARED + 1, REC_B2:].to_broadcast([P, TQ, E]), ALU.add).then_inc(s["y_r"], 1)
            dve.wait_ge(s["y_r"], n + 1)
            at = bass.ds(n * TQ, TQ)
            nc.vector.scalar_tensor_tensor(xs[:, at, :], ysh[:, :, :], SHARED_SCALE, xs[:, at, :], ALU.mult, ALU.add).then_inc(s["ysh_r"], 2)

        def shared(n):
            for k in range(3) if n == 0 else range(n + 2, min(n + 3, NS)):
                dve.wait_ge(a["xkeep"], k + 1)
                shared_parts(k, k % XT)
            if n >= 2:
                dve.wait_ge(a["x2keep"], n - 1)
                shared_out(n - 2, (n - 2) % 2)

        c = Chain(dve, s["listc"], 18, 0)

        def rows_by_expert():
            dve.wait_ge(a["cnt_ps"], 1)
            c(nc.vector.tensor_copy(cnt[:, :], v["mi"]["POS"][:, 0:NE]))
            c(nc.vector.tensor_tensor(padf[:, :], cnt[:, :], con("region"), ALU.add))
            nc.vector.tensor_copy(padi[:, :], padf[:, :]).then_inc(s["pad_i_r"], 1)
            c(nc.vector.tensor_tensor(full[:, :, :], cnt[:, :].unsqueeze(2).to_broadcast([P, NE, NS]), con("steps").unsqueeze(1).to_broadcast([P, NE, NS]), ALU.is_gt))
            c(nc.vector.tensor_reduce(ntile[:, :], full[:, :, :], AX.X, ALU.add))
            c(nc.vector.tensor_tensor(low[:, :, :], con("lower").rearrange("p (a b) -> p a b", b=NE), ntile[:, :].unsqueeze(1).to_broadcast([P, NE, NE]), ALU.mult))
            c(nc.vector.tensor_reduce(tbase[:, :], low[:, :, :], AX.X, ALU.add))
            c(nc.vector.tensor_tensor(total[:, :], tbase[:, NE - 1:NE], ntile[:, NE - 1:NE], ALU.add))

        def experts_by_tile():
            c(nc.vector.tensor_tensor(ge[:, :, :], con("tiles").unsqueeze(2).to_broadcast([P, TILES, NE]), tbase[:, :].unsqueeze(1).to_broadcast([P, TILES, NE]), ALU.is_ge))
            c(nc.vector.tensor_reduce(ex[:, :], ge[:, :, :], AX.X, ALU.add))
            c(nc.vector.tensor_tensor(gt_[:, :, :], ge[:, :, :], tbase[:, :].unsqueeze(1).to_broadcast([P, TILES, NE]), ALU.mult))
            c(nc.vector.tensor_reduce(tb[:, :], gt_[:, :, :], AX.X, ALU.max))

        def starts_by_tile():
            c(nc.vector.tensor_scalar(ex[:, :], ex[:, :], -1.0, None, ALU.add))
            c(nc.vector.tensor_tensor(tb[:, :], con("tiles"), tb[:, :], ALU.subtract))
            c(nc.vector.tensor_scalar(tb[:, :], tb[:, :], float(TT), None, ALU.mult))
            c(nc.vector.scalar_tensor_tensor(stf[:, :], ex[:, :], float(REGION), tb[:, :], ALU.mult, ALU.add))
            c(nc.vector.tensor_scalar(dead[:, :], con("tiles"), total[:, 0:1], None, ALU.is_ge))
            c(nc.vector.scalar_tensor_tensor(tb[:, :], stf[:, :], -float(DUMMY), dead[:, :], ALU.add, ALU.mult))
            c(nc.vector.tensor_tensor(stf[:, :], stf[:, :], tb[:, :], ALU.subtract))
            c.done()
            nc.vector.tensor_copy(starts[:, 0:TILES], stf[:, :])
            nc.vector.tensor_copy(experts[:, 0:TILES], ex[:, :]).then_inc(list_r, 1)

        def routed_parts(t, j):
            e = dve.value_load(experts[0:1, bass.ds(t, 1)], min_val=0, max_val=NE - 1)
            wait(dve, s["y_r"], t + NS - XT + 1)
            nc.vector.tensor_copy(rec[j % XT][:, :], records[:, bass.ds(e, 1), :].rearrange("p o w -> p (o w)")).then_inc(s["rec_r"], 1)
            dve.wait_ge(s["xt_ps"], t + 1)
            parts(t + NS, j % XT, ps_t[j % 2][:, 0:TT])

        def bias(r, j):
            t = r * XB + j
            dve.wait_ge(s["y_ps"], t + NS + 1)
            wait(dve, s_out[j], 16 * TQ * r)
            nc.vector.tensor_tensor(yb[j][:, :, :], ps_y, rec[j % XT][:, REC_B2:].unsqueeze(1).to_broadcast([P, TQ, E]), ALU.add).then_inc(s["y_r"], 1)

        def routed():
            dve.wait_ge(list_r, 1)
            dve.wait_ge(a["w2_in"], 16 * (NE + 1))
            dve.wait_ge(a["split_r"], 2 * (NE + 1))
            routed_parts(0, 0)
            routed_parts(1, 1)
            shared_out(NS - 2, 0)
            dve.wait_ge(a["keep_r"], B)
            nc.vector.tensor_tensor(dl[:, :, 0:NE], logits[:, 0:NT, :], top8[:, 0:NT, 0:1].to_broadcast([P, NT, NE]), ALU.subtract)
            nc.vector.tensor_tensor(dl[:, :, NE:], top8[:, 0:NT, 1:2], top8[:, 0:NT, 0:1], ALU.subtract).then_inc(s["wt_d"], 1)
            def step(r, j):
                t = r * XB + j
                static = isinstance(r, int)
                if not static or t + 2 < TILES:
                    routed_parts(t + 2, (j + 2) % XB)
                if static and t == 0:
                    shared_out(NS - 1, (NS - 1) % 2)
                else:
                    bias(r + (j - 1) // XB, (j - 1) % XB)

            for j in range(XB):
                step(0, j)
            for j in range(XB):
                step(1, j)
            with dve.Fori(2, ROUNDS - 1) as r:
                for j in range(XB):
                    step(r, j)
            for j in range(XB):
                step(ROUNDS - 1, j)
            bias(ROUNDS - 1, XB - 1)

            dve.wait_ge(s["wt_e"], 1)
            c = Chain(dve, s["wtc"], 4, 0)
            c(nc.vector.tensor_reduce(esum[:, :], el[:, :, 0:NE], AX.X, ALU.add))
            c(nc.vector.scalar_tensor_tensor(esum[:, :], esum[:, :], EPS_W, el[:, :, NE], ALU.mult, ALU.add))
            c(nc.vector.tensor_scalar(esum[:, :], esum[:, :], 1.0, None, ALU.add))
            c(nc.vector.reciprocal(wt[:, 0, :], esum[:, :]))
            c.done()
            nc.vector.tensor_tensor(wt[:, 1, :], wt[:, 0, :], el[:, :, NE], ALU.mult).then_inc(s["wt_r"], 1)

            for n in range(NCH):
                dve.wait_ge(s_og[n % OG], 16 * (n // OG + 1))
                if n >= OG:
                    dve.wait_ge(s_fin[n % OG], 16 * (n // OG))
                o, g = ob[n % OG], og[n % OG]
                for q in range(CH):
                    last = nc.vector.scalar_tensor_tensor(o[:, q, :], g[:, q, 0, :], wt[:, 0, CH * n + q:CH * n + q + 1], xs[:, CH * n + q, :], ALU.mult, ALU.add)
                last.then_inc(s["o_c"], 1)
                dve.wait_ge(s["og_w"], n + 1)
                dve.wait_ge(s["o_c"], n + 1)
                nc.vector.tensor_tensor(o[:, :, :], o[:, :, :], g[:, :, 1, :], ALU.add).then_inc(s["o_r"], 1)
        return shared, (rows_by_expert, experts_by_tile, starts_by_tile), routed

    def gpsimd(pool):
        def send(r, j):
            wait_apart(pool, passed, (s["y_r"], r * XB + j + 1 + NS))
            for q in range(TQ):
                nc.gpsimd.indirect_dma_start(out=orows, out_offset=bass.IndirectOffsetOnAxis(ap=xg[j][:, q, E:XW].bitcast(I32), axis=0),
                                             in_=yb[j][:, q, :], in_offset=None, bounds_check=OROWS - 1, oob_is_err=False).then_inc(s_out[j], 16)

        with pool.Fori(0, ROUNDS) as r:
            for j in range(XB):
                send(r, j)

    return {"sync": sync, "tensor": tensor, "scalar": scalar, "vector": vector, "gpsimd": gpsimd}


_INS = ["L0_attn_x", "L0_attn_Wq", "L0_attn_Wk", "L0_attn_Wv", "L0_attn_Wo", "L0_ffn_Wg", "L0_ffn_W1", "L0_ffn_b1",
        "L0_ffn_W2", "L0_ffn_b2", "L0_ffn_Ws1", "L0_ffn_bs1", "L0_ffn_Ws2", "L0_ffn_bs2"]


def kernel(**inputs):
    import concourse.bacc as _bacc
    from concourse.bass_utils import run_bass_kernel_spmd as _run

    nc = _bacc.Bacc("TRN2", target_bir_lowering=False, num_devices=1)
    arrays, args = {}, []
    for name in _INS:
        a = np.ascontiguousarray(inputs[name])
        arrays[name] = a
        args.append(nc.dram_tensor(name, a.shape, mybir.dt.from_np(a.dtype), kind="ExternalInput").ap())
    arrays["consts"] = constants()
    args.append(nc.dram_tensor("consts", [P, NCONST], F32, kind="ExternalInput").ap())
    args.append(nc.dram_tensor("result", [B, S, E], F32, kind="ExternalOutput").ap())
    block_kernel(nc, *args)
    r = _run(nc, [arrays], core_ids=[0])
    return r.results[0]["result"]
```
